# Optimizing a Trainium2 kernel written in Bass

```python
import numpy as np
import jax
import jax.numpy as jnp

def _softmax(x, axis=-1):
    return jax.nn.softmax(x, axis=axis)

def _gelu(x):
    return jax.nn.gelu(x, approximate=True)

def _silu(x):
    return jax.nn.silu(x)

def _sigmoid(x):
    return jax.nn.sigmoid(x)

def _layernorm(x, axis=-1, eps=1e-05):
    m = jnp.mean(x, axis=axis, keepdims=True)
    v = jnp.var(x, axis=axis, keepdims=True)
    return (x - m) / jnp.sqrt(v + eps)

def _scatter_add(tgt, idx, src, axis=0):
    return tgt.at[idx].add(src)

def _segment_sum(src, seg, n):
    return jax.ops.segment_sum(src, seg, n)
kernel_name = 'mk_gnn_preln_d4_gnn_r64_718678'

def setup_inputs(seed: int=0):
    np.random.seed(seed)
    _w = jnp.asarray

    def _rec_inputs():
        import jax
        import jax.numpy as jnp
        _gk = jax.random.key(seed)
        x = -0.0008691 + 1 * jax.random.normal(jax.random.fold_in(_gk, 1), (50000, 128), jnp.float32)
        src = jax.random.randint(jax.random.fold_in(_gk, 2), (25000,), 0, 50000, jnp.int32)
        dst = jnp.minimum((50000 * jax.random.uniform(jax.random.fold_in(_gk, 3), (25000,)) ** 2.0).astype(jnp.int32), 49999)
        _o = jnp.argsort(dst, stable=True)
        src = src[_o]
        dst = dst[_o]
        edge_type_8 = jax.random.randint(jax.random.fold_in(_gk, 13), (25000,), 0, 8, jnp.int32)
        return (x, src, dst, edge_type_8)
    x, src, dst, edge_type_8 = _rec_inputs()

    def _L0_gnn_setup():
        import jax, jax.numpy as jnp
        import numpy as np
        N_NODES = 10000
        N_EDGES = 10000
        C_IN = 128
        HIDDEN = 128

        def gcn_conv(x, W, b, src, dst):
            N = x.shape[0]
            loops = jnp.arange(N, dtype=src.dtype)
            s = jnp.concatenate([src, loops])
            d = jnp.concatenate([dst, loops])
            h = x @ W
            deg = jax.ops.segment_sum(jnp.ones(d.shape, dtype=x.dtype), d, num_segments=N)
            dinv = jnp.where(deg > 0, jax.lax.rsqrt(deg), jnp.zeros_like(deg))
            norm = dinv[s] * dinv[d]
            msgs = h[s] * norm[:, None]
            out = jax.ops.segment_sum(msgs, d, num_segments=N)
            return out + b
        key = jax.random.key(seed)
        k1, k2, k3, k4, k5 = jax.random.split(key, 5)
        x = jax.random.normal(k1, (N_NODES, C_IN), dtype=jnp.float32)
        edge_src = jax.random.randint(k2, (N_EDGES,), 0, N_NODES)
        edge_dst = jax.random.randint(k3, (N_EDGES,), 0, N_NODES)
        W1 = jax.random.normal(k4, (C_IN, HIDDEN), dtype=jnp.float32) * (1.0 / np.sqrt(C_IN))
        b1 = jnp.zeros((HIDDEN,), dtype=jnp.float32)
        W2 = jax.random.normal(k5, (HIDDEN, HIDDEN), dtype=jnp.float32) * (1.0 / np.sqrt(HIDDEN))
        b2 = jnp.zeros((HIDDEN,), dtype=jnp.float32)
        return {'x': x, 'edge_src': edge_src, 'edge_dst': edge_dst, 'W1': W1, 'b1': b1, 'W2': W2, 'b2': b2, 't': 0}
    _L0_gnn_all = _L0_gnn_setup()
    _L0_gnn_in = {k: v for k, v in _L0_gnn_all.items() if k in ('W1', 'b1', 'W2', 'b2')}
    del _L0_gnn_all

    def _L1_gnn_setup():
        import jax, jax.numpy as jnp
        import numpy as np
        N_REL = 8
        EPS = 1e-05

        def _rgcn_bn_mish(x, W, root, bias, gamma, beta, edge_index, edge_type):
            N = x.shape[0]
            src, dst = (edge_index[0], edge_index[1])
            h = jnp.einsum('ni,rio->rno', x, W)
            seg = edge_type * N + dst
            counts = jax.ops.segment_sum(jnp.ones(edge_type.shape, dtype=x.dtype), seg, num_segments=N_REL * N).reshape(N_REL, N)
            counts = jnp.maximum(counts, 1.0)
            msgs = h[edge_type, src] / counts[edge_type, dst][:, None]
            agg = jax.ops.segment_sum(msgs, dst, num_segments=N)
            out = agg + x @ root + bias
            mu = jnp.mean(out, axis=0)
            var = jnp.var(out, axis=0)
            out = (out - mu) * jax.lax.rsqrt(var + EPS) * gamma + beta
            return out * jnp.tanh(jax.nn.softplus(out))
        key = jax.random.key(seed)
        k1, k2, k3, k4, k5 = jax.random.split(key, 5)
        N, E, D_IN, D_OUT = (100000, 9375, 128, 128)
        x = jax.random.normal(k1, (N, D_IN), dtype=jnp.float32)
        edge_index = jax.random.randint(k2, (2, E), 0, N, dtype=jnp.int64)
        edge_type = jax.random.randint(k3, (E,), 0, N_REL, dtype=jnp.int64)
        W = jax.random.normal(k4, (N_REL, D_IN, D_OUT), dtype=jnp.float32) * 0.05
        root = jax.random.normal(k5, (D_IN, D_OUT), dtype=jnp.float32) * 0.05
        bias = jnp.zeros((D_OUT,), dtype=jnp.float32)
        gamma = jnp.ones((D_OUT,), dtype=jnp.float32)
        beta = jnp.zeros((D_OUT,), dtype=jnp.float32)
        return {'x': x, 'edge_index': edge_index, 'edge_type': edge_type, 'W': W, 'root': root, 'bias': bias, 'gamma': gamma, 'beta': beta}
    _L1_gnn_all = _L1_gnn_setup()
    _L1_gnn_in = {k: v for k, v in _L1_gnn_all.items() if k in ('W', 'root', 'bias', 'gamma', 'beta')}
    del _L1_gnn_all

    def _L2_gnn_setup():
        import jax, jax.numpy as jnp
        import numpy as np
        N = 50000
        E = 12500
        D = 128
        EPS = 1e-05
        key = jax.random.key(seed)
        ks = jax.random.split(key, 12)
        s1 = 1.0 / np.sqrt(2 * D)
        s2 = 1.0 / np.sqrt(D)
        return {'x': jax.random.normal(ks[0], (N, D), dtype=jnp.float32), 'edge_index': jax.random.randint(ks[1], (2, E), 0, N, dtype=jnp.int32), 'wm1': jax.random.uniform(ks[2], (2 * D, D), jnp.float32, -s1, s1), 'bm1': jax.random.uniform(ks[3], (D,), jnp.float32, -s1, s1), 'wm2': jax.random.uniform(ks[4], (D, D), jnp.float32, -s2, s2), 'bm2': jax.random.uniform(ks[5], (D,), jnp.float32, -s2, s2), 'wu1': jax.random.uniform(ks[6], (2 * D, D), jnp.float32, -s1, s1), 'bu1': jax.random.uniform(ks[7], (D,), jnp.float32, -s1, s1), 'wu2': jax.random.uniform(ks[8], (D, D), jnp.float32, -s2, s2), 'bu2': jax.random.uniform(ks[9], (D,), jnp.float32, -s2, s2), 'gamma': jnp.ones((D,), jnp.float32), 'beta': jnp.zeros((D,), jnp.float32)}
    _L2_gnn_all = _L2_gnn_setup()
    _L2_gnn_in = {k: v for k, v in _L2_gnn_all.items() if k in ('wm1', 'bm1', 'wm2', 'bm2', 'wu1', 'bu1', 'wu2', 'bu2', 'gamma', 'beta')}
    del _L2_gnn_all

    def _L3_gnn_setup():
        import jax, jax.numpy as jnp
        import numpy as np
        N_NODES = 10000
        N_EDGES = 10000
        C = 128
        key = jax.random.key(seed)
        k1, k2, k3, k4 = jax.random.split(key, 4)
        x = jax.random.normal(k1, (N_NODES, C), dtype=jnp.float32)
        edge_index = jax.random.randint(k2, (2, N_EDGES), 0, N_NODES, dtype=jnp.int64)
        W2 = jax.random.normal(k3, (C,), dtype=jnp.float32)
        W3 = jax.random.normal(k4, (C,), dtype=jnp.float32)
        return {'x': x, 'edge_index': edge_index, 'W2': W2, 'W3': W3}
    _L3_gnn_all = _L3_gnn_setup()
    _L3_gnn_in = {k: v for k, v in _L3_gnn_all.items() if k in ('W2', 'W3')}
    del _L3_gnn_all
    return {'x': x, 'src': src, 'dst': dst, 'edge_type_8': edge_type_8, 'L0_gnn_W1': _L0_gnn_in['W1'], 'L0_gnn_b1': _L0_gnn_in['b1'], 'L0_gnn_W2': _L0_gnn_in['W2'], 'L0_gnn_b2': _L0_gnn_in['b2'], 'L1_gnn_W': _L1_gnn_in['W'], 'L1_gnn_root': _L1_gnn_in['root'], 'L1_gnn_bias': _L1_gnn_in['bias'], 'L1_gnn_gamma': _L1_gnn_in['gamma'], 'L1_gnn_beta': _L1_gnn_in['beta'], 'L2_gnn_wm1': _L2_gnn_in['wm1'], 'L2_gnn_bm1': _L2_gnn_in['bm1'], 'L2_gnn_wm2': _L2_gnn_in['wm2'], 'L2_gnn_bm2': _L2_gnn_in['bm2'], 'L2_gnn_wu1': _L2_gnn_in['wu1'], 'L2_gnn_bu1': _L2_gnn_in['bu1'], 'L2_gnn_wu2': _L2_gnn_in['wu2'], 'L2_gnn_bu2': _L2_gnn_in['bu2'], 'L2_gnn_gamma': _L2_gnn_in['gamma'], 'L2_gnn_beta': _L2_gnn_in['beta'], 'L3_gnn_W2': _L3_gnn_in['W2'], 'L3_gnn_W3': _L3_gnn_in['W3']}

def reference(x, src, dst, edge_type_8, L0_gnn_W1, L0_gnn_b1, L0_gnn_W2, L0_gnn_b2, L1_gnn_W, L1_gnn_root, L1_gnn_bias, L1_gnn_gamma, L1_gnn_beta, L2_gnn_wm1, L2_gnn_bm1, L2_gnn_wm2, L2_gnn_bm2, L2_gnn_wu1, L2_gnn_bu1, L2_gnn_wu2, L2_gnn_bu2, L2_gnn_gamma, L2_gnn_beta, L3_gnn_W2, L3_gnn_W3):
    import jax
    import jax.numpy as jnp

    def _L0_gnn_ref(x, edge_src, edge_dst, W1, b1, W2, b2, t):
        import jax, jax.numpy as jnp
        import numpy as np
        N_NODES = 10000
        N_EDGES = 10000
        C_IN = 128
        HIDDEN = 128

        def gcn_conv(x, W, b, src, dst):
            N = x.shape[0]
            loops = jnp.arange(N, dtype=src.dtype)
            s = jnp.concatenate([src, loops])
            d = jnp.concatenate([dst, loops])
            h = x @ W
            deg = jax.ops.segment_sum(jnp.ones(d.shape, dtype=x.dtype), d, num_segments=N)
            dinv = jnp.where(deg > 0, jax.lax.rsqrt(deg), jnp.zeros_like(deg))
            norm = dinv[s] * dinv[d]
            msgs = h[s] * norm[:, None]
            out = jax.ops.segment_sum(msgs, d, num_segments=N)
            return out + b
        h = jax.nn.relu(gcn_conv(x, W1, b1, edge_src, edge_dst))
        return gcn_conv(h, W2, b2, edge_src, edge_dst)

    def _L1_gnn_ref(x, edge_index, edge_type, W, root, bias, gamma, beta):
        import jax, jax.numpy as jnp
        import numpy as np
        N_REL = 8
        EPS = 1e-05

        def _rgcn_bn_mish(x, W, root, bias, gamma, beta, edge_index, edge_type):
            N = x.shape[0]
            src, dst = (edge_index[0], edge_index[1])
            h = jnp.einsum('ni,rio->rno', x, W)
            seg = edge_type * N + dst
            counts = jax.ops.segment_sum(jnp.ones(edge_type.shape, dtype=x.dtype), seg, num_segments=N_REL * N).reshape(N_REL, N)
            counts = jnp.maximum(counts, 1.0)
            msgs = h[edge_type, src] / counts[edge_type, dst][:, None]
            agg = jax.ops.segment_sum(msgs, dst, num_segments=N)
            out = agg + x @ root + bias
            mu = jnp.mean(out, axis=0)
            var = jnp.var(out, axis=0)
            out = (out - mu) * jax.lax.rsqrt(var + EPS) * gamma + beta
            return out * jnp.tanh(jax.nn.softplus(out))
        return _rgcn_bn_mish(x, W, root, bias, gamma, beta, edge_index, edge_type)

    def _L2_gnn_ref(x, edge_index, wm1, bm1, wm2, bm2, wu1, bu1, wu2, bu2, gamma, beta):
        import jax, jax.numpy as jnp
        import numpy as np
        N = 50000
        E = 12500
        D = 128
        EPS = 1e-05
        row, col = (edge_index[0], edge_index[1])
        msg_in = jnp.concatenate([x[row], x[col]], axis=-1)
        h = jax.nn.silu(msg_in @ wm1 + bm1)
        messages = h @ wm2 + bm2
        aggr = jax.ops.segment_sum(messages, row, num_segments=x.shape[0])
        upd_in = jnp.concatenate([x, aggr], axis=-1)
        u = jax.nn.silu(upd_in @ wu1 + bu1)
        out = u @ wu2 + bu2
        y = x + out
        mu = jnp.mean(y, axis=-1, keepdims=True)
        var = jnp.var(y, axis=-1, keepdims=True)
        yn = (y - mu) * jax.lax.rsqrt(var + EPS)
        return yn * gamma + beta

    def _L3_gnn_ref(x, edge_index, W2, W3):
        import jax, jax.numpy as jnp
        import numpy as np
        N_NODES = 10000
        N_EDGES = 10000
        C = 128
        src = edge_index[0]
        dst = edge_index[1]
        x2 = x * W2
        x3 = x * W3
        attn = jnp.einsum('ec,ec->e', x3[src], x[dst])
        out = jax.ops.segment_sum(attn[:, None] * x2[src], dst, num_segments=x.shape[0])
        return out
    edge_index = jnp.stack([src, dst])
    h = jnp.maximum(_layernorm(x, axis=-1), 0.0)
    x = x + _L0_gnn_ref(h, src, dst, L0_gnn_W1, L0_gnn_b1, L0_gnn_W2, L0_gnn_b2, 0)
    h = jnp.maximum(_layernorm(x, axis=-1), 0.0)
    x = x + _L1_gnn_ref(h, edge_index, edge_type_8, L1_gnn_W, L1_gnn_root, L1_gnn_bias, L1_gnn_gamma, L1_gnn_beta)
    h = jnp.maximum(_layernorm(x, axis=-1), 0.0)
    x = x + _L2_gnn_ref(h, edge_index, L2_gnn_wm1, L2_gnn_bm1, L2_gnn_wm2, L2_gnn_bm2, L2_gnn_wu1, L2_gnn_bu1, L2_gnn_wu2, L2_gnn_bu2, L2_gnn_gamma, L2_gnn_beta)
    h = jnp.maximum(_layernorm(x, axis=-1), 0.0)
    x = x + _L3_gnn_ref(h, edge_index, L3_gnn_W2, L3_gnn_W3)
    return x

_drawn_inputs = setup_inputs


def setup_inputs(seed=0):
    import zlib

    import numpy as np

    out = dict(_drawn_inputs(seed))
    spreads = {'L0_gnn_b1': (0.0, 0.1),
     'L0_gnn_b2': (0.0, 0.1),
     'L1_gnn_bias': (0.0, 0.8),
     'L1_gnn_gamma': (1.0, 0.2),
     'L1_gnn_beta': (0.0, 0.1),
     'L2_gnn_gamma': (1.0, 0.2),
     'L2_gnn_beta': (0.0, 0.1)}
    factors = {'L2_gnn_wm1': 2.875,
     'L2_gnn_bm1': 8.0,
     'L2_gnn_wm2': 2.766,
     'L2_gnn_bm2': 5.648,
     'L2_gnn_bu1': 4.997}
    for name, (base, spread) in spreads.items():
        noise = np.random.default_rng([zlib.crc32(name.encode()), seed]).standard_normal(out[name].shape)
        drawn = base * np.exp(spread * noise) if base else spread * noise
        out[name] = jnp.asarray(drawn.astype(out[name].dtype))
    for name, factor in factors.items():
        out[name] = (out[name] * factor).astype(out[name].dtype)
    return out
```

```python
from contextlib import ExitStack

import concourse.bass as bass
from concourse import mybir

P = 128
F32 = mybir.dt.float32
BF16 = mybir.dt.bfloat16
I32 = mybir.dt.int32
ALU = mybir.AluOpType
ACT = mybir.ActivationFunctionType
AX = mybir.AxisListType

C = 128
N = 50000
E = 25000
R = 8
EPS = 1e-5
J = 4
GROUP = P * J
NG = -(-N // GROUP)
FULL = N // GROUP
TAIL = (N - FULL * GROUP) // J
HI = NG * J
MID = HI // 2
T = -(-E // P)
ETAIL = E - (P - 1) * T
PAD = NG * GROUP - 1
SKIP = 1 << 20
assert N % J == 0 and T % 2 == 0 and 0 < ETAIL <= T and PAD >= N


class Phase:

    def __init__(self, nc):
        self.nc, self.stack, self.semaphores = nc, ExitStack(), []

    def __enter__(self):
        self.stack.__enter__()
        return self

    def enter_context(self, what):
        return self.stack.enter_context(what)

    def semaphore(self, name):
        self.semaphores.append(self.nc.alloc_semaphore(name))
        return self.semaphores[-1]

    def __exit__(self, *error):
        self.stack.__exit__(*error)
        if error[0] is None:
            self.nc.clear_and_free_semaphores(self.semaphores)
            with self.nc.Block():
                pass


def constants(nc, k):
    with Phase(nc) as ctx:
        raw = ctx.enter_context(nc.sbuf_tensor("raw_iota", [P, HI], I32))
        part = ctx.enter_context(nc.sbuf_tensor("raw_part", [P, 1], I32))
        iota_ready = ctx.semaphore("const_iota_ready")
        chain = ctx.semaphore("const_chain")
        pads_set = ctx.semaphore("const_pads_set")
        edges_in = ctx.semaphore("const_edges_in")
        weights_in = ctx.semaphore("const_weights_in")
        block = ctx.enter_context(nc.Block())

        @block.gpsimd
        def _(pool):
            pool.iota(raw[:, :], pattern=[[1, HI]], base=0, channel_multiplier=0).then_inc(iota_ready, 1)
            pool.iota(part[:, :], pattern=[[0, 1]], base=0, channel_multiplier=1).then_inc(iota_ready, 1)

        @block.vector
        def _(dve):
            dve.memset(k.edge_i[:, :, :], PAD).then_inc(pads_set, 1)
            dve.memset(k.ones[:, :], 1.0)
            dve.memset(k.zero_row[:, :], 0.0)
            dve.wait_ge(iota_ready, 2)
            dve.tensor_copy(k.iota[:, :], raw[:, :]).then_inc(chain, 1)
            dve.tensor_copy(k.part[:, :], part[:, :]).then_inc(chain, 1)
            dve.wait_ge(chain, 2)
            dve.tensor_scalar(k.ident[:, :], k.iota[:, 0:P], k.part[:, :], None, ALU.is_equal).then_inc(chain, 1)
            dve.tensor_scalar(k.before[:, :], k.iota[:, 0:P], k.part[:, :], None, ALU.is_gt).then_inc(chain, 1)
            dve.tensor_scalar(k.shift[:, :], k.iota[:, 0:P], 1.0, k.part[:, :], ALU.add, ALU.is_equal).then_inc(chain, 1)
            dve.tensor_scalar(k.unshift[:, :], k.iota[:, 0:P], -1.0, k.part[:, :], ALU.add, ALU.is_equal).then_inc(chain, 1)
            dve.tensor_scalar(k.first[:, :], k.part[:, :], 0.0, None, ALU.is_equal).then_inc(chain, 1)
            dve.tensor_scalar(k.last[:, :], k.part[:, :], P - 1.0, None, ALU.is_equal).then_inc(chain, 1)
            dve.tensor_scalar(k.ident_b[:, :], k.iota[:, 0:P], k.part[:, :], None, ALU.is_equal)
            dve.tensor_scalar(k.iota_b[:, :], k.iota[:, :], -float(MID), None, ALU.add).then_inc(chain, 1)
            dve.wait_ge(chain, 9)
            dve.tensor_scalar(k.wrap[:, :], k.iota[:, 0:P], P - 1.0, k.first[:, :], ALU.is_equal, ALU.mult).then_inc(chain, 1)
            dve.wait_ge(chain, 10)

        @block.sync
        def _(sp):
            sp.dma_start(k.w1[:, :], k.L0_W1).then_inc(weights_in, 16)
            sp.dma_start(k.w2[:, :], k.L0_W2).then_inc(weights_in, 16)
            sp.dma_start(k.w_rel[:, :, :], k.L1_W.rearrange("r i o -> i r o")).then_inc(weights_in, 16)
            sp.dma_start(k.root[:, :], k.L1_root).then_inc(weights_in, 16)
            sp.dma_start(k.b1_col[:, :], k.L0_b1.rearrange("(c a) -> c a", a=1)).then_inc(weights_in, 16)
            sp.wait_ge(pads_set, 1)
            lists = [k.dst, k.src, k.edge_type]
            for r, flat in enumerate(lists):
                sp.dma_start(k.edge_i[0:P - 1, r, :],
                             flat[0:(P - 1) * T].rearrange("(p t) -> p t", t=T)).then_inc(edges_in, 16)
                sp.dma_start(k.edge_i[P - 1:P, r, 0:ETAIL],
                             flat[(P - 1) * T:E].rearrange("(a t) -> a t", a=1)).then_inc(edges_in, 16)
            sp.wait_ge(edges_in, 16 * 2 * len(lists))
            sp.wait_ge(weights_in, 16 * 5)


def sort_edges(nc, k):
    with Phase(nc) as ctx:
        sb = lambda name, shape, dt=F32: ctx.enter_context(nc.sbuf_tensor("so_" + name, shape, dt))
        ps = lambda name: ctx.enter_context(nc.psum_tensor("so_" + name, [P, 512], F32))
        sem = lambda name: ctx.semaphore("so_" + name)
        node = k.edge_i
        part_i, hi_i, tmp_i = (sb(n, [P, 2, T], I32) for n in ("part_i", "hi_i", "tmp_i"))
        lo, hi, node_f, pay, place = (sb(n, [P, 2, T]) for n in ("lo", "hi", "node_f", "pay", "place"))
        lo_b = sb("lo_b", [P, 2, T], BF16)
        type_i = sb("type_i", [P, T], I32)
        type_f = sb("type_f", [P, T])
        place_i = sb("place_i", [P, 2, T], I32)
        one_lo = sb("one_lo", [P, 2, P], BF16)
        one_hi = sb("one_hi", [P, 2, HI], BF16)
        lo_t = sb("lo_t", [P, 2, P])
        same_lo = sb("same_lo", [P, 2, P], BF16)
        base = sb("base", [P, 2, HI])
        hist = sb("hist", [P, 2, HI])
        picked = sb("picked", [P, 2, HI])
        got = sb("got", [P, 2, 1])
        rows = sb("rows", [P, 2, 1])
        starts = sb("starts", [P, 2, 1])
        zero_b = sb("zero_b", [P, HI], BF16)
        put_lo = sb("put_lo", [P, 2, P])
        put_hi = sb("put_hi", [P, 2, 2, T])
        run_ps = [ps("run0"), ps("run1")]
        pick_ps = [ps("pick0"), ps("pick1")]
        row_ps = [ps("row0"), ps("row1")]
        sum_ps = ps("sum")
        chain = sem("chain")
        digits = sem("digits")
        zeroed = sem("zeroed")
        ones_ready, ones_used = sem("ones_ready"), sem("ones_used")
        rows_ready, starts_ready, base_ready, base_in = (sem(n) for n in ("rows_ready", "starts_ready", "base_ready", "base_in"))
        row_ready, masks_ready, run_copied, run_updated = (sem(n) for n in ("row_ready", "masks_ready", "run_copied", "run_updated"))
        pick_ready, pick_read, got_free, turn = (sem(n) for n in ("pick_ready", "pick_read", "got_free", "turn"))
        put_ready, put_used = sem("put_ready"), sem("put_used")
        block = ctx.enter_context(nc.Block())

        def one_hots(dve, t, o):
            dve.tensor_scalar(one_lo[:, o, :], k.iota_b[:, MID:MID + P], lo[:, o, bass.ds(t, 1)], None, ALU.is_equal)
            return dve.tensor_scalar(one_hi[:, o, :], k.iota_b[:, :], hi[:, o, bass.ds(t, 1)], None, ALU.is_equal)

        @block.vector
        def _(dve):
            links = [0]

            def link(ins):
                links[0] += 1
                ins.then_inc(chain, 1)
                dve.wait_ge(chain, links[0])

            dve.memset(zero_b[:, :], 0.0).then_inc(zeroed, 1)
            both = node[:, 0:2, :]
            dve.tensor_scalar(part_i[:, :, :], both, 2, 127, ALU.logical_shift_right, ALU.bitwise_and).then_inc(digits, 1)
            dve.tensor_scalar(hi_i[:, :, :], both, 9, 2, ALU.logical_shift_right, ALU.logical_shift_left).then_inc(digits, 1)
            dve.tensor_scalar(tmp_i[:, :, :], both, 3, None, ALU.bitwise_and).then_inc(digits, 1)
            dve.tensor_scalar(type_i[:, :], node[:, 2, :], R - 1, None, ALU.bitwise_and).then_inc(digits, 1)
            dve.wait_ge(digits, 4)
            dve.tensor_tensor(hi[:, :, :], hi_i[:, :, :], tmp_i[:, :, :], ALU.add).then_inc(digits, 1)
            dve.tensor_copy(lo[:, :, :], part_i[:, :, :]).then_inc(digits, 1)
            dve.wait_ge(digits, 5)
            dve.tensor_scalar(hi[:, :, :], hi[:, :, :], -float(MID), None, ALU.add)
            dve.tensor_copy(type_f[:, :], type_i[:, :]).then_inc(digits, 1)
            dve.tensor_copy(node_f[:, :, :], both).then_inc(digits, 1)
            dve.tensor_copy(lo_b[:, :, :], part_i[:, :, :]).then_inc(digits, 1)
            dve.wait_ge(digits, 9)
            for o in range(2):
                dve.scalar_tensor_tensor(pay[:, o, :], node_f[:, o, :], float(R), type_f[:, :],
                                         ALU.mult, ALU.add).then_inc(digits, 1)
            dve.wait_ge(digits, 11)
            with dve.Fori(0, T) as t:
                for o in range(2):
                    dve.wait_ge(ones_used, t * 2 + o + 1)
                    one_hots(dve, t, o).then_inc(ones_ready, 1)
            dve.wait_ge(ones_used, 2 * T + 2)
            for o in range(2):
                dve.tensor_copy(hist[:, o, :], run_ps[o][:, 0:HI]).then_inc(base_ready, 1)
            dve.wait_ge(base_ready, 2)
            dve.tensor_copy(k.indeg[:, :], hist[:, 0, :])
            for o in range(2):
                dve.tensor_reduce(rows[:, o, :], hist[:, o, :], AX.X, ALU.add).then_inc(rows_ready, 1)
            dve.wait_ge(starts_ready, 1)
            for o in range(2):
                link(dve.tensor_copy(starts[:, o, :], sum_ps[:, o:o + 1]))
                link(dve.tensor_tensor_scan(picked[:, o, :], k.ones[:, 0:HI], hist[:, o, :], starts[:, o, :],
                                            ALU.mult, ALU.add))
                dve.tensor_tensor(base[:, o, :], picked[:, o, :], hist[:, o, :], ALU.subtract).then_inc(base_in, 1)
            dve.wait_ge(base_in, 2)
            dve.sem_inc(pick_read, 2)
            with dve.Fori(0, T) as t:
                for o in range(2):
                    n = t * 2 + o + 1
                    dve.wait_ge(run_updated, n)
                    dve.wait_ge(pick_read, n)
                    one_hots(dve, t, o)
                    dve.wait_ge(row_ready, n)
                    dve.tensor_scalar(lo_t[:, o, :], row_ps[o][:, 0:P], k.part[:, :], None, ALU.is_equal)
                    dve.scalar_tensor_tensor(same_lo[:, o, :], row_ps[o][:, 0:P], lo[:, o, bass.ds(t, 1)],
                                             k.before[:, :], ALU.is_equal, ALU.mult).then_inc(masks_ready, 1)
                for o in range(2):
                    n = t * 2 + o + 1
                    dve.wait_ge(pick_ready, n)
                    dve.wait_ge(got_free, n)
                    dve.tensor_tensor_reduce(picked[:, o, :], pick_ps[o][:, 0:HI], one_hi[:, o, :], 1.0, 0.0,
                                             ALU.mult, ALU.add, got[:, o, :]).then_inc(pick_read, 1)
            dve.wait_ge(got_free, 2 * T + 2)
            link(dve.tensor_copy(place_i[:, :, :], place[:, :, :]))
            link(dve.tensor_scalar(hi_i[:, :, :], place_i[:, :, :], 7, None, ALU.logical_shift_right))
            link(dve.tensor_scalar(part_i[:, :, :], place_i[:, :, :], 127, None, ALU.bitwise_and))
            link(dve.tensor_copy(hi[:, :, :], hi_i[:, :, :]))
            link(dve.tensor_copy(lo[:, :, :], part_i[:, :, :]))
            with dve.Fori(0, T) as t:
                for o in range(2):
                    at = bass.ds(t, 1)
                    dve.wait_ge(put_used, t * 2 + o + 1)
                    dve.tensor_scalar(put_lo[:, o, :], k.iota[:, 0:P], lo[:, o, at], None, ALU.is_equal)
                    dve.tensor_scalar(put_hi[:, o, 0, :], k.iota[:, 0:T], hi[:, o, at], pay[:, o, at],
                                      ALU.is_equal, ALU.mult)
                    dve.tensor_scalar(put_hi[:, o, 1, :], k.iota[:, 0:T], hi[:, o, at], node_f[:, 1 - o, at],
                                      ALU.is_equal, ALU.mult).then_inc(put_ready, 1)
            dve.wait_ge(put_used, 2 * T + 2)
            for o in range(2):
                for w in range(2):
                    link(dve.tensor_copy(k.sorted[:, o, w, :], run_ps[o][:, w * T:(w + 1) * T]))

        @block.tensor
        def _(pe):
            pe.wait_ge(zeroed, 1)
            pe.sem_inc(ones_used, 2)
            for o in range(2):
                pe.matmul(run_ps[o][:, 0:HI], zero_b[:, 0:P], zero_b[:, :], start=True, stop=True, skip_group_check=True)
            with pe.Fori(0, T) as t:
                for o in range(2):
                    pe.wait_ge(ones_ready, t * 2 + o + 1)
                    pe.matmul(run_ps[o][:, 0:HI], one_lo[:, o, :], one_hi[:, o, :], start=False, stop=True,
                              skip_group_check=True).then_inc(ones_used, 1)
            pe.wait_ge(rows_ready, 2)
            pe.matmul(sum_ps[:, 0:2], k.before[:, :], rows[:, :, :].rearrange("p a b -> p (a b)"),
                      start=True, stop=True).then_inc(starts_ready, 1)
            pe.wait_ge(base_in, 2)
            pe.sem_inc(masks_ready, 2)
            for o in range(2):
                pe.matmul(run_ps[o][:, 0:HI], k.ident[:, :], base[:, o, :], start=True, stop=True,
                          skip_group_check=True).then_inc(run_updated, 1)
            with pe.Fori(0, T) as t:
                for o in range(2):
                    n = t * 2 + o + 1
                    pe.wait_ge(masks_ready, n)
                    pe.matmul(row_ps[o][:, 0:P], lo_b[:, o, bass.ds(t, 1)].to_broadcast([P, P]), k.ident_b[:, :],
                              start=True, stop=True).then_inc(row_ready, 1)
                for o in range(2):
                    n = t * 2 + o + 1
                    pe.wait_ge(masks_ready, n + 2)
                    pe.wait_ge(run_copied, n)
                    pe.matmul(pick_ps[o][:, 0:HI], lo_t[:, o, :], base[:, o, :], start=True, stop=False,
                              skip_group_check=True)
                    pe.matmul(pick_ps[o][:, 0:HI], same_lo[:, o, :], one_hi[:, o, :], start=False, stop=True,
                              skip_group_check=True).then_inc(pick_ready, 1)
                    pe.matmul(run_ps[o][:, 0:HI], one_lo[:, o, :], one_hi[:, o, :], start=False, stop=True,
                              skip_group_check=True).then_inc(run_updated, 1)
            pe.sem_inc(put_used, 2)
            for o in range(2):
                pe.matmul(run_ps[o][:, 0:2 * T], zero_b[:, 0:P], zero_b[:, 0:2 * T], start=True, stop=True,
                          skip_group_check=True)
            with pe.Fori(0, T) as t:
                for o in range(2):
                    pe.wait_ge(put_ready, t * 2 + o + 1)
                    pe.matmul(run_ps[o][:, 0:2 * T], put_lo[:, o, :],
                              put_hi[:, o, :, :].rearrange("p w t -> p (w t)"), start=False, stop=True,
                              skip_group_check=True).then_inc(put_used, 1)

        @block.scalar
        def _(act):
            with act.Fori(0, T) as t:
                for o in range(2):
                    n = t * 2 + o + 1
                    act.wait_ge(run_updated, n)
                    act.copy(base[:, o, :], run_ps[o][:, 0:HI]).then_inc(run_copied, 1)

        @block.gpsimd
        def _(pool):
            pool.sem_inc(got_free, 2)
            with pool.Fori(0, T) as t:
                for o in range(2):
                    pool.wait_ge(pick_read, t * 2 + o + 3)
                    pool.sem_inc(turn, 1)
                    pool.tensor_copy(place[:, o, bass.ds(t, 1)], got[:, o, :]).then_inc(got_free, 1)


def edge_tables(nc, k):
    with Phase(nc) as ctx:
        sb = lambda name, shape, dt=F32: ctx.enter_context(nc.sbuf_tensor("ta_" + name, shape, dt))
        ps = lambda name: ctx.enter_context(nc.psum_tensor("ta_" + name, [P, 512], F32))
        sem = lambda name: ctx.semaphore("ta_" + name)
        H = T // 2
        pay_i, key_i, type_i = (sb(n, [P, 2, T], I32) for n in ("pay_i", "key_i", "type_i"))
        keys = sb("keys", [P, 2, T + 1])
        typ = sb("typ", [P, T])
        nxt = sb("nxt", [P, 2, T])
        lasts, real, real2, idx = (sb(n, [P, 2, T]) for n in ("lasts", "real", "real2", "idx"))
        turned = sb("turned", [H, 2, 2, P])
        flat = sb("flat", [P, 2, T])
        first_f, last_f = sb("first_f", [P, T]), sb("last_f", [P, T])
        edge_key = sb("edge_key", [P, 2])
        of_r = sb("of_r", [P, R, T])
        upto, begin, count = (sb(n, [P, R, T]) for n in ("upto", "begin", "count"))
        hold = sb("hold", [P, R, T])
        per = sb("per", [P, R])
        carry, carry_t = sb("carry", [P, R]), sb("carry_t", [R, P])
        scanned = sb("scanned", [R, P + 1])
        mine = sb("mine", [P, T])
        weight = sb("weight", [P, 2, T])
        w_rows = sb("w_rows", [H, 2, 2, P])
        a_ps, b_ps, c_ps = ps("a"), ps("b"), ps("c")
        deg_inv = sb("deg_inv", [P, T])
        chain, deg_ready = sem("chain"), sem("deg_ready")
        nxt_ready, nxt_done = sem("nxt_ready"), sem("nxt_done")
        turn_asked, turn_ready, rows_ready = sem("turn_asked"), sem("turn_ready"), sem("rows_ready")
        flat_out, flat_in = sem("flat_out"), sem("flat_in")
        pe_asked, pe_done = sem("pe_asked"), sem("pe_done")
        w_ready, w_out, w_in, w_turned = (sem(n) for n in ("w_ready", "w_out", "w_in", "w_turned"))
        key_asked, key_done = sem("key_asked"), sem("key_done")
        block = ctx.enter_context(nc.Block())
        flat_dram = k.flat.rearrange("w (r c) -> r w c", c=P)
        flat_rows = k.flat.rearrange("w (p t) -> p w t", t=T)

        @block.vector
        def _(dve):
            links = [0]

            def link(ins):
                links[0] += 1
                ins.then_inc(chain, 1)
                dve.wait_ge(chain, links[0])

            link(dve.memset(keys[:, :, :], -1.0))
            link(dve.memset(k.key[:, :, :], -1.0))
            link(dve.tensor_copy(pay_i[:, :, :], k.sorted[:, :, 0, :]))
            link(dve.tensor_scalar(key_i[:, :, :], pay_i[:, :, :], 3, None, ALU.logical_shift_right))
            link(dve.tensor_scalar(type_i[:, :, :], pay_i[:, :, :], R - 1, None, ALU.bitwise_and))
            link(dve.tensor_copy(keys[:, :, 0:T], key_i[:, :, :]))
            link(dve.tensor_copy(k.key[:, :, 1:T + 1], key_i[:, :, :]))
            dve.tensor_copy(typ[:, :], type_i[:, 0, :]).then_inc(turn_asked, 1)
            dve.wait_ge(turn_asked, 1)
            dve.sem_inc(nxt_ready, 1)
            dve.wait_ge(turn_ready, 1)
            dve.tensor_copy(turned[:, :, :, :].rearrange("p a b c -> p (a b c)"), a_ps[0:H, :]).then_inc(rows_ready, 1)
            dve.wait_ge(nxt_done, 1)
            for o in range(2):
                link(dve.tensor_copy(nxt[:, o, :], b_ps[:, o * T:(o + 1) * T]))
            link(dve.tensor_tensor(lasts[:, :, :], nxt[:, :, :], keys[:, :, 0:T], ALU.not_equal))
            link(dve.tensor_scalar(real[:, :, :], keys[:, :, 0:T], N - 0.5, None, ALU.is_lt))
            link(dve.tensor_tensor(lasts[:, :, :], lasts[:, :, :], real[:, :, :], ALU.mult))
            link(dve.tensor_copy(k.is_last[:, :], lasts[:, 0, :]))
            link(dve.tensor_scalar(idx[:, :, :], lasts[:, :, :], -float(SKIP), float(SKIP), ALU.mult, ALU.add))
            link(dve.tensor_tensor(idx[:, :, :], idx[:, :, :], keys[:, :, 0:T], ALU.add))
            for o in range(2):
                link(dve.tensor_copy(k.index[:, o, :, 2], idx[:, o, :]))
            link(dve.tensor_tensor(idx[:, :, :], keys[:, :, 0:T], real[:, :, :], ALU.mult))
            for o in range(2):
                link(dve.tensor_copy(k.index[:, o, :, 1 - o], idx[:, o, :]))
            link(dve.tensor_scalar(real2[:, :, :], k.sorted[:, :, 1, :], N - 0.5, None, ALU.is_lt))
            link(dve.tensor_tensor(idx[:, :, :], k.sorted[:, :, 1, :], real2[:, :, :], ALU.mult))
            for o in range(2):
                link(dve.tensor_copy(k.index[:, o, :, o], idx[:, o, :]))
            dve.wait_ge(flat_in, 16)
            link(dve.memset(edge_key[:, :], 0.0))
            dve.tensor_copy(edge_key[:, 0:1], flat[:, 0, 0:1])
            dve.tensor_copy(edge_key[:, 1:2], flat[:, 0, T - 1:T]).then_inc(key_asked, 1)
            dve.wait_ge(key_done, 1)
            link(dve.tensor_tensor(first_f[:, 1:T], flat[:, 0, 1:T], flat[:, 0, 0:T - 1], ALU.not_equal))
            link(dve.tensor_copy(carry[:, 0:2], c_ps[:, 0:2]))
            link(dve.tensor_tensor(first_f[:, 0:1], carry[:, 1:2], flat[:, 0, 0:1], ALU.not_equal))
            link(dve.tensor_tensor(last_f[:, 0:T - 1], flat[:, 0, 1:T], flat[:, 0, 0:T - 1], ALU.not_equal))
            link(dve.tensor_tensor(last_f[:, T - 1:T], carry[:, 0:1], flat[:, 0, T - 1:T], ALU.not_equal))
            link(dve.tensor_tensor(first_f[:, 0:1], first_f[:, 0:1], k.first[:, :], ALU.max))
            link(dve.tensor_tensor(last_f[:, T - 1:T], last_f[:, T - 1:T], k.last[:, :], ALU.max))
            for r in range(R):
                link(dve.tensor_scalar(of_r[:, r, :], flat[:, 1, :], float(r), None, ALU.is_equal))
            for r in range(R):
                link(dve.tensor_tensor_scan(upto[:, r, :], k.ones[:, 0:T], of_r[:, r, :], 0.0, ALU.mult, ALU.add))
            dve.tensor_copy(per[:, :], upto[:, :, T - 1]).then_inc(pe_asked, 1)
            dve.wait_ge(pe_done, 1)
            link(dve.tensor_copy(carry[:, :], c_ps[:, 0:R]))
            for r in range(R):
                link(dve.tensor_scalar(upto[:, r, :], upto[:, r, :], carry[:, r:r + 1], None, ALU.add))
            link(dve.tensor_tensor(begin[:, :, :], upto[:, :, :], of_r[:, :, :], ALU.subtract))
            fb = first_f[:, :].rearrange("p (a t) -> p a t", a=1).to_broadcast([P, R, T])
            link(dve.tensor_tensor(hold[:, :, :], begin[:, :, :], fb, ALU.mult))
            for r in range(R):
                link(dve.tensor_tensor_scan(begin[:, r, :], k.ones[:, 0:T], hold[:, r, :], 0.0, ALU.mult, ALU.max))
            dve.tensor_copy(per[:, :], begin[:, :, T - 1]).then_inc(pe_asked, 1)
            dve.wait_ge(pe_done, 2)
            link(dve.memset(scanned[:, :], 0.0))
            link(dve.tensor_copy(carry_t[:, :], c_ps[0:R, 0:P]))
            link(dve.tensor_tensor_scan(scanned[:, 1:P + 1], k.ones[0:R, 0:P], carry_t[:, :], 0.0, ALU.mult, ALU.max))
            dve.sem_inc(pe_asked, 1)
            dve.wait_ge(pe_done, 3)
            link(dve.tensor_copy(carry[:, :], c_ps[:, 0:R]))
            for r in range(R):
                link(dve.tensor_scalar(begin[:, r, :], begin[:, r, :], carry[:, r:r + 1], None, ALU.max))
            lb = last_f[:, :].rearrange("p (a t) -> p a t", a=1).to_broadcast([P, R, T])
            link(dve.tensor_scalar(hold[:, :, :], upto[:, :, :], -1.0, float(P * T), ALU.mult, ALU.add))
            link(dve.tensor_tensor(hold[:, :, :], hold[:, :, :], lb, ALU.mult))
            for r in range(R):
                link(dve.tensor_tensor_scan(count[:, r, ::-1], k.ones[:, 0:T], hold[:, r, ::-1], 0.0, ALU.mult, ALU.max))
            dve.tensor_copy(per[:, :], count[:, :, 0]).then_inc(pe_asked, 1)
            dve.wait_ge(pe_done, 4)
            link(dve.memset(scanned[:, :], 0.0))
            link(dve.tensor_copy(carry_t[:, :], c_ps[0:R, 0:P]))
            link(dve.tensor_tensor_scan(scanned[:, P - 1::-1], k.ones[0:R, 0:P], carry_t[:, ::-1], 0.0,
                                        ALU.mult, ALU.max))
            dve.sem_inc(pe_asked, 1)
            dve.wait_ge(pe_done, 5)
            link(dve.tensor_copy(carry[:, :], c_ps[:, 0:R]))
            for r in range(R):
                link(dve.tensor_scalar(count[:, r, :], count[:, r, :], carry[:, r:r + 1], None, ALU.max))
            link(dve.tensor_tensor(count[:, :, :], count[:, :, :], begin[:, :, :], ALU.add))
            link(dve.tensor_scalar(count[:, :, :], count[:, :, :], -1.0, float(P * T), ALU.mult, ALU.add))
            link(dve.tensor_reduce(mine[:, :], count[:, :, :].rearrange("p r t -> p t r"), AX.X, ALU.add))
            link(dve.tensor_scalar(mine[:, :], mine[:, :], 1.0, None, ALU.add))
            dve.reciprocal(deg_inv[:, :], mine[:, :]).then_inc(deg_ready, 1)
            link(dve.tensor_tensor(hold[:, :, :], count[:, :, :], of_r[:, :, :], ALU.mult))
            dve.wait_ge(w_ready, 1)
            link(dve.tensor_reduce(mine[:, :], hold[:, :, :].rearrange("p r t -> p t r"), AX.X, ALU.add))
            dve.reciprocal(weight[:, 1, :], mine[:, :]).then_inc(w_ready, 1)
            dve.wait_ge(w_turned, 1)
            link(dve.tensor_copy(k.dinv[:, :], a_ps[:, 0:T]))
            link(dve.tensor_copy(mine[:, :], a_ps[:, T:2 * T]))
            for r in range(R):
                link(dve.tensor_scalar(nxt[:, 0, :], typ[:, :], float(r), None, ALU.is_equal))
                link(dve.tensor_tensor(k.rel_weight[:, :, r], nxt[:, 0, :], mine[:, :], ALU.mult))

        @block.tensor
        def _(pe):
            pe.wait_ge(turn_asked, 1)
            pe.wait_ge(nxt_ready, 1)
            for half in range(2):
                for w, table in enumerate((keys[:, 0, :], typ[:, :])):
                    last = pe.transpose(a_ps[0:H, (w * 2 + half) * P:(w * 2 + half + 1) * P],
                                        table[:, half * H:(half + 1) * H], k.ident[:, :])
            last.then_inc(turn_ready, 1)
            for o in range(2):
                pe.matmul(b_ps[:, o * T:(o + 1) * T], k.shift[:, :], keys[:, o, 0:T], start=True, stop=False)
                last = pe.matmul(b_ps[:, o * T:(o + 1) * T], k.wrap[:, :], keys[:, o, 1:T + 1], start=False, stop=True)
            last.then_inc(nxt_done, 1)
            pe.wait_ge(key_asked, 1)
            pe.matmul(c_ps[:, 0:1], k.shift[:, :], edge_key[:, 0:1], start=True, stop=True)

            pe.matmul(c_ps[:, 1:2], k.unshift[:, :], edge_key[:, 1:2], start=True, stop=True).then_inc(key_done, 1)
            pe.wait_ge(pe_asked, 1)
            pe.matmul(c_ps[:, 0:R], k.before[:, :], per[:, :], start=True, stop=True).then_inc(pe_done, 1)
            pe.wait_ge(pe_asked, 2)
            pe.transpose(c_ps[0:R, 0:P], per[:, :], k.ident[:, :]).then_inc(pe_done, 1)
            pe.wait_ge(pe_asked, 3)
            pe.transpose(c_ps[:, 0:R], scanned[:, 0:P], k.ident[0:R, 0:R]).then_inc(pe_done, 1)
            pe.wait_ge(pe_asked, 4)
            pe.transpose(c_ps[0:R, 0:P], per[:, :], k.ident[:, :]).then_inc(pe_done, 1)
            pe.wait_ge(pe_asked, 5)
            pe.transpose(c_ps[:, 0:R], scanned[:, 1:P + 1], k.ident[0:R, 0:R]).then_inc(pe_done, 1)
            pe.wait_ge(w_in, 32)
            for w in range(2):
                for half in range(2):
                    last = pe.transpose(a_ps[:, w * T + half * H:w * T + (half + 1) * H],
                                        w_rows[:, w, half, :], k.ident[0:H, 0:H])
            last.then_inc(w_turned, 1)

        @block.scalar
        def _(act):
            act.wait_ge(deg_ready, 1)
            act.activation(weight[:, 0, :], deg_inv[:, :], ACT.Sqrt).then_inc(w_ready, 1)

        @block.sync
        def _(sp):
            sp.wait_ge(rows_ready, 1)
            for half in range(2):
                sp.dma_start(flat_dram[half * H:(half + 1) * H], turned[:, :, half, :]).then_inc(flat_out, 16)
            sp.wait_ge(flat_out, 32)
            sp.dma_start(flat[:, :, :], flat_rows).then_inc(flat_in, 16)
            sp.wait_ge(w_ready, 2)
            sp.wait_ge(flat_in, 16)
            sp.dma_start(flat_rows, weight[:, :, :]).then_inc(w_out, 16)
            sp.wait_ge(w_out, 16)
            for half in range(2):
                sp.dma_start(w_rows[:, :, half, :], flat_dram[half * H:(half + 1) * H]).then_inc(w_in, 16)
            sp.wait_ge(w_in, 32)


def split_rows(nc, k):
    with Phase(nc) as ctx:
        sb = lambda name, shape, dt=F32: ctx.enter_context(nc.sbuf_tensor("sp_" + name, shape, dt))
        V = len(k.vectors)
        whole, rest, rest2 = (sb(n, [3, V, C]) for n in ("whole", "rest", "rest2"))
        part = [sb(f"part{i}", [3, V, C], BF16) for i in range(3)]
        sel = sb("sel", [3, 3])
        acc = sb("acc", [3, V, C])
        chain = ctx.semaphore("sp_chain")
        rows_in = ctx.semaphore("sp_rows_in")
        exponent = ctx.semaphore("sp_exponent")
        block = ctx.enter_context(nc.Block())

        @block.sync
        def _(sp):
            for v, vector in enumerate(k.vectors):
                for i in range(3):
                    sp.dma_start(whole[i:i + 1, v, :], vector.rearrange("(a c) -> a c", a=1)).then_inc(rows_in, 16)
            sp.wait_ge(rows_in, 16 * 3 * V)

        @block.gpsimd
        def _(pool):
            pool.memset(k.minus_half[:, :], -0.5).then_inc(exponent, 1)
            pool.wait_ge(exponent, 1)
            pool.tensor_scalar(k.node_dinv[:, :], k.indeg[:, :], 1.0, None, ALU.add).then_inc(exponent, 1)
            pool.tensor_scalar(k.whole[:, :], k.indeg[:, :], 0.5, None, ALU.is_lt).then_inc(exponent, 1)
            pool.wait_ge(exponent, 3)
            pool.tensor_tensor(k.node_dinv[:, :], k.node_dinv[:, :], k.minus_half[:, :], ALU.pow).then_inc(exponent, 1)
            pool.wait_ge(exponent, 4)

        @block.vector
        def _(dve):
            links = [0]

            def link(ins):
                links[0] += 1
                ins.then_inc(chain, 1)
                dve.wait_ge(chain, links[0])

            link(dve.memset(k.ones3[:, :], 1.0))
            dve.wait_ge(rows_in, 16 * 3 * V)
            link(dve.tensor_copy(part[0][:, :, :], whole[:, :, :]))
            link(dve.tensor_tensor(rest[:, :, :], whole[:, :, :], part[0][:, :, :], ALU.subtract))
            link(dve.tensor_copy(part[1][:, :, :], rest[:, :, :]))
            link(dve.tensor_tensor(rest2[:, :, :], rest[:, :, :], part[1][:, :, :], ALU.subtract))
            link(dve.tensor_copy(part[2][:, :, :], rest2[:, :, :]))
            for i in range(3):
                link(dve.tensor_scalar(sel[:, i:i + 1], k.part[0:3, :], float(i), None, ALU.is_equal))
            link(dve.tensor_scalar(acc[:, :, :], part[0][:, :, :], sel[:, 0:1], None, ALU.mult))
            for i in (1, 2):
                link(dve.scalar_tensor_tensor(acc[:, :, :], part[i][:, :, :], sel[:, i:i + 1], acc[:, :, :],
                                              ALU.mult, ALU.add))
            link(dve.tensor_copy(k.rows3[:, :, :], acc[:, :, :]))


def node_rows(table, g, rows):
    return table[bass.ds(g * GROUP, rows * J), :].rearrange("(p j) c -> p j c", j=J)


def each_group(eng, group):
    with eng.Fori(0, FULL // 2) as i:
        group([(i * 2 + b, b, i * 2 + b + 1, P) for b in range(2)])
    rest = list(range(FULL // 2 * 2, NG))
    group([(g, g % 2, g + 1, P if g < FULL else TAIL) for g in rest])


class Turns:

    def __init__(self, nc, ctx, prefix, L, steps, moves, soft=""):
        self.L = L
        self.steps = {name: ctx.semaphore(f"{prefix}_{name}") for name in steps.split()}
        self.moves = {name: [ctx.semaphore(f"{prefix}_{name}{b}") for b in range(L)]
                      for name in (moves + " " + soft).split()}
        self.start = {name: 0 if name in soft.split() else 16 for name in self.moves}

    def __getitem__(self, name):
        return self.steps[name]

    def credit(self, eng):
        for step in self.steps.values():
            eng.sem_inc(step, self.L)
        for name, lanes in self.moves.items():
            for lane in lanes:
                if self.start[name]:
                    eng.sem_inc(lane, self.start[name])

    def done(self, eng, name, n):
        eng.wait_ge(self.steps[name], n + self.L)

    def freed(self, eng, name, n, back=0):
        eng.wait_ge(self.steps[name], n + self.L - (back or self.L))

    def landed(self, eng, name, b, n):
        eng.wait_ge(self.moves[name][b], (n - b - 1) * (16 // self.L) + 16 + self.start[name])

    def drained(self, eng, name, b, n):
        if isinstance(n, int) and n <= self.L and not self.start[name]:
            return
        eng.wait_ge(self.moves[name][b], (n - b - 1) * (16 // self.L) + self.start[name])

    def drain(self, eng, name, count):
        for n in range(count + 1, count + self.L + 1):
            self.drained(eng, name, (n - 1) % self.L, n)


def row_blocks(bank):
    return bank[:, :].rearrange("c (j p) -> c j p", j=J)


def nodes_first(nc, k):
    with Phase(nc) as ctx:
        sb = lambda name, shape, dt=F32: ctx.enter_context(nc.sbuf_tensor("n1_" + name, shape, dt))
        X, XN, H, G, X1, XN1, H1, O, OSQ = ([sb(f"{n}{b}", [P, J, C]) for b in range(2)]
                                            for n in ("X", "XN", "H", "G", "X1", "XN1", "H1", "O", "OSQ"))
        HT, GT, H1T = ([sb(f"{n}{b}", [C, J, P]) for b in range(2)] for n in ("HT", "GT", "H1T"))
        six = [sb(f"six{b}", [P, 2, J, 6]) for b in range(2)]
        mv = [sb(f"mv{b}", [P, 2, J, 2]) for b in range(2)]
        ve, rs = ([sb(f"{n}{b}", [P, 2, J]) for b in range(2)] for n in ("ve", "rs"))
        rsd = [sb(f"rsd{b}", [P, 1, J]) for b in range(2)]
        whole = [sb(f"whole{b}", [P, J]) for b in range(2)]
        q = [[ctx.enter_context(nc.psum_tensor(f"n1_q{i}{b}", [P, 512], F32)) for i in range(3)] for b in range(2)]
        stat_ps = ctx.enter_context(nc.psum_tensor("n1_stat", [P, 512], F32))
        w = Turns(nc, ctx, "n1", 2,
                  "six_a mv_a ve_a rs_a rsd_a xn_a h_a hT_a ht_a w1 gt g_ps g w2 x1 "
                  "six_b mv_b ve_b rs_b xn_b h_b hT_b ht_b root o osq whole stats", "x_in h_out g_out x1_out o_out")
        stats_taken = ctx.semaphore("n1_stats_taken")
        turn = ctx.semaphore("n1_turn")
        dve_turn = ctx.semaphore("n1_dve_turn")
        block = ctx.enter_context(nc.Block())

        @block.sync
        def _(sp):
            w.credit(sp)

            def group(lanes):
                for g, b, n, rows in lanes:
                    w.freed(sp, "x1", n)
                    sp.dma_start(X[b][0:rows], node_rows(k.x, g, rows)).then_inc(w.moves["x_in"][b], 16)
                for table, tile, step, move in ((k.H0, H, "h_a", "h_out"), (k.G1, G, "g", "g_out"),
                                                (k.X1, X1, "x1", "x1_out"), (k.O, O, "o", "o_out")):
                    for g, b, n, rows in lanes:
                        w.done(sp, step, n)
                        sp.dma_start(node_rows(table, g, rows), tile[b][0:rows]).then_inc(w.moves[move][b], 16)

            each_group(sp, group)
            for lanes in w.moves.values():
                for lane in lanes:
                    sp.wait_ge(lane, 16 * (NG // 2 + 1))

        @block.vector
        def _(dve):
            def stats(lanes, X, ln, ab):
                for g, b, n, rows in lanes:
                    w.freed(dve, "mv" + ab, n)
                    if ln == 0:
                        w.landed(dve, "x_in", b, n)
                    else:
                        w.done(dve, "x1", n)
                    for j in range(J):
                        last = dve.bn_stats(six[b][0:rows, ln, j, :], X[b][0:rows, j, :])
                    last.then_inc(w["six" + ab], 1)
                for g, b, n, rows in lanes:
                    w.done(dve, "six" + ab, n)
                    w.freed(dve, "xn" + ab, n)
                    dve.sem_inc(dve_turn, 1)
                    for j in range(J):
                        last = dve.bn_aggr(mv[b][0:rows, ln, j, :], six[b][0:rows, ln, j, :])
                    last.then_inc(w["mv" + ab], 1)

            def normal(lanes, X, XN, ln, ab, scale, scale_step):
                for g, b, n, rows in lanes:
                    w.done(dve, scale_step, n)
                    w.freed(dve, "h" + ab, n)
                    for j in range(J):
                        last = dve.tensor_scalar(XN[b][0:rows, j, :], X[b][0:rows, j, :], mv[b][0:rows, ln, j, 0:1],
                                                 scale[b][0:rows, ln, j:j + 1], ALU.subtract, ALU.mult)
                    last.then_inc(w["xn" + ab], 1)

            def group(lanes):
                stats(lanes, X, 0, "_a")
                normal(lanes, X, XN, 0, "_a", rsd, "rsd_a")
                for g, b, n, rows in lanes:
                    w.done(dve, "w2", n)
                    w.drained(dve, "x1_out", b, n)
                    w.freed(dve, "xn_b", n)
                    dve.tensor_tensor(X1[b][0:rows].rearrange("p j c -> p (j c)"), q[b][2][0:rows, :],
                                      X[b][0:rows].rearrange("p j c -> p (j c)"), ALU.add).then_inc(w["x1"], 1)
                stats(lanes, X1, 1, "_b")
                normal(lanes, X1, XN1, 1, "_b", rs, "rs_b")

            each_group(dve, group)
            dve.wait_ge(w["stats"], NG + 2)
            dve.tensor_copy(k.stats_whole[:, :], stat_ps[:, 0:2]).then_inc(stats_taken, 1)
            dve.wait_ge(stats_taken, 1)

        @block.gpsimd
        def _(pool):
            def scales(lanes, ln, ab):
                for g, b, n, rows in lanes:
                    w.done(pool, "mv" + ab, n)
                    w.freed(pool, "rs" + ab, n)
                    pool.sem_inc(turn, 1)
                    pool.tensor_scalar(ve[b][0:rows, ln, :], mv[b][0:rows, ln, :, 1], EPS, None, ALU.add)\
                        .then_inc(w["ve" + ab], 1)
                for g, b, n, rows in lanes:
                    w.done(pool, "ve" + ab, n)
                    if ln == 0:
                        w.freed(pool, "rsd_a", n)
                    pool.tensor_tensor(rs[b][0:rows, ln, :], ve[b][0:rows, ln, :], k.minus_half[0:rows, 0:J], ALU.pow)\
                        .then_inc(w["rs" + ab], 1)

            def relu(lanes, XN, H, ab):
                for g, b, n, rows in lanes:
                    w.done(pool, "xn" + ab, n)
                    w.freed(pool, "hT" + ab, n)
                    if ab == "_a":
                        w.drained(pool, "h_out", b, n)
                    pool.sem_inc(turn, 1)
                    pool.tensor_scalar(H[b][0:rows], XN[b][0:rows], 0.0, None, ALU.max).then_inc(w["h" + ab], 1)

            def group(lanes):
                for g, b, n, rows in lanes:
                    w.freed(pool, "stats", n)
                    pool.sem_inc(turn, 1)
                    pool.tensor_copy(whole[b][:, :], k.whole[:, bass.ds(g * J, J)]).then_inc(w["whole"], 1)
                scales(lanes, 0, "_a")
                for g, b, n, rows in lanes:
                    w.done(pool, "rs_a", n)
                    pool.sem_inc(turn, 1)
                    pool.tensor_tensor(rsd[b][0:rows, 0, :], rs[b][0:rows, 0, :],
                                       k.node_dinv[0:rows, bass.ds(g * J, J)], ALU.mult).then_inc(w["rsd_a"], 1)
                relu(lanes, XN, H, "_a")
                scales(lanes, 1, "_b")
                relu(lanes, XN1, H1, "_b")

            each_group(pool, group)

        @block.tensor
        def _(pe):
            pe.matmul(stat_ps[:, 0:2], k.zero_row[:, :], k.zero_row[:, 0:2], start=True, stop=True, skip_group_check=True)

            def rowwise(dst, src, weight, v, rows):
                pe.matmul(dst[0:rows, :].rearrange("p (j c) -> p j c", j=J), k.ones3[:, 0:rows],
                          k.rows3[:, v:v + 1, :].to_broadcast([3, J, C]), start=True, stop=False, skip_group_check=True)
                for j in range(J):
                    last = pe.matmul(dst[0:rows, j * C:(j + 1) * C], src[:, j, 0:rows], weight[:, :], start=False,
                                     stop=True, skip_group_check=True)
                return last

            def turned(dst, src, rows):
                for j in range(J):
                    last = pe.transpose(dst[:, j * P:j * P + rows], src[0:rows, j, :], k.ident[0:rows, 0:rows])
                return last

            def group(lanes):
                for g, b, n, rows in lanes:
                    w.done(pe, "h_a", n)
                    w.freed(pe, "g", n)
                    turned(q[b][0], H[b], rows).then_inc(w["hT_a"], 1)
                for g, b, n, rows in lanes:
                    w.done(pe, "ht_a", n)
                    w.freed(pe, "ht_b", n)
                    pe.matmul(row_blocks(q[b][1])[:, :, 0:rows], k.w1[:, :], HT[b][:, :, 0:rows],
                              start=True, stop=True).then_inc(w["w1"], 1)
                for g, b, n, rows in lanes:
                    w.done(pe, "gt", n)
                    for j in range(J):
                        last = pe.transpose(q[b][0][0:rows, j * C:(j + 1) * C], GT[b][:, j, 0:rows], k.ident[:, :])
                    last.then_inc(w["g_ps"], 1)
                    w.freed(pe, "osq", n)
                    rowwise(q[b][2], GT[b], k.w2, 1, rows).then_inc(w["w2"], 1)
                for g, b, n, rows in lanes:
                    w.done(pe, "h_b", n)
                    turned(q[b][1], H1[b], rows).then_inc(w["hT_b"], 1)
                for g, b, n, rows in lanes:
                    w.done(pe, "ht_b", n)
                    rowwise(q[b][2], H1T[b], k.root, 2, rows).then_inc(w["root"], 1)
                for g, b, n, rows in lanes:
                    w.done(pe, "osq", n)
                    w.done(pe, "whole", n)
                    for c, src in enumerate((O, OSQ)):
                        for j in range(J):
                            last = pe.matmul(stat_ps[:, c:c + 1], src[b][0:rows, j, :], whole[b][0:rows, j:j + 1],
                                             start=False, stop=True, skip_group_check=True)
                    last.then_inc(w["stats"], 1)

            each_group(pe, group)

        @block.scalar
        def _(act):
            def group(lanes):
                for g, b, n, rows in lanes:
                    w.done(act, "hT_a", n)
                    w.freed(act, "w1", n)
                    act.copy(HT[b][:, :, 0:rows], row_blocks(q[b][0])[:, :, 0:rows]).then_inc(w["ht_a"], 1)
                for g, b, n, rows in lanes:
                    w.done(act, "w1", n)
                    w.freed(act, "w2", n)
                    act.activation(GT[b][:, :, 0:rows], row_blocks(q[b][1])[:, :, 0:rows], ACT.Relu,
                                   bias=k.b1_col[:, :]).then_inc(w["gt"], 1)
                for g, b, n, rows in lanes:
                    w.done(act, "g_ps", n)
                    w.drained(act, "g_out", b, n)
                    act.copy(G[b][0:rows].rearrange("p j c -> p (j c)"), q[b][0][0:rows, :]).then_inc(w["g"], 1)
                for g, b, n, rows in lanes:
                    w.done(act, "hT_b", n)
                    w.freed(act, "root", n)
                    act.copy(H1T[b][:, :, 0:rows], row_blocks(q[b][1])[:, :, 0:rows]).then_inc(w["ht_b"], 1)
                for g, b, n, rows in lanes:
                    w.done(act, "root", n)
                    w.drained(act, "o_out", b, n)
                    w.freed(act, "stats", n)
                    act.copy(O[b][0:rows].rearrange("p j c -> p (j c)"), q[b][2][0:rows, :]).then_inc(w["o"], 1)
                    act.activation(OSQ[b][0:rows].rearrange("p j c -> p (j c)"), q[b][2][0:rows, :],
                                   ACT.Square).then_inc(w["osq"], 1)

            each_group(act, group)


L = 4
LONG = 8


def each_step(eng, step, lag, count=T, L=L):
    for i in range(2 * L):
        step(i, i)
    with eng.Fori(2, count // L) as r:
        for b in range(L):
            step(r * L + b, b)
    for i in range(count // L * L, count + lag):
        step(i, i)


def live(t, count=T):
    return not isinstance(t, int) or 0 <= t < count


def tile_rows(table, t):
    return table[bass.ds(t * P, P), :]


class EdgePass:

    def __init__(self, nc, ctx, prefix, k, order, steps, moves, soft, L=L):
        self.k, self.o, self.L = k, order, L
        sb = lambda name, shape, dt=F32: ctx.enter_context(nc.sbuf_tensor(f"{prefix}_{name}", shape, dt))
        self.w = Turns(nc, ctx, prefix, L, "ids sid keys krow masks tot totsb " + steps, moves, soft)
        self.gid = [sb(f"gid{b}", [P, 2], I32) for b in range(L)]
        self.sid = [sb(f"sid{b}", [P, 1], I32) for b in range(L)]
        self.keys = [sb(f"keys{b}", [P, 2]) for b in range(L)]
        self.same, self.carry = ([sb(f"{n}{b}", [P, P]) for b in range(L)] for n in ("same", "carry"))
        self.totsb = [sb(f"totsb{b}", [P, C]) for b in range(L)]
        self.zeroed = ctx.semaphore(f"{prefix}_zeroed")
        self.turn = {e: ctx.semaphore(f"{prefix}_turn_{e}") for e in ("pool", "dve", "act")}

    def start(self, dve):
        dve.memset(self.totsb[self.L - 1][:, :], 0.0).then_inc(self.zeroed, 1)

    def load_ids(self, pool, t, b, n, gathered):
        for move in gathered:
            self.w.drained(pool, move, b, n)
        pool.sem_inc(self.turn["pool"], 1)
        pool.tensor_copy(self.gid[b][:, :], self.k.index[:, self.o, bass.ds(t, 1), 0:2].rearrange("p a c -> p (a c)"))\
            .then_inc(self.w["ids"], 1)

    def gather(self, pool, tile, table, which, b, n, move):
        self.w.done(pool, "ids", n)
        pool.sem_inc(self.turn["pool"], 1)
        pool.indirect_dma_start(tile, None, table, bass.IndirectOffsetOnAxis(ap=self.gid[b][:, which:which + 1], axis=0))\
            .then_inc(self.w.moves[move][b], 16)

    def scatter(self, pool, table, tile, t, b, n, move):
        self.w.drained(pool, move, b, n)
        pool.sem_inc(self.turn["pool"], 1)
        pool.tensor_copy(self.sid[b][:, :], self.k.index[:, self.o, bass.ds(t, 1), 2]).then_inc(self.w["sid"], 1)
        self.w.done(pool, "sid", n)
        pool.sem_inc(self.turn["pool"], 1)
        pool.indirect_dma_start(table, bass.IndirectOffsetOnAxis(ap=self.sid[b][:, 0:1], axis=0), tile, None,
                                bounds_check=N - 1, oob_is_err=False).then_inc(self.w.moves[move][b], 16)

    def load_keys(self, dve, t, b, n):
        self.w.freed(dve, "masks", n)
        dve.tensor_copy(self.keys[b][:, :], self.k.key[:, self.o, bass.ds(t, 2)]).then_inc(self.w["keys"], 1)

    def spread_keys(self, pe, banks, b, n, back=2):
        self.w.done(pe, "keys", n)
        self.w.freed(pe, "masks", n, back)
        pe.matmul(banks[b % 2][:, 0:P], self.keys[b][:, 1:2].to_broadcast([P, P]), self.k.ident[:, :], start=True,
                  stop=True).then_inc(self.w["krow"], 1)

    def masks(self, dve, banks, b, n):
        self.w.done(dve, "krow", n)
        self.w.freed(dve, "tot", n)
        dve.tensor_scalar(self.same[b][:, :], banks[b % 2][:, 0:P], self.keys[b][:, 1:2], None, ALU.is_equal)
        dve.tensor_scalar(self.carry[b][:, :], banks[b % 2][:, 0:P], self.keys[b][:, 0:1], self.k.last[:, :],
                          ALU.is_equal, ALU.mult).then_inc(self.w["masks"], 1)

    def sums(self, pe, banks, parts, b, n):
        self.w.done(pe, "masks", n)
        self.w.done(pe, "totsb", n - 1)
        for i, rows in enumerate(parts):
            pe.matmul(banks[b % 2][:, 0:C], self.same[b][:, :], rows, start=i == 0, stop=False)
        pe.matmul(banks[b % 2][:, 0:C], self.carry[b][:, :], self.totsb[(b - 1) % self.L][:, :], start=False,
                  stop=True).then_inc(self.w["tot"], 1)

    def keep_sums(self, act, banks, b, n):
        self.w.done(act, "tot", n)
        act.copy(self.totsb[b][:, :], banks[b % 2][:, 0:C]).then_inc(self.w["totsb"], 1)


class Norm:

    STEPS = "ln_six ln_mv ln_ve ln_iv ln_rs "

    def __init__(self, nc, ctx, prefix, w, S, go, used, name="ln"):
        L = w.L
        sb = lambda n, shape: [ctx.enter_context(nc.sbuf_tensor(f"{prefix}_{name}_{n}{b}", shape, F32)) for b in range(L)]
        self.w, self.S, self.go, self.name = w, S, go, name
        self.used = used
        self.six, self.mv = sb("six", [P, S, 6]), sb("mv", [P, S, 2])
        self.ve, self.iv, self.rs = (sb(n, [P, S]) for n in ("ve", "iv", "rs"))

    def stats(self, dve, X, b, n):
        w, a = self.w, self.name
        w.freed(dve, a + "_mv", n)
        for s in range(self.S):
            last = dve.bn_stats(self.six[b][:, s, :], X[:, s, :])
        last.then_inc(w[a + "_six"], 1)
        w.done(dve, a + "_six", n)
        w.freed(dve, self.used, n)
        dve.sem_inc(self.go, 1)
        for s in range(self.S):
            last = dve.bn_aggr(self.mv[b][:, s, :], self.six[b][:, s, :])
        last.then_inc(w[a + "_mv"], 1)
        w.done(dve, a + "_mv", n)
        dve.tensor_scalar(self.ve[b][:, :], self.mv[b][:, :, 1], EPS, None, ALU.add).then_inc(w[a + "_ve"], 1)

    def inverse(self, dve, b, n):
        self.w.done(dve, self.name + "_ve", n)
        dve.reciprocal(self.iv[b][:, :], self.ve[b][:, :]).then_inc(self.w[self.name + "_iv"], 1)

    def root(self, act, b, n):
        self.w.done(act, self.name + "_iv", n)
        act.activation(self.rs[b][:, :], self.iv[b][:, :], ACT.Sqrt).then_inc(self.w[self.name + "_rs"], 1)


def edges_first(nc, k):
    with Phase(nc) as ctx:
        sb = lambda name, shape: [ctx.enter_context(nc.sbuf_tensor(f"e1_{name}{b}", shape, F32)) for b in range(L)]
        p = EdgePass(nc, ctx, "e1", k, 0, Norm.STEPS + "rs3 dv nm a aT at y go hd", "slot_x slot_g", "g_in x_in go_out")
        w = p.w
        ln = Norm(nc, ctx, "e1", w, 1, p.turn["dve"], "nm")
        GS, HD, A, AT, GO = (sb(n, [P, C]) for n in ("GS", "HD", "A", "AT", "GO"))
        XD = sb("XD", [P, 1, C])
        rs3, nm, dv = (sb(n, [P, 1]) for n in ("rs3", "nm", "dv"))
        krow, tot, aT, y = ([ctx.enter_context(nc.psum_tensor(f"e1_{n}{b}", [P, 512], F32)) for b in range(2)]
                            for n in ("krow", "tot", "aT", "y"))
        block = ctx.enter_context(nc.Block())

        @block.sync
        def _(sp):
            w.credit(sp)

            def step(i, b):
                t, b1, n = i - 1, (b - 1) % L, i
                if live(t):
                    w.landed(sp, "x_in", b1, n)
                    sp.dma_start(tile_rows(k.slot_x, t), XD[b1][:, 0, :]).then_inc(w.moves["slot_x"][b1], 16)
                t, b5, n = i - 5, (b - 5) % L, i - 4
                if live(t):
                    w.done(sp, "go", n)
                    sp.dma_start(tile_rows(k.slot_g, t), GO[b5][:, :]).then_inc(w.moves["slot_g"][b5], 16)

            each_step(sp, step, 5)
            w.drain(sp, "slot_x", T)
            w.drain(sp, "slot_g", T)

        @block.gpsimd
        def _(pool):
            def step(i, b):
                t, b, n = i, b % L, i + 1
                if live(t):
                    p.load_ids(pool, t, b, n, ("g_in", "x_in"))
                    w.freed(pool, "tot", n)
                    p.gather(pool, GS[b][:, :], k.H0, 0, b, n, "g_in")
                    w.freed(pool, "hd", n)
                    w.drained(pool, "slot_x", b, n)
                    p.gather(pool, XD[b][:, 0, :], k.x, 1, b, n, "x_in")
                t, b, n = i - 5, (b - 5) % L, i - 4
                if live(t):
                    w.done(pool, "go", n)
                    p.scatter(pool, k.G1, GO[b][:, :], t, b, n, "go_out")

            each_step(pool, step, 5)
            w.drain(pool, "go_out", T)

        @block.vector
        def _(dve):
            p.start(dve)

            def step(i, b0):
                t, b, n = i, b0 % L, i + 1
                if live(t):
                    p.load_keys(dve, t, b, n)
                t, b, n = i - 3, (b0 - 3) % L, i - 2
                if live(t):
                    w.done(dve, "totsb", n)
                    w.done(dve, "hd", n)
                    w.freed(dve, "aT", n)
                    dve.scalar_tensor_tensor(A[b][:, :], p.totsb[b][:, :], dv[b][:, :], HD[b][:, :], ALU.mult,
                                             ALU.add).then_inc(w["a"], 1)
                t, b, n = i - 2, (b0 - 2) % L, i - 1
                if live(t):
                    w.done(dve, "ln_rs", n)
                    w.done(dve, "dv", n)
                    w.freed(dve, "hd", n)
                    dve.tensor_scalar(rs3[b][:, :], ln.rs[b][:, :], dv[b][:, :], dv[b][:, :], ALU.mult, ALU.mult)\
                        .then_inc(w["rs3"], 1)
                    w.done(dve, "rs3", n)
                    dve.tensor_scalar(nm[b][:, :], ln.mv[b][:, :, 0], rs3[b][:, :], -1.0, ALU.mult, ALU.mult)\
                        .then_inc(w["nm"], 1)
                t, b, n = i - 1, (b0 - 1) % L, i
                if live(t):
                    w.freed(dve, "go", n)
                    w.freed(dve, "a", n)
                    dve.tensor_copy(dv[b][:, :], k.dinv[:, bass.ds(t, 1)]).then_inc(w["dv"], 1)
                    p.masks(dve, krow, b, n)
                    w.landed(dve, "x_in", b, n)
                    w.freed(dve, "nm", n)
                    ln.stats(dve, XD[b], b, n)
                    ln.inverse(dve, b, n)

            each_step(dve, step, 3)

        @block.tensor
        def _(pe):
            pe.wait_ge(p.zeroed, 1)

            def step(i, b0):
                t, b, n = i, b0 % L, i + 1
                if live(t):
                    p.spread_keys(pe, krow, b, n)
                t, b, n = i - 4, (b0 - 4) % L, i - 3
                if live(t):
                    w.done(pe, "at", n)
                    w.freed(pe, "go", n, 2)
                    pe.matmul(y[b % 2][:, 0:C], k.ones3[:, :], k.rows3[:, 0, :], start=True, stop=False, skip_group_check=True)
                    pe.matmul(y[b % 2][:, 0:C], AT[b][:, :], k.w1[:, :], start=False, stop=True, skip_group_check=True)\
                        .then_inc(w["y"], 1)
                t, b, n = i - 3, (b0 - 3) % L, i - 2
                if live(t):
                    w.done(pe, "a", n)
                    w.freed(pe, "at", n, 2)
                    pe.transpose(aT[b % 2][:, 0:P], A[b][:, :], k.ident[:, :]).then_inc(w["aT"], 1)
                t, b, n = i - 1, (b0 - 1) % L, i
                if live(t):
                    w.landed(pe, "g_in", b, n)
                    p.sums(pe, tot, [GS[b][:, :]], b, n)

            each_step(pe, step, 4)

        @block.scalar
        def _(act):
            def step(i, b0):
                t, b, n = i - 4, (b0 - 4) % L, i - 3
                if live(t):
                    w.done(act, "y", n)
                    w.drained(act, "go_out", b, n)
                    w.drained(act, "slot_g", b, n)
                    act.activation(GO[b][:, :], y[b % 2][:, 0:C], ACT.Relu, scale=dv[b][:, :]).then_inc(w["go"], 1)
                t, b, n = i - 2, (b0 - 2) % L, i - 1
                if live(t):
                    w.done(act, "nm", n)
                    w.freed(act, "a", n)
                    act.activation(HD[b][:, :], XD[b][:, 0, :], ACT.Relu, bias=nm[b][:, :], scale=rs3[b][:, :])\
                        .then_inc(w["hd"], 1)
                t, b, n = i - 3, (b0 - 3) % L, i - 2
                if live(t):
                    w.done(act, "aT", n)
                    w.freed(act, "y", n)
                    act.copy(AT[b][:, :], aT[b % 2][:, 0:P]).then_inc(w["at"], 1)
                t, b, n = i - 1, (b0 - 1) % L, i
                if live(t):
                    w.freed(act, "a", n)
                    p.keep_sums(act, tot, b, n)
                    ln.root(act, b, n)

            each_step(act, step, 4)


def edges_second(nc, k):
    with Phase(nc) as ctx:
        sb = lambda name, shape: [ctx.enter_context(nc.sbuf_tensor(f"e2_{name}{b}", shape, F32)) for b in range(L)]
        p = EdgePass(nc, ctx, "e2", k, 0, "dv a as aT at y xo", "x_in d_in slot_x", "g_in xo_out")
        w = p.w
        GS, XD, GD, A, AS, AT, XO = (sb(n, [P, C]) for n in ("GS", "XD", "GD", "A", "AS", "AT", "XO"))
        dv = sb("dv", [P, 1])
        krow, tot, aT, y = ([ctx.enter_context(nc.psum_tensor(f"e2_{n}{b}", [P, 512], F32)) for b in range(2)]
                            for n in ("krow", "tot", "aT", "y"))
        block = ctx.enter_context(nc.Block())

        @block.sync
        def _(sp):
            w.credit(sp)

            def step(i, b0):
                t, b, n = i, b0 % L, i + 1
                if live(t):
                    w.freed(sp, "xo", n)
                    sp.dma_start(XD[b][:, :], tile_rows(k.slot_x, t)).then_inc(w.moves["x_in"][b], 16)
                    w.freed(sp, "a", n)
                    sp.dma_start(GD[b][:, :], tile_rows(k.slot_g, t)).then_inc(w.moves["d_in"][b], 16)
                t, b, n = i - 4, (b0 - 4) % L, i - 3
                if live(t):
                    w.done(sp, "xo", n)
                    sp.dma_start(tile_rows(k.slot_x2, t), XO[b][:, :]).then_inc(w.moves["slot_x"][b], 16)

            each_step(sp, step, 4)
            w.drain(sp, "slot_x", T)

        @block.gpsimd
        def _(pool):
            def step(i, b0):
                t, b, n = i, b0 % L, i + 1
                if live(t):
                    p.load_ids(pool, t, b, n, ("g_in",))
                    w.freed(pool, "tot", n)
                    p.gather(pool, GS[b][:, :], k.G1, 0, b, n, "g_in")
                t, b, n = i - 4, (b0 - 4) % L, i - 3
                if live(t):
                    w.done(pool, "xo", n)
                    p.scatter(pool, k.X1, XO[b][:, :], t, b, n, "xo_out")

            each_step(pool, step, 4)
            w.drain(pool, "xo_out", T)

        @block.vector
        def _(dve):
            p.start(dve)

            def step(i, b0):
                t, b, n = i, b0 % L, i + 1
                if live(t):
                    p.load_keys(dve, t, b, n)
                t, b, n = i - 3, (b0 - 3) % L, i - 2
                if live(t):
                    w.done(dve, "y", n)
                    w.landed(dve, "x_in", b, n)
                    w.drained(dve, "xo_out", b, n)
                    w.drained(dve, "slot_x", b, n)
                    dve.tensor_tensor(XO[b][:, :], y[b % 2][:, 0:C], XD[b][:, :], ALU.add).then_inc(w["xo"], 1)
                t, b, n = i - 2, (b0 - 2) % L, i - 1
                if live(t):
                    w.done(dve, "totsb", n)
                    w.landed(dve, "d_in", b, n)
                    w.freed(dve, "as", n)
                    dve.tensor_tensor(A[b][:, :], p.totsb[b][:, :], GD[b][:, :], ALU.add).then_inc(w["a"], 1)
                    w.done(dve, "a", n)
                    w.done(dve, "dv", n)
                    w.freed(dve, "aT", n)
                    dve.tensor_scalar(AS[b][:, :], A[b][:, :], dv[b][:, :], None, ALU.mult).then_inc(w["as"], 1)
                t, b, n = i - 1, (b0 - 1) % L, i
                if live(t):
                    w.freed(dve, "as", n)
                    dve.tensor_copy(dv[b][:, :], k.dinv[:, bass.ds(t, 1)]).then_inc(w["dv"], 1)
                    p.masks(dve, krow, b, n)

            each_step(dve, step, 3)

        @block.tensor
        def _(pe):
            pe.wait_ge(p.zeroed, 1)

            def step(i, b0):
                t, b, n = i, b0 % L, i + 1
                if live(t):
                    p.spread_keys(pe, krow, b, n)
                t, b, n = i - 3, (b0 - 3) % L, i - 2
                if live(t):
                    w.done(pe, "at", n)
                    w.freed(pe, "xo", n, 2)
                    pe.matmul(y[b % 2][:, 0:C], k.ones3[:, :], k.rows3[:, 1, :], start=True, stop=False, skip_group_check=True)
                    pe.matmul(y[b % 2][:, 0:C], AT[b][:, :], k.w2[:, :], start=False, stop=True, skip_group_check=True)\
                        .then_inc(w["y"], 1)
                t, b, n = i - 2, (b0 - 2) % L, i - 1
                if live(t):
                    w.done(pe, "as", n)
                    w.freed(pe, "at", n, 2)
                    pe.transpose(aT[b % 2][:, 0:P], AS[b][:, :], k.ident[:, :]).then_inc(w["aT"], 1)
                t, b, n = i - 1, (b0 - 1) % L, i
                if live(t):
                    w.landed(pe, "g_in", b, n)
                    p.sums(pe, tot, [GS[b][:, :]], b, n)

            each_step(pe, step, 3)

        @block.scalar
        def _(act):
            def step(i, b0):
                t, b, n = i - 2, (b0 - 2) % L, i - 1
                if live(t):
                    w.done(act, "aT", n)
                    w.freed(act, "y", n)
                    act.copy(AT[b][:, :], aT[b % 2][:, 0:P]).then_inc(w["at"], 1)
                t, b, n = i - 1, (b0 - 1) % L, i
                if live(t):
                    w.freed(act, "a", n)
                    p.keep_sums(act, tot, b, n)

            each_step(act, step, 2)


def edges_third(nc, k):
    with Phase(nc) as ctx:
        sb = lambda name, shape: [ctx.enter_context(nc.sbuf_tensor(f"e3_{name}{b}", shape, F32)) for b in range(L)]
        p = EdgePass(nc, ctx, "e3", k, 0, Norm.STEPS + "rw nm h hT ht rel pm ps y o osq st", "x_in", "g_in o_out")
        w = p.w
        ln = Norm(nc, ctx, "e3", w, 2, p.turn["dve"], "h")
        XX, H = sb("XX", [P, 2, C]), sb("H", [P, 2, C])
        HT = sb("HT", [C, 2, P])
        PM = [ctx.enter_context(nc.sbuf_tensor(f"e3_PM{b}", [P, R, C], F32)) for b in range(2)]
        PS = sb("PS", [P, R // 2, C])
        O, OSQ = sb("O", [P, C]), sb("OSQ", [P, C])
        rw, lst, nm = sb("rw", [P, R]), sb("lst", [P, 1]), sb("nm", [P, 2])
        bank = lambda name: ctx.enter_context(nc.psum_tensor(f"e3_{name}", [P, 512], F32))
        krow, tot = ([bank(f"{n}{b}") for b in range(2)] for n in ("krow", "tot"))
        hT, stat = bank("hT"), bank("stat")
        rel = [bank(f"rel{h}") for h in range(2)]
        stats_taken = ctx.semaphore("e3_stats_taken")
        block = ctx.enter_context(nc.Block())

        @block.sync
        def _(sp):
            w.credit(sp)

            def step(i, b0):
                t, b, n = i, b0 % L, i + 1
                w.freed(sp, "h", n)
                sp.dma_start(XX[b][:, 1, :], tile_rows(k.slot_x2, t)).then_inc(w.moves["x_in"][b], 16)

            each_step(sp, step, 0)

        @block.gpsimd
        def _(pool):
            def step(i, b0):
                t, b, n = i, b0 % L, i + 1
                if live(t):
                    p.load_ids(pool, t, b, n, ("g_in",))
                    w.freed(pool, "h", n)
                    p.gather(pool, XX[b][:, 0, :], k.X1, 0, b, n, "g_in")
                t, b, n = i - 5, (b0 - 5) % L, i - 4
                if live(t):
                    w.done(pool, "o", n)
                    p.scatter(pool, k.O, O[b][:, :], t, b, n, "o_out")

            each_step(pool, step, 5)
            w.drain(pool, "o_out", T)

        @block.vector
        def _(dve):
            p.start(dve)

            def step(i, b0):
                t, b, n = i - 4, (b0 - 4) % L, i - 3
                if live(t):
                    w.done(dve, "totsb", n)
                    w.done(dve, "y", n)
                    w.drained(dve, "o_out", b, n)
                    w.freed(dve, "st", n)
                    dve.tensor_tensor(O[b][:, :], krow[b % 2][:, 128:128 + C], p.totsb[b][:, :], ALU.add)\
                        .then_inc(w["o"], 1)
                t, b, n = i - 1, (b0 - 1) % L, i
                if live(t):
                    w.landed(dve, "g_in", b, n)
                    w.landed(dve, "x_in", b, n)
                    w.freed(dve, "nm", n)
                    ln.stats(dve, XX[b], b, n)
                    ln.inverse(dve, b, n)
                t, b, n = i - 2, (b0 - 2) % L, i - 1
                if live(t):
                    p.load_keys(dve, t, b, n)
                    w.done(dve, "ln_rs", n)
                    w.freed(dve, "h", n)
                    dve.scalar_tensor_tensor(nm[b][:, :], ln.mv[b][:, :, 0], -1.0, ln.rs[b][:, :], ALU.mult, ALU.mult)\
                        .then_inc(w["nm"], 1)
                t, b, n = i - 3, (b0 - 3) % L, i - 2
                if live(t):
                    w.freed(dve, "pm", n)
                    w.freed(dve, "st", n)
                    dve.tensor_copy(lst[b][:, :], k.is_last[:, bass.ds(t, 1)])
                    dve.tensor_copy(rw[b][:, :], k.rel_weight[:, bass.ds(t, 1), :].rearrange("p a r -> p (a r)"))\
                        .then_inc(w["rw"], 1)
                    p.masks(dve, krow, b, n)
                    w.done(dve, "rw", n)
                    w.done(dve, "rel", n)
                    w.freed(dve, "ps", n, 2)
                    for h in range(2):
                        last = dve.tensor_tensor(
                            PM[b % 2][:, h * 4:h * 4 + 4, :], rel[h][:, :].rearrange("p (r c) -> p r c", c=C),
                            rw[b][:, h * 4:h * 4 + 4].rearrange("p (r c) -> p r c", c=1).to_broadcast([P, 4, C]), ALU.mult)
                    last.then_inc(w["pm"], 1)
                    w.done(dve, "pm", n)
                    w.freed(dve, "tot", n)
                    dve.tensor_tensor(PS[b][:, :, :], PM[b % 2][:, 0:4, :], PM[b % 2][:, 4:8, :], ALU.add)\
                        .then_inc(w["ps"], 1)

            each_step(dve, step, 4)
            dve.wait_ge(w["st"], T + L)
            dve.tensor_copy(k.stats_edges[:, :], stat[:, 0:2]).then_inc(stats_taken, 1)
            dve.wait_ge(stats_taken, 1)

        @block.tensor
        def _(pe):
            pe.wait_ge(p.zeroed, 1)
            pe.matmul(stat[:, 0:2], k.zero_row[:, :], k.zero_row[:, 0:2], start=True, stop=True, skip_group_check=True)

            def step(i, b0):
                t, b, n = i - 2, (b0 - 2) % L, i - 1
                if live(t):
                    w.freed(pe, "o", n, 2)
                    p.spread_keys(pe, krow, b, n)
                    w.done(pe, "h", n)
                    w.freed(pe, "ht", n, 1)
                    for s in range(2):
                        last = pe.transpose(hT[:, s * P:(s + 1) * P], H[b][:, s, :], k.ident[:, :])
                    last.then_inc(w["hT"], 1)
                t, b, n = i - 5, (b0 - 5) % L, i - 4
                if live(t):
                    w.done(pe, "osq", n)
                    for c, src in enumerate((O, OSQ)):
                        last = pe.matmul(stat[:, c:c + 1], src[b][:, :], lst[b][:, :], start=False, stop=True,
                                         skip_group_check=True)
                    last.then_inc(w["st"], 1)
                t, b, n = i - 3, (b0 - 3) % L, i - 2
                if live(t):
                    w.done(pe, "ht", n)
                    w.freed(pe, "pm", n, 1)
                    for h in range(2):
                        last = pe.matmul(rel[h][:, :], HT[b][:, 0, :],
                                         k.w_rel[:, h * 4:h * 4 + 4, :].rearrange("c r d -> c (r d)"), start=True, stop=True)
                    last.then_inc(w["rel"], 1)
                    w.done(pe, "masks", n)
                    pe.matmul(krow[b % 2][:, 128:128 + C], k.ones3[:, :], k.rows3[:, 2, :], start=True, stop=False,
                              skip_group_check=True)
                    pe.matmul(krow[b % 2][:, 128:128 + C], HT[b][:, 1, :], k.root[:, :], start=False, stop=True,
                              skip_group_check=True).then_inc(w["y"], 1)
                    w.done(pe, "ps", n)
                    p.sums(pe, tot, [PS[b][:, r, :] for r in range(R // 2)], b, n)

            each_step(pe, step, 5)

        @block.scalar
        def _(act):
            def step(i, b0):
                t, b, n = i - 1, (b0 - 1) % L, i
                if live(t):
                    ln.root(act, b, n)
                t, b, n = i - 2, (b0 - 2) % L, i - 1
                if live(t):
                    w.done(act, "nm", n)
                    w.freed(act, "hT", n)
                    act.activation(H[b][:, 0, :], XX[b][:, 0, :], ACT.Relu, bias=nm[b][:, 0:1], scale=ln.rs[b][:, 0:1])
                    act.activation(H[b][:, 1, :], XX[b][:, 1, :], ACT.Relu, bias=nm[b][:, 1:2], scale=ln.rs[b][:, 1:2])\
                        .then_inc(w["h"], 1)
                    w.done(act, "hT", n)
                    w.freed(act, "y", n)
                    act.copy(HT[b][:, :, :].rearrange("c s p -> c (s p)"), hT[:, 0:2 * P]).then_inc(w["ht"], 1)
                t, b, n = i - 3, (b0 - 3) % L, i - 2
                if live(t):
                    w.freed(act, "o", n)
                    p.keep_sums(act, tot, b, n)
                t, b, n = i - 4, (b0 - 4) % L, i - 3
                if live(t):
                    w.done(act, "o", n)
                    w.freed(act, "st", n)
                    act.activation(OSQ[b][:, :], O[b][:, :], ACT.Square).then_inc(w["osq"], 1)

            each_step(act, step, 4)


def row_tables(nc, k):
    with Phase(nc) as ctx:
        sb = lambda name, shape: ctx.enter_context(nc.sbuf_tensor("rt_" + name, shape, F32))
        cols = sb("cols", [C, 6])
        gamma_beta = sb("gamma_beta", [C, 2])
        bm2 = sb("bm2", [C, 1])
        total, mean, tmp, var, std, shift = (sb(n, [C, w]) for n, w in
                                             (("total", 2), ("mean", 2), ("tmp", 1), ("var", 1), ("std", 1), ("shift", 1)))
        wm2, wm2_t, wu1b = (sb(n, [C, C]) for n in ("wm2", "wm2_t", "wu1b"))
        spread = [ctx.enter_context(nc.psum_tensor(f"rt_spread{i}", [P, 512], F32)) for i in range(2)]
        wt_ps, wc_ps = (ctx.enter_context(nc.psum_tensor(f"rt_{n}", [P, 512], F32)) for n in ("wt", "wc"))
        chain, loaded, var_ready, std_ready = (ctx.semaphore("rt_" + n) for n in ("chain", "loaded", "var_ready", "std_ready"))
        turned, turned_in, product, cols_ready, spread_ready = (
            ctx.semaphore("rt_" + n) for n in ("turned", "turned_in", "product", "cols_ready", "spread_ready"))
        block = ctx.enter_context(nc.Block())
        col = lambda vector: vector.rearrange("(c a) -> c a", a=1)
        loads = [(gamma_beta[:, 0:1], col(k.L1_gamma)), (gamma_beta[:, 1:2], col(k.L1_beta)),
                 (cols[:, 2:3], col(k.L2_gamma)), (cols[:, 3:4], col(k.L2_beta)),
                 (cols[:, 4:5], col(k.L3_W2)), (cols[:, 5:6], col(k.L3_W3)), (bm2[:, :], col(k.L2_bm2)),
                 (k.bm1_col[:, :], col(k.L2_bm1)), (k.bu1_col[:, :], col(k.L2_bu1)), (wm2[:, :], k.L2_wm2),
                 (wu1b[:, :], k.L2_wu1[C:2 * C, :]), (k.wu1a[:, :], k.L2_wu1[0:C, :]), (k.wu2[:, :], k.L2_wu2),
                 (k.wm1a[:, :], k.L2_wm1[0:C, :]), (k.wm1b[:, :], k.L2_wm1[C:2 * C, :])]

        @block.sync
        def _(sp):
            for tile, source in loads:
                sp.dma_start(tile, source).then_inc(loaded, 16)
            sp.wait_ge(loaded, 16 * len(loads))

        @block.vector
        def _(dve):
            links = [0]

            def link(ins):
                links[0] += 1
                ins.then_inc(chain, 1)
                dve.wait_ge(chain, links[0])

            link(dve.tensor_tensor(total[:, :], k.stats_whole[:, :], k.stats_edges[:, :], ALU.add))
            link(dve.tensor_scalar(mean[:, :], total[:, :], 1.0 / N, None, ALU.mult))
            link(dve.tensor_tensor(tmp[:, :], mean[:, 0:1], mean[:, 0:1], ALU.mult))
            link(dve.tensor_tensor(var[:, :], mean[:, 1:2], tmp[:, :], ALU.subtract))
            link(dve.tensor_scalar(var[:, :], var[:, :], 0.0, EPS, ALU.max, ALU.add))
            dve.reciprocal(tmp[:, :], var[:, :]).then_inc(var_ready, 1)
            dve.wait_ge(std_ready, 1)
            dve.wait_ge(loaded, 16 * len(loads))
            link(dve.tensor_tensor(cols[:, 0:1], gamma_beta[:, 0:1], std[:, :], ALU.mult))
            link(dve.tensor_tensor(shift[:, :], mean[:, 0:1], cols[:, 0:1], ALU.mult))
            dve.tensor_tensor(cols[:, 1:2], gamma_beta[:, 1:2], shift[:, :], ALU.subtract).then_inc(cols_ready, 1)
            dve.wait_ge(turned, 1)
            dve.tensor_copy(wm2_t[:, :], wt_ps[:, 0:C]).then_inc(turned_in, 1)
            dve.wait_ge(product, 1)
            dve.tensor_copy(k.wc[:, :], wc_ps[:, 0:C])
            link(dve.tensor_copy(k.cb[:, :], wc_ps[:, C:2 * C]))
            dve.wait_ge(spread_ready, 1)
            for i in range(2):
                link(dve.tensor_copy(k.spread[:, i * 3:i * 3 + 3, :].rearrange("p a c -> p (a c)"), spread[i][:, 0:3 * C]))

        @block.scalar
        def _(act):
            act.wait_ge(var_ready, 1)
            act.activation(std[:, :], tmp[:, :], ACT.Sqrt).then_inc(std_ready, 1)

        @block.tensor
        def _(pe):
            pe.wait_ge(loaded, 16 * len(loads))
            pe.transpose(wt_ps[:, 0:C], wm2[:, :], k.ident[:, :]).then_inc(turned, 1)
            pe.wait_ge(turned_in, 1)
            pe.matmul(wc_ps[:, 0:C], wm2_t[:, :], wu1b[:, :], start=True, stop=True)
            pe.matmul(wc_ps[:, C:2 * C], bm2[:, :].to_broadcast([C, P]), wu1b[:, :], start=True, stop=True)\
                .then_inc(product, 1)
            pe.wait_ge(cols_ready, 1)
            for i in range(6):
                last = pe.matmul(spread[i // 3][:, i % 3 * C:(i % 3 + 1) * C], cols[:, i:i + 1].to_broadcast([C, P]),
                                 k.ident[:, :], start=True, stop=True)
            last.then_inc(spread_ready, 1)


class PowerNorm:

    def __init__(self, nc, ctx, prefix, k, w, S, go, used, name):
        sb = lambda n, shape: [ctx.enter_context(nc.sbuf_tensor(f"{prefix}_{name}_{n}{b}", shape, F32)) for b in range(w.L)]
        self.k, self.w, self.S, self.go, self.used, self.name = k, w, S, go, used, name
        self.six, self.mv = sb("six", [P, S, 6]), sb("mv", [P, S, 2])
        self.ve, self.rs = sb("ve", [P, S]), sb("rs", [P, S])

    @staticmethod
    def steps(name):
        return f" {name}_six {name}_mv {name}_ve {name}_rs "

    def stats(self, dve, X, b, n, rows=P):
        w, a = self.w, self.name
        w.freed(dve, a + "_mv", n)
        for s in range(self.S):
            last = dve.bn_stats(self.six[b][0:rows, s, :], X[0:rows, s, :])
        last.then_inc(w[a + "_six"], 1)
        w.done(dve, a + "_six", n)
        w.freed(dve, self.used, n)
        dve.sem_inc(self.go["dve"], 1)
        for s in range(self.S):
            last = dve.bn_aggr(self.mv[b][0:rows, s, :], self.six[b][0:rows, s, :])
        last.then_inc(w[a + "_mv"], 1)

    def power(self, pool, b, n, rows=P):
        w, a = self.w, self.name
        w.done(pool, a + "_mv", n)
        w.freed(pool, a + "_rs", n)
        pool.sem_inc(self.go["pool"], 1)
        pool.tensor_scalar(self.ve[b][0:rows, :], self.mv[b][0:rows, :, 1], EPS, None, ALU.add).then_inc(w[a + "_ve"], 1)
        w.done(pool, a + "_ve", n)
        w.freed(pool, self.used, n)
        pool.tensor_tensor(self.rs[b][0:rows, :], self.ve[b][0:rows, :], self.k.minus_half[0:rows, 0:self.S], ALU.pow)\
            .then_inc(w[a + "_rs"], 1)

    def apply(self, dve, Y, X, b, n, step, rows=P):
        self.w.done(dve, self.name + "_rs", n)
        for s in range(self.S):
            last = dve.tensor_scalar(Y[0:rows, s, :], X[0:rows, s, :], self.mv[b][0:rows, s, 0:1],
                                     self.rs[b][0:rows, s:s + 1], ALU.subtract, ALU.mult)
        last.then_inc(self.w[step], 1)


def nodes_second(nc, k):
    with Phase(nc) as ctx:
        L = LONG
        ring = lambda name, count, shape=[P, J, C]: [ctx.enter_context(nc.sbuf_tensor(f"n2_{name}{b}", shape, F32))
                                                     for b in range(count)]
        X1, O, Z, Q, H, Y, YN = (ring(n, 4) for n in ("X1", "O", "Z", "Q", "H", "Y", "YN"))
        S = ring("S", 2)
        X2 = ring("X2", L)
        HT, SU, UT = (ring(n, 2, [C, J, P]) for n in ("HT", "SU", "UT"))
        hT, u, y = ([ctx.enter_context(nc.psum_tensor(f"n2_{n}{b}", [P, 512], F32)) for b in range(2)]
                    for n in ("hT", "u", "y"))
        w = Turns(nc, ctx, "n2", L, "z0 z d s sq q1 iq rz x2" + PowerNorm.steps("a") + "xn h hT ht u su ut y yy"
                  + PowerNorm.steps("b") + "yn yg yb x3", "x1_in o_in x2_out out")
        turn = {e: ctx.semaphore(f"n2_turn_{e}") for e in ("pool", "dve")}
        lnA = PowerNorm(nc, ctx, "n2", k, w, J, turn, "xn", "a")
        lnB = PowerNorm(nc, ctx, "n2", k, w, J, turn, "yn", "b")
        block = ctx.enter_context(nc.Block())
        height = lambda g: TAIL if isinstance(g, int) and g == FULL else P
        each = lambda eng, step, lag: each_step(eng, step, lag, NG, L)
        vec = lambda i, rows: k.spread[0:rows, i:i + 1, :].to_broadcast([rows, J, C])

        def stage(lag, i, b0):
            g = i - lag
            return (g, (b0 - lag) % L, g + 1, height(g)) if live(g, NG) else None

        @block.sync
        def _(sp):
            w.credit(sp)

            def step(i, b0):
                at = stage(0, i, b0)
                if at:
                    g, b, n, rows = at
                    w.freed(sp, "x2", n, 4)
                    sp.dma_start(X1[b % 4][0:rows], node_rows(k.X1, g, rows)).then_inc(w.moves["x1_in"][b], 16)
                    w.freed(sp, "z0", n, 4)
                    sp.dma_start(O[b % 4][0:rows], node_rows(k.O, g, rows)).then_inc(w.moves["o_in"][b], 16)
                at = stage(3, i, b0)
                if at:
                    g, b, n, rows = at
                    w.done(sp, "x2", n)
                    sp.dma_start(node_rows(k.X2, g, rows), X2[b][0:rows]).then_inc(w.moves["x2_out"][b], 16)
                at = stage(9, i, b0)
                if at:
                    g, b, n, rows = at
                    w.done(sp, "x3", n)
                    sp.dma_start(node_rows(k.out, g, rows), X2[b][0:rows]).then_inc(w.moves["out"][b], 16)

            each(sp, step, 9)
            w.drain(sp, "x2_out", NG)
            w.drain(sp, "out", NG)

        @block.gpsimd
        def _(pool):
            def step(i, b0):
                at = stage(8, i, b0)
                if at:
                    g, b, n, rows = at
                    y_ = YN[b % 4][0:rows]
                    w.done(pool, "yn", n)
                    pool.tensor_tensor(y_, y_, vec(2, rows), ALU.mult).then_inc(w["yg"], 1)
                    w.done(pool, "yg", n)
                    pool.tensor_tensor(y_, y_, vec(3, rows), ALU.add).then_inc(w["yb"], 1)
                    w.done(pool, "yb", n)
                    w.landed(pool, "x2_out", b, n)
                    pool.tensor_tensor(X2[b][0:rows], y_, X2[b][0:rows], ALU.add).then_inc(w["x3"], 1)
                at = stage(7, i, b0)
                if at:
                    g, b, n, rows = at
                    lnB.power(pool, b, n, rows)
                at = stage(4, i, b0)
                if at:
                    g, b, n, rows = at
                    w.done(pool, "xn", n)
                    pool.sem_inc(turn["pool"], 1)
                    pool.tensor_scalar(H[b % 4][0:rows], H[b % 4][0:rows], 0.0, None, ALU.max).then_inc(w["h"], 1)
                at = stage(3, i, b0)
                if at:
                    g, b, n, rows = at
                    lnA.power(pool, b, n, rows)
                at = stage(2, i, b0)
                if at:
                    g, b, n, rows = at
                    w.done(pool, "rz", n)
                    w.done(pool, "d", n)
                    w.drained(pool, "out", b, n)
                    pool.tensor_tensor(X2[b][0:rows], X1[b % 4][0:rows], Q[b % 4][0:rows], ALU.add).then_inc(w["x2"], 1)
                at = stage(1, i, b0)
                if at:
                    g, b, n, rows = at
                    z = Z[b % 4][0:rows]
                    w.landed(pool, "o_in", b, n)
                    w.freed(pool, "x2", n, 4)
                    pool.tensor_tensor(z, O[b % 4][0:rows], vec(0, rows), ALU.mult).then_inc(w["z0"], 1)
                    w.done(pool, "z0", n)
                    pool.tensor_tensor(z, z, vec(1, rows), ALU.add).then_inc(w["z"], 1)
                    w.done(pool, "z", n)
                    w.landed(pool, "x1_in", b, n)
                    pool.tensor_tensor(X1[b % 4][0:rows], X1[b % 4][0:rows], z, ALU.subtract).then_inc(w["d"], 1)

            each(pool, step, 8)

        @block.vector
        def _(dve):
            def step(i, b0):
                at = stage(8, i, b0)
                if at:
                    g, b, n, rows = at
                    w.freed(dve, "x3", n, 4)
                    lnB.apply(dve, YN[b % 4], Y[b % 4], b, n, "yn", rows)
                at = stage(7, i, b0)
                if at:
                    g, b, n, rows = at
                    w.done(dve, "yy", n)
                    lnB.stats(dve, Y[b % 4], b, n, rows)
                at = stage(6, i, b0)
                if at:
                    g, b, n, rows = at
                    w.done(dve, "y", n)
                    w.freed(dve, "yn", n, 4)
                    dve.tensor_tensor(Y[b % 4][0:rows].rearrange("p j c -> p (j c)"), y[b % 2][0:rows, :],
                                      H[b % 4][0:rows].rearrange("p j c -> p (j c)"), ALU.add).then_inc(w["yy"], 1)
                at = stage(5, i, b0)
                if at:
                    g, b, n, rows = at
                    w.done(dve, "su", n)
                    w.freed(dve, "y", n, 2)
                    dve.scalar_tensor_tensor(UT[b % 2][:, :, 0:rows], row_blocks(u[b % 2])[:, :, 0:rows],
                                             k.bu1_col[:, :], SU[b % 2][:, :, 0:rows], ALU.add, ALU.mult)\
                        .then_inc(w["ut"], 1)
                at = stage(4, i, b0)
                if at:
                    g, b, n, rows = at
                    w.freed(dve, "yy", n, 4)
                    lnA.apply(dve, H[b % 4], X2[b], b, n, "xn", rows)
                at = stage(3, i, b0)
                if at:
                    g, b, n, rows = at
                    w.done(dve, "x2", n)
                    lnA.stats(dve, X2[b], b, n, rows)
                at = stage(2, i, b0)
                if at:
                    g, b, n, rows = at
                    q = Q[b % 4][0:rows]
                    w.done(dve, "q1", n)
                    dve.reciprocal(q, q).then_inc(w["iq"], 1)
                    w.done(dve, "iq", n)
                    w.done(dve, "z", n)
                    dve.scalar_tensor_tensor(q, q, 2.0, Z[b % 4][0:rows], ALU.mult, ALU.mult).then_inc(w["rz"], 1)

            each(dve, step, 8)

        @block.scalar
        def _(act):
            def step(i, b0):
                at = stage(5, i, b0)
                if at:
                    g, b, n, rows = at
                    w.done(act, "u", n)
                    w.freed(act, "ut", n, 2)
                    act.activation(SU[b % 2][:, :, 0:rows], row_blocks(u[b % 2])[:, :, 0:rows], ACT.Sigmoid,
                                   bias=k.bu1_col[:, :]).then_inc(w["su"], 1)
                at = stage(4, i, b0)
                if at:
                    g, b, n, rows = at
                    w.done(act, "hT", n)
                    w.freed(act, "u", n, 2)
                    act.copy(HT[b % 2][:, :, 0:rows], row_blocks(hT[b % 2])[:, :, 0:rows]).then_inc(w["ht"], 1)
                at = stage(1, i, b0)
                if at:
                    g, b, n, rows = at
                    s, q = S[b % 2][0:rows], Q[b % 4][0:rows]
                    w.done(act, "z", n)
                    w.freed(act, "sq", n, 2)
                    act.activation(s, Z[b % 4][0:rows], ACT.Sigmoid, scale=-1.0).then_inc(w["s"], 1)
                    w.done(act, "s", n)
                    w.freed(act, "x2", n, 4)
                    act.activation(q, s, ACT.Square).then_inc(w["sq"], 1)
                    w.done(act, "sq", n)
                    act.activation(q, q, ACT.Relu, bias=k.ones[0:rows, 0:1]).then_inc(w["q1"], 1)

            each(act, step, 5)

        @block.tensor
        def _(pe):
            def step(i, b0):
                at = stage(6, i, b0)
                if at:
                    g, b, n, rows = at
                    w.done(pe, "ut", n)
                    w.freed(pe, "yy", n, 2)
                    pe.matmul(y[b % 2][0:rows, :].rearrange("p (j c) -> p j c", j=J), k.ones3[:, 0:rows],
                              k.rows3[:, 6:7, :].to_broadcast([3, J, C]), start=True, stop=False, skip_group_check=True)
                    for j in range(J):
                        last = pe.matmul(y[b % 2][0:rows, j * C:(j + 1) * C], UT[b % 2][:, j, 0:rows], k.wu2[:, :],
                                         start=False, stop=True, skip_group_check=True)
                    last.then_inc(w["y"], 1)
                at = stage(5, i, b0)
                if at:
                    g, b, n, rows = at
                    w.done(pe, "ht", n)
                    w.freed(pe, "ut", n, 2)
                    pe.matmul(row_blocks(u[b % 2])[:, :, 0:rows], k.wu1a[:, :], HT[b % 2][:, :, 0:rows],
                              start=True, stop=True).then_inc(w["u"], 1)
                at = stage(4, i, b0)
                if at:
                    g, b, n, rows = at
                    w.done(pe, "h", n)
                    w.freed(pe, "ht", n, 2)
                    for j in range(J):
                        last = pe.transpose(hT[b % 2][:, j * P:j * P + rows], H[b % 4][0:rows, j, :],
                                            k.ident[0:rows, 0:rows])
                    last.then_inc(w["hT"], 1)

            each(pe, step, 6)


def edges_fourth(nc, k):
    with Phase(nc) as ctx:
        L = LONG
        sb = lambda name, shape, count=L: [ctx.enter_context(nc.sbuf_tensor(f"e4_{name}{b}", shape, F32))
                                           for b in range(count)]
        p = EdgePass(nc, ctx, "e4", k, 1, PowerNorm.steps("a") + "nm h hT ht m sm mt q qq u su ut y yy"
                     + PowerNorm.steps("b") + "yn yg yb x3", "", "s_in d_in x_out", L)
        w = p.w
        lnA = PowerNorm(nc, ctx, "e4", k, w, 2, p.turn, "h", "a")
        lnB = PowerNorm(nc, ctx, "e4", k, w, 1, p.turn, "yn", "b")
        XX, H = sb("XX", [P, 2, C]), sb("H", [P, 2, C])
        HT = sb("HT", [C, 2, P])
        nm = sb("nm", [P, 2])
        SM, MT, QQ, SU, UT = (sb(n, [P, C]) for n in ("SM", "MT", "QQ", "SU", "UT"))
        Y, YN = sb("Y", [P, 1, C]), sb("YN", [P, 1, C])
        bank = lambda name: ctx.enter_context(nc.psum_tensor(f"e4_{name}", [P, 512], F32))
        krow, hT, m, q, tot, u, y = (bank(n) for n in ("krow", "hT", "m", "q", "tot", "u", "y"))
        block = ctx.enter_context(nc.Block())
        each = lambda eng, step, lag: each_step(eng, step, lag, T, L)

        def stage(lag, i, b0):
            return (i - lag, (b0 - lag) % L, i - lag + 1) if live(i - lag) else None

        @block.sync
        def _(sp):
            w.credit(sp)

        @block.gpsimd
        def _(pool):
            def step(i, b0):
                at = stage(9, i, b0)
                if at:
                    t, b, n = at
                    w.done(pool, "x3", n)
                    p.scatter(pool, k.out, YN[b][:, 0, :], t, b, n, "x_out")
                at = stage(8, i, b0)
                if at:
                    t, b, n = at
                    lnB.power(pool, b, n)
                at = stage(2, i, b0)
                if at:
                    t, b, n = at
                    lnA.power(pool, b, n)
                at = stage(0, i, b0)
                if at:
                    t, b, n = at
                    p.load_ids(pool, t, b, n, ("s_in", "d_in"))
                    w.freed(pool, "x3", n, 8)
                    p.gather(pool, XX[b][:, 0, :], k.X2, 0, b, n, "s_in")
                    w.freed(pool, "h", n)
                    p.gather(pool, XX[b][:, 1, :], k.X2, 1, b, n, "d_in")

            each(pool, step, 9)
            w.drain(pool, "x_out", T)

        @block.vector
        def _(dve):
            p.start(dve)

            def step(i, b0):
                at = stage(9, i, b0)
                if at:
                    t, b, n = at
                    w.drained(dve, "x_out", b, n)
                    lnB.apply(dve, YN[b], Y[b], b, n, "yn")
                    w.done(dve, "yn", n)
                    dve.tensor_tensor(YN[b][:, 0, :], YN[b][:, 0, :], k.spread[:, 2, :], ALU.mult).then_inc(w["yg"], 1)
                    w.done(dve, "yg", n)
                    dve.tensor_tensor(YN[b][:, 0, :], YN[b][:, 0, :], k.spread[:, 3, :], ALU.add).then_inc(w["yb"], 1)
                    w.done(dve, "yb", n)
                    dve.tensor_tensor(YN[b][:, 0, :], YN[b][:, 0, :], XX[b][:, 0, :], ALU.add).then_inc(w["x3"], 1)
                at = stage(8, i, b0)
                if at:
                    t, b, n = at
                    w.done(dve, "y", n)
                    w.freed(dve, "yn", n)
                    dve.tensor_tensor(Y[b][:, 0, :], y[:, 0:C], H[b][:, 0, :], ALU.add).then_inc(w["yy"], 1)
                    w.done(dve, "yy", n)
                    lnB.stats(dve, Y[b], b, n)
                at = stage(7, i, b0)
                if at:
                    t, b, n = at
                    w.done(dve, "su", n)
                    w.freed(dve, "y", n)
                    dve.scalar_tensor_tensor(UT[b][:, :], u[:, 0:P], k.bu1_col[:, :], SU[b][:, :], ALU.add, ALU.mult)\
                        .then_inc(w["ut"], 1)
                at = stage(5, i, b0)
                if at:
                    t, b, n = at
                    w.done(dve, "q", n)
                    w.freed(dve, "tot", n)
                    dve.tensor_tensor(QQ[b][:, :], q[:, 0:C], k.cb[:, :], ALU.add).then_inc(w["qq"], 1)
                at = stage(4, i, b0)
                if at:
                    t, b, n = at
                    w.done(dve, "sm", n)
                    w.freed(dve, "q", n)
                    dve.scalar_tensor_tensor(MT[b][:, :], m[:, 0:P], k.bm1_col[:, :], SM[b][:, :], ALU.add, ALU.mult)\
                        .then_inc(w["mt"], 1)
                at = stage(3, i, b0)
                if at:
                    t, b, n = at
                    w.done(dve, "a_rs", n)
                    w.freed(dve, "h", n)
                    dve.scalar_tensor_tensor(nm[b][:, :], lnA.mv[b][:, :, 0], -1.0, lnA.rs[b][:, :], ALU.mult, ALU.mult)\
                        .then_inc(w["nm"], 1)
                    p.masks(dve, [krow, krow], b, n)
                at = stage(2, i, b0)
                if at:
                    t, b, n = at
                    w.landed(dve, "s_in", b, n)
                    w.landed(dve, "d_in", b, n)
                    w.freed(dve, "nm", n)
                    lnA.stats(dve, XX[b], b, n)
                    p.load_keys(dve, t, b, n)

            each(dve, step, 9)

        @block.scalar
        def _(act):
            def step(i, b0):
                at = stage(7, i, b0)
                if at:
                    t, b, n = at
                    w.done(act, "u", n)
                    w.freed(act, "ut", n)
                    act.activation(SU[b][:, :], u[:, 0:P], ACT.Sigmoid, bias=k.bu1_col[:, :]).then_inc(w["su"], 1)
                at = stage(6, i, b0)
                if at:
                    t, b, n = at
                    w.freed(act, "u", n)
                    p.keep_sums(act, [tot, tot], b, n)
                at = stage(4, i, b0)
                if at:
                    t, b, n = at
                    w.done(act, "m", n)
                    w.freed(act, "mt", n)
                    act.activation(SM[b][:, :], m[:, 0:P], ACT.Sigmoid, bias=k.bm1_col[:, :]).then_inc(w["sm"], 1)
                at = stage(3, i, b0)
                if at:
                    t, b, n = at
                    w.done(act, "nm", n)
                    w.freed(act, "yy", n)
                    for s in range(2):
                        last = act.activation(H[b][:, s, :], XX[b][:, s, :], ACT.Relu, bias=nm[b][:, s:s + 1],
                                              scale=lnA.rs[b][:, s:s + 1])
                    last.then_inc(w["h"], 1)
                    w.done(act, "hT", n)
                    w.freed(act, "u", n)
                    act.copy(HT[b][:, :, :].rearrange("c s p -> c (s p)"), hT[:, 0:2 * P]).then_inc(w["ht"], 1)

            each(act, step, 7)

        @block.tensor
        def _(pe):
            pe.wait_ge(p.zeroed, 1)

            def step(i, b0):
                at = stage(8, i, b0)
                if at:
                    t, b, n = at
                    w.done(pe, "ut", n)
                    w.freed(pe, "yy", n, 1)
                    pe.matmul(y[:, 0:C], k.ones3[:, :], k.rows3[:, 6, :], start=True, stop=False, skip_group_check=True)
                    pe.matmul(y[:, 0:C], UT[b][:, :], k.wu2[:, :], start=False, stop=True, skip_group_check=True)\
                        .then_inc(w["y"], 1)
                at = stage(7, i, b0)
                if at:
                    t, b, n = at
                    w.done(pe, "totsb", n)
                    w.freed(pe, "ut", n, 1)
                    pe.matmul(u[:, 0:P], k.wu1a[:, :], HT[b][:, 0, :], start=True, stop=False)
                    pe.matmul(u[:, 0:P], p.totsb[b][:, :], k.ident[:, :], start=False, stop=True).then_inc(w["u"], 1)
                at = stage(6, i, b0)
                if at:
                    t, b, n = at
                    w.done(pe, "qq", n)
                    p.sums(pe, [tot, tot], [QQ[b][:, :]], b, n)
                at = stage(5, i, b0)
                if at:
                    t, b, n = at
                    w.done(pe, "mt", n)
                    w.freed(pe, "qq", n, 1)
                    pe.matmul(q[:, 0:C], MT[b][:, :], k.wc[:, :], start=True, stop=True).then_inc(w["q"], 1)
                at = stage(4, i, b0)
                if at:
                    t, b, n = at
                    w.done(pe, "ht", n)
                    w.freed(pe, "mt", n, 1)
                    pe.matmul(m[:, 0:P], k.wm1a[:, :], HT[b][:, 0, :], start=True, stop=False)
                    pe.matmul(m[:, 0:P], k.wm1b[:, :], HT[b][:, 1, :], start=False, stop=True).then_inc(w["m"], 1)
                at = stage(3, i, b0)
                if at:
                    t, b, n = at
                    p.spread_keys(pe, [krow, krow], b, n, 1)
                    w.done(pe, "h", n)
                    w.freed(pe, "ht", n, 1)
                    for s in range(2):
                        last = pe.transpose(hT[:, s * P:(s + 1) * P], H[b][:, s, :], k.ident[:, :])
                    last.then_inc(w["hT"], 1)

            each(pe, step, 8)


def edges_fifth(nc, k):
    with Phase(nc) as ctx:
        L = LONG
        sb = lambda name, shape: [ctx.enter_context(nc.sbuf_tensor(f"e5_{name}{b}", shape, F32)) for b in range(L)]
        p = EdgePass(nc, ctx, "e5", k, 0, Norm.STEPS + "nm h hw attn msg st r", "r_out", "s_in d_in", L)
        w = p.w
        ln = Norm(nc, ctx, "e5", w, 2, p.turn["dve"], "h")
        XX, H = sb("XX", [P, 2, C]), sb("H", [P, 2, C])
        HW, HH, MSG, ST, RES = (sb(n, [P, C]) for n in ("HW", "HH", "MSG", "ST", "RES"))
        nm, attn = sb("nm", [P, 2]), sb("attn", [P, 1])
        krow, tot = ([ctx.enter_context(nc.psum_tensor(f"e5_{n}{b}", [P, 512], F32)) for b in range(2)]
                     for n in ("krow", "tot"))
        block = ctx.enter_context(nc.Block())
        each = lambda eng, step, lag: each_step(eng, step, lag, T, L)

        def stage(lag, i, b0):
            return (i - lag, (b0 - lag) % L, i - lag + 1) if live(i - lag) else None

        @block.sync
        def _(sp):
            w.credit(sp)

            def step(i, b0):
                at = stage(6, i, b0)
                if at:
                    t, b, n = at
                    w.done(sp, "r", n)
                    sp.dma_start(tile_rows(k.slot_g, t), RES[b][:, :]).then_inc(w.moves["r_out"][b], 16)

            each(sp, step, 6)
            w.drain(sp, "r_out", T)

        @block.gpsimd
        def _(pool):
            def step(i, b0):
                at = stage(0, i, b0)
                if at:
                    t, b, n = at
                    p.load_ids(pool, t, b, n, ("s_in", "d_in"))
                    w.freed(pool, "r", n)
                    p.gather(pool, XX[b][:, 0, :], k.out, 0, b, n, "s_in")
                    p.gather(pool, XX[b][:, 1, :], k.out, 1, b, n, "d_in")

            each(pool, step, 0)

        @block.vector
        def _(dve):
            p.start(dve)

            def step(i, b0):
                at = stage(6, i, b0)
                if at:
                    t, b, n = at
                    w.done(dve, "totsb", n)
                    w.freed(dve, "r", n)
                    dve.tensor_tensor(ST[b][:, :], p.totsb[b][:, :], k.spread[:, 4, :], ALU.mult).then_inc(w["st"], 1)
                    w.done(dve, "st", n)
                    w.drained(dve, "r_out", b, n)
                    dve.tensor_tensor(RES[b][:, :], ST[b][:, :], XX[b][:, 1, :], ALU.add).then_inc(w["r"], 1)
                at = stage(4, i, b0)
                if at:
                    t, b, n = at
                    w.done(dve, "h", n)
                    w.freed(dve, "attn", n)
                    dve.tensor_tensor(HW[b][:, :], H[b][:, 1, :], k.spread[:, 5, :], ALU.mult).then_inc(w["hw"], 1)
                    p.masks(dve, krow, b, n)
                    w.done(dve, "hw", n)
                    w.freed(dve, "msg", n)
                    dve.tensor_tensor_reduce(HH[b][:, :], HW[b][:, :], H[b][:, 0, :], 1.0, 0.0, ALU.mult, ALU.add,
                                             attn[b][:, :]).then_inc(w["attn"], 1)
                    w.done(dve, "attn", n)
                    w.freed(dve, "tot", n)
                    dve.tensor_scalar(MSG[b][:, :], H[b][:, 0, :], attn[b][:, :], None, ALU.mult).then_inc(w["msg"], 1)
                at = stage(3, i, b0)
                if at:
                    t, b, n = at
                    w.done(dve, "ln_rs", n)
                    w.freed(dve, "h", n)
                    dve.scalar_tensor_tensor(nm[b][:, :], ln.mv[b][:, :, 0], -1.0, ln.rs[b][:, :], ALU.mult, ALU.mult)\
                        .then_inc(w["nm"], 1)
                    p.load_keys(dve, t, b, n)
                at = stage(2, i, b0)
                if at:
                    t, b, n = at
                    w.landed(dve, "s_in", b, n)
                    w.landed(dve, "d_in", b, n)
                    w.freed(dve, "nm", n)
                    ln.stats(dve, XX[b], b, n)
                    ln.inverse(dve, b, n)

            each(dve, step, 6)

        @block.scalar
        def _(act):
            def step(i, b0):
                at = stage(5, i, b0)
                if at:
                    t, b, n = at
                    w.freed(act, "st", n)
                    p.keep_sums(act, tot, b, n)
                at = stage(3, i, b0)
                if at:
                    t, b, n = at
                    w.done(act, "nm", n)
                    w.freed(act, "msg", n)
                    for s in range(2):
                        last = act.activation(H[b][:, s, :], XX[b][:, s, :], ACT.Relu, bias=nm[b][:, s:s + 1],
                                              scale=ln.rs[b][:, s:s + 1])
                    last.then_inc(w["h"], 1)
                at = stage(2, i, b0)
                if at:
                    t, b, n = at
                    ln.root(act, b, n)

            each(act, step, 5)

        @block.tensor
        def _(pe):
            pe.wait_ge(p.zeroed, 1)

            def step(i, b0):
                at = stage(5, i, b0)
                if at:
                    t, b, n = at
                    w.done(pe, "msg", n)
                    p.sums(pe, tot, [MSG[b][:, :]], b, n)
                at = stage(3, i, b0)
                if at:
                    t, b, n = at
                    p.spread_keys(pe, krow, b, n)

            each(pe, step, 5)


def last_rows(nc, k):
    with Phase(nc) as ctx:
        L = LONG
        p = EdgePass(nc, ctx, "e6", k, 0, "", "r_in", "x_out", L)
        w = p.w
        RES = [ctx.enter_context(nc.sbuf_tensor(f"e6_RES{b}", [P, C], F32)) for b in range(L)]
        block = ctx.enter_context(nc.Block())

        @block.sync
        def _(sp):
            w.credit(sp)

            def step(i, b):
                if live(i):
                    w.drained(sp, "x_out", b % L, i + 1)
                    sp.dma_start(RES[b % L][:, :], tile_rows(k.slot_g, i)).then_inc(w.moves["r_in"][b % L], 16)

            each_step(sp, step, 0, T, L)

        @block.gpsimd
        def _(pool):
            def step(i, b):
                if live(i):
                    w.landed(pool, "r_in", b % L, i + 1)
                    p.scatter(pool, k.out, RES[b % L][:, :], i, b % L, i + 1, "x_out")

            each_step(pool, step, 0, T, L)
            w.drain(pool, "x_out", T)


class Kept:
    pass


def program(nc, x, src, dst, edge_type, weights, out):
    k = Kept()
    k.x, k.src, k.dst, k.edge_type, k.out = x, src, dst, edge_type, out
    k.L0_W1, k.L0_b1, k.L0_W2, k.L0_b2 = (weights["L0_" + n] for n in ("W1", "b1", "W2", "b2"))
    k.L1_W, k.L1_root, k.L1_bias, k.L1_gamma, k.L1_beta = (
        weights["L1_" + n] for n in ("W", "root", "bias", "gamma", "beta"))
    k.L2_wm1, k.L2_bm1, k.L2_wm2, k.L2_bm2 = (weights["L2_" + n] for n in ("wm1", "bm1", "wm2", "bm2"))
    k.L2_wu1, k.L2_bu1, k.L2_wu2, k.L2_bu2 = (weights["L2_" + n] for n in ("wu1", "bu1", "wu2", "bu2"))
    k.L2_gamma, k.L2_beta, k.L3_W2, k.L3_W3 = (weights[n] for n in ("L2_gamma", "L2_beta", "L3_W2", "L3_W3"))
    with ExitStack() as ctx:
        sb = lambda name, shape, dt=F32: ctx.enter_context(nc.sbuf_tensor(name, shape, dt))
        k.edge_i = sb("edge_i", [P, 3, T], I32)
        k.iota = sb("iota", [P, HI])
        k.iota_b = sb("iota_b", [P, HI], BF16)
        k.ident_b = sb("ident_b", [P, P], BF16)
        k.part = sb("part", [P, 1])
        k.ident, k.before, k.shift, k.unshift, k.wrap = (sb(n, [P, P]) for n in ("ident", "before", "shift", "unshift", "wrap"))
        k.first, k.last = sb("first", [P, 1]), sb("last", [P, 1])
        k.ones = sb("ones", [P, HI])
        k.w1, k.w2, k.root = (sb(n, [C, C]) for n in ("w1", "w2", "root"))
        k.b1_col = sb("b1_col", [C, 1])
        k.indeg = sb("indeg", [P, HI])
        k.sorted = sb("sorted", [P, 2, 2, T])
        k.key = sb("key", [P, 2, T + 2])
        k.index = sb("index", [P, 2, T, 3], I32)
        k.is_last = sb("is_last", [P, T])
        k.dinv = sb("dinv", [P, T])
        k.rel_weight = sb("rel_weight", [P, T, R])
        k.flat = nc.dram_tensor("flat_dram", (2, P * T), F32, kind="Internal").ap()
        k.minus_half = sb("minus_half", [P, HI])
        k.node_dinv, k.whole = sb("node_dinv", [P, HI]), sb("whole", [P, HI])
        k.vectors = [k.L0_b1, k.L0_b2, k.L1_bias, k.L2_bm1, k.L2_bm2, k.L2_bu1, k.L2_bu2]
        k.ones3, k.rows3 = sb("ones3", [3, P], BF16), sb("rows3", [3, len(k.vectors), C], BF16)
        k.zero_row = sb("zero_row", [1, P])
        k.w_rel = sb("w_rel", [C, R, C])
        k.stats_edges = sb("stats_edges", [C, 2])
        k.stats_whole = sb("stats_whole", [C, 2])
        k.spread = sb("spread", [P, 6, C])
        k.bm1_col, k.bu1_col = sb("bm1_col", [C, 1]), sb("bu1_col", [C, 1])
        k.wm1a, k.wm1b, k.wu1a, k.wu2, k.wc, k.cb = (sb(n, [C, C]) for n in ("wm1a", "wm1b", "wu1a", "wu2", "wc", "cb"))
        table = lambda name: nc.dram_tensor(name, (N, C), F32, kind="Internal").ap()
        k.H0, k.G1, k.X1, k.O, k.X2 = (table(n) for n in ("h0_dram", "g1_dram", "x1_dram", "o_dram", "x2_dram"))
        slots = lambda name: nc.dram_tensor(name, (T * P, C), F32, kind="Internal").ap()
        k.slot_x, k.slot_g, k.slot_x2 = (slots(n) for n in ("slot_x_dram", "slot_g_dram", "slot_x2_dram"))
        constants(nc, k)
        sort_edges(nc, k)
        edge_tables(nc, k)
        split_rows(nc, k)
        nodes_first(nc, k)
        edges_first(nc, k)
        edges_second(nc, k)
        edges_third(nc, k)
        row_tables(nc, k)
        nodes_second(nc, k)
        edges_fourth(nc, k)
        edges_fifth(nc, k)
        last_rows(nc, k)


def kernel(**inputs):
    import numpy as np
    import concourse.bacc as bacc
    from concourse.bass_utils import run_bass_kernel_spmd

    nc = bacc.Bacc("TRN2", target_bir_lowering=False, num_devices=1)
    arrays = {"in_" + name: np.ascontiguousarray(array) for name, array in inputs.items()}
    given = {name: nc.dram_tensor("in_" + name, array.shape, mybir.dt.from_np(array.dtype), kind="ExternalInput").ap()
             for name, array in ((n[3:], a) for n, a in arrays.items())}
    out = nc.dram_tensor("out", (N, C), F32, kind="ExternalOutput").ap()
    weights = {name.replace("_gnn_", "_"): ap for name, ap in given.items() if name.startswith("L")}
    program(nc, given["x"], given["src"], given["dst"], given["edge_type_8"], weights, out)
    run = run_bass_kernel_spmd(nc, [arrays], core_ids=[0])
    return run.results[0]["out"]
```

```python
from contextlib import ExitStack

import concourse.bass as bass
from concourse import mybir

P = 128
F32 = mybir.dt.float32
BF16 = mybir.dt.bfloat16
I32 = mybir.dt.int32
ALU = mybir.AluOpType
ACT = mybir.ActivationFunctionType
AX = mybir.AxisListType

C = 128
N = 50000
E = 25000
R = 8
EPS = 1e-5
J = 4
GROUP = P * J
NG = -(-N // GROUP)
FULL = N // GROUP
TAIL = (N - FULL * GROUP) // J
HI = NG * J
MID = HI // 2
T = -(-E // P)
ETAIL = E - (P - 1) * T
PAD = NG * GROUP - 1
SKIP = 1 << 20
assert N % J == 0 and T % 2 == 0 and 0 < ETAIL <= T and PAD >= N


class Phase:

    def __init__(self, nc):
        self.nc, self.stack, self.semaphores = nc, ExitStack(), []

    def __enter__(self):
        self.stack.__enter__()
        return self

    def enter_context(self, what):
        return self.stack.enter_context(what)

    def semaphore(self, name):
        self.semaphores.append(self.nc.alloc_semaphore(name))
        return self.semaphores[-1]

    def __exit__(self, *error):
        self.stack.__exit__(*error)
        if error[0] is None:
            self.nc.clear_and_free_semaphores(self.semaphores)
            with self.nc.Block():
                pass


def constants(nc, k):
    with Phase(nc) as ctx:
        raw = ctx.enter_context(nc.sbuf_tensor("raw_iota", [P, HI], I32))
        part = ctx.enter_context(nc.sbuf_tensor("raw_part", [P, 1], I32))
        iota_ready = ctx.semaphore("const_iota_ready")
        chain = ctx.semaphore("const_chain")
        pads_set = ctx.semaphore("const_pads_set")
        edges_in = ctx.semaphore("const_edges_in")
        weights_in = ctx.semaphore("const_weights_in")
        block = ctx.enter_context(nc.Block())

        @block.gpsimd
        def _(pool):
            pool.iota(raw[:, :], pattern=[[1, HI]], base=0, channel_multiplier=0).then_inc(iota_ready, 1)
            pool.iota(part[:, :], pattern=[[0, 1]], base=0, channel_multiplier=1).then_inc(iota_ready, 1)

        @block.vector
        def _(dve):
            dve.memset(k.edge_i[:, :, :], PAD).then_inc(pads_set, 1)
            dve.memset(k.ones[:, :], 1.0)
            dve.memset(k.zero_row[:, :], 0.0)
            dve.wait_ge(iota_ready, 2)
            dve.tensor_copy(k.iota[:, :], raw[:, :]).then_inc(chain, 1)
            dve.tensor_copy(k.part[:, :], part[:, :]).then_inc(chain, 1)
            dve.wait_ge(chain, 2)
            dve.tensor_scalar(k.ident[:, :], k.iota[:, 0:P], k.part[:, :], None, ALU.is_equal).then_inc(chain, 1)
            dve.tensor_scalar(k.before[:, :], k.iota[:, 0:P], k.part[:, :], None, ALU.is_gt).then_inc(chain, 1)
            dve.tensor_scalar(k.shift[:, :], k.iota[:, 0:P], 1.0, k.part[:, :], ALU.add, ALU.is_equal).then_inc(chain, 1)
            dve.tensor_scalar(k.unshift[:, :], k.iota[:, 0:P], -1.0, k.part[:, :], ALU.add, ALU.is_equal).then_inc(chain, 1)
            dve.tensor_scalar(k.first[:, :], k.part[:, :], 0.0, None, ALU.is_equal).then_inc(chain, 1)
            dve.tensor_scalar(k.last[:, :], k.part[:, :], P - 1.0, None, ALU.is_equal).then_inc(chain, 1)
            dve.tensor_scalar(k.ident_b[:, :], k.iota[:, 0:P], k.part[:, :], None, ALU.is_equal)
            dve.tensor_scalar(k.iota_b[:, :], k.iota[:, :], -float(MID), None, ALU.add).then_inc(chain, 1)
            dve.wait_ge(chain, 9)
            dve.tensor_scalar(k.wrap[:, :], k.iota[:, 0:P], P - 1.0, k.first[:, :], ALU.is_equal, ALU.mult).then_inc(chain, 1)
            dve.wait_ge(chain, 10)

        @block.sync
        def _(sp):
            sp.dma_start(k.w1[:, :], k.L0_W1).then_inc(weights_in, 16)
            sp.dma_start(k.w2[:, :], k.L0_W2).then_inc(weights_in, 16)
            sp.dma_start(k.w_rel[:, :, :], k.L1_W.rearrange("r i o -> i r o")).then_inc(weights_in, 16)
            sp.dma_start(k.root[:, :], k.L1_root).then_inc(weights_in, 16)
            sp.dma_start(k.b1_col[:, :], k.L0_b1.rearrange("(c a) -> c a", a=1)).then_inc(weights_in, 16)
            sp.wait_ge(pads_set, 1)
            lists = [k.dst, k.src, k.edge_type]
            for r, flat in enumerate(lists):
                sp.dma_start(k.edge_i[0:P - 1, r, :],
                             flat[0:(P - 1) * T].rearrange("(p t) -> p t", t=T)).then_inc(edges_in, 16)
                sp.dma_start(k.edge_i[P - 1:P, r, 0:ETAIL],
                             flat[(P - 1) * T:E].rearrange("(a t) -> a t", a=1)).then_inc(edges_in, 16)
            sp.wait_ge(edges_in, 16 * 2 * len(lists))
            sp.wait_ge(weights_in, 16 * 5)


def sort_edges(nc, k):
    with Phase(nc) as ctx:
        sb = lambda name, shape, dt=F32: ctx.enter_context(nc.sbuf_tensor("so_" + name, shape, dt))
        ps = lambda name: ctx.enter_context(nc.psum_tensor("so_" + name, [P, 512], F32))
        sem = lambda name: ctx.semaphore("so_" + name)
        node = k.edge_i
        part_i, hi_i, tmp_i = (sb(n, [P, 2, T], I32) for n in ("part_i", "hi_i", "tmp_i"))
        lo, hi, node_f, pay, place = (sb(n, [P, 2, T]) for n in ("lo", "hi", "node_f", "pay", "place"))
        lo_b = sb("lo_b", [P, 2, T], BF16)
        type_i = sb("type_i", [P, T], I32)
        type_f = sb("type_f", [P, T])
        place_i = sb("place_i", [P, 2, T], I32)
        one_lo = sb("one_lo", [P, 2, P], BF16)
        one_hi = sb("one_hi", [P, 2, HI], BF16)
        lo_t = sb("lo_t", [P, 2, P])
        same_lo = sb("same_lo", [P, 2, P], BF16)
        base = sb("base", [P, 2, HI])
        hist = sb("hist", [P, 2, HI])
        picked = sb("picked", [P, 2, HI])
        got = sb("got", [P, 2, 1])
        rows = sb("rows", [P, 2, 1])
        starts = sb("starts", [P, 2, 1])
        zero_b = sb("zero_b", [P, HI], BF16)
        warm = sb("warm", [P, 1])
        put_lo = sb("put_lo", [P, 2, P])
        put_hi = sb("put_hi", [P, 2, 2, T])
        run_ps = [ps("run0"), ps("run1")]
        pick_ps = [ps("pick0"), ps("pick1")]
        row_ps = [ps("row0"), ps("row1")]
        sum_ps = ps("sum")
        chain = sem("chain")
        digits = sem("digits")
        zeroed = sem("zeroed")
        ones_ready, ones_used = sem("ones_ready"), sem("ones_used")
        rows_ready, starts_ready, base_ready, base_in = (sem(n) for n in ("rows_ready", "starts_ready", "base_ready", "base_in"))
        row_ready, masks_ready, run_copied, run_updated = (sem(n) for n in ("row_ready", "masks_ready", "run_copied", "run_updated"))
        pick_ready, pick_read, got_free, turn = (sem(n) for n in ("pick_ready", "pick_read", "got_free", "turn"))
        put_ready, put_used = sem("put_ready"), sem("put_used")
        block = ctx.enter_context(nc.Block())

        def one_hots(dve, t, o):
            dve.tensor_scalar(one_lo[:, o, :], k.iota_b[:, MID:MID + P], lo[:, o, bass.ds(t, 1)], None, ALU.is_equal)
            return dve.tensor_scalar(one_hi[:, o, :], k.iota_b[:, :], hi[:, o, bass.ds(t, 1)], None, ALU.is_equal)

        @block.vector
        def _(dve):
            links = [0]

            def link(ins):
                links[0] += 1
                ins.then_inc(chain, 1)
                dve.wait_ge(chain, links[0])

            dve.memset(zero_b[:, :], 0.0).then_inc(zeroed, 1)
            both = node[:, 0:2, :]
            dve.tensor_scalar(part_i[:, :, :], both, 2, 127, ALU.logical_shift_right, ALU.bitwise_and).then_inc(digits, 1)
            dve.tensor_scalar(hi_i[:, :, :], both, 9, 2, ALU.logical_shift_right, ALU.logical_shift_left).then_inc(digits, 1)
            dve.tensor_scalar(tmp_i[:, :, :], both, 3, None, ALU.bitwise_and).then_inc(digits, 1)
            dve.tensor_scalar(type_i[:, :], node[:, 2, :], R - 1, None, ALU.bitwise_and).then_inc(digits, 1)
            dve.wait_ge(digits, 4)
            dve.tensor_tensor(hi[:, :, :], hi_i[:, :, :], tmp_i[:, :, :], ALU.add).then_inc(digits, 1)
            dve.tensor_copy(lo[:, :, :], part_i[:, :, :]).then_inc(digits, 1)
            dve.wait_ge(digits, 5)
            dve.tensor_scalar(hi[:, :, :], hi[:, :, :], -float(MID), None, ALU.add)
            dve.tensor_copy(type_f[:, :], type_i[:, :]).then_inc(digits, 1)
            dve.tensor_copy(node_f[:, :, :], both).then_inc(digits, 1)
            dve.tensor_copy(lo_b[:, :, :], part_i[:, :, :]).then_inc(digits, 1)
            dve.wait_ge(digits, 9)
            for o in range(2):
                dve.scalar_tensor_tensor(pay[:, o, :], node_f[:, o, :], float(R), type_f[:, :],
                                         ALU.mult, ALU.add).then_inc(digits, 1)
            dve.wait_ge(digits, 11)
            with dve.Fori(0, T) as t:
                for o in range(2):
                    dve.wait_ge(ones_used, t * 2 + o + 1)
                    one_hots(dve, t, o).then_inc(ones_ready, 1)
            dve.wait_ge(ones_used, 2 * T + 2)
            for o in range(2):
                dve.tensor_copy(hist[:, o, :], run_ps[o][:, 0:HI]).then_inc(base_ready, 1)
            dve.wait_ge(base_ready, 2)
            dve.tensor_copy(k.indeg[:, :], hist[:, 0, :])
            for o in range(2):
                dve.tensor_reduce(rows[:, o, :], hist[:, o, :], AX.X, ALU.add).then_inc(rows_ready, 1)
            dve.wait_ge(starts_ready, 1)
            for o in range(2):
                link(dve.tensor_copy(starts[:, o, :], sum_ps[:, o:o + 1]))
                link(dve.tensor_tensor_scan(picked[:, o, :], k.ones[:, 0:HI], hist[:, o, :], starts[:, o, :],
                                            ALU.mult, ALU.add))
                dve.tensor_tensor(base[:, o, :], picked[:, o, :], hist[:, o, :], ALU.subtract).then_inc(base_in, 1)
            dve.wait_ge(base_in, 2)
            dve.sem_inc(pick_read, 2)
            with dve.Fori(0, T) as t:
                for o in range(2):
                    n = t * 2 + o + 1
                    dve.wait_ge(run_updated, n)
                    dve.wait_ge(pick_read, n)
                    one_hots(dve, t, o)
                    dve.wait_ge(row_ready, n)
                    dve.tensor_scalar(lo_t[:, o, :], row_ps[o][:, 0:P], k.part[:, :], None, ALU.is_equal)
                    dve.scalar_tensor_tensor(same_lo[:, o, :], row_ps[o][:, 0:P], lo[:, o, bass.ds(t, 1)],
                                             k.before[:, :], ALU.is_equal, ALU.mult).then_inc(masks_ready, 1)
                for o in range(2):
                    n = t * 2 + o + 1
                    dve.wait_ge(pick_ready, n)
                    dve.wait_ge(got_free, n)
                    dve.tensor_tensor_reduce(picked[:, o, :], pick_ps[o][:, 0:HI], one_hi[:, o, :], 1.0, 0.0,
                                             ALU.mult, ALU.add, got[:, o, :]).then_inc(pick_read, 1)
            dve.wait_ge(got_free, 2 * T + 2)
            link(dve.tensor_copy(place_i[:, :, :], place[:, :, :]))
            link(dve.tensor_scalar(hi_i[:, :, :], place_i[:, :, :], 7, None, ALU.logical_shift_right))
            link(dve.tensor_scalar(part_i[:, :, :], place_i[:, :, :], 127, None, ALU.bitwise_and))
            link(dve.tensor_copy(hi[:, :, :], hi_i[:, :, :]))
            link(dve.tensor_copy(lo[:, :, :], part_i[:, :, :]))
            with dve.Fori(0, T) as t:
                for o in range(2):
                    at = bass.ds(t, 1)
                    dve.wait_ge(put_used, t * 2 + o + 1)
                    dve.tensor_scalar(put_lo[:, o, :], k.iota[:, 0:P], lo[:, o, at], None, ALU.is_equal)
                    dve.tensor_scalar(put_hi[:, o, 0, :], k.iota[:, 0:T], hi[:, o, at], pay[:, o, at],
                                      ALU.is_equal, ALU.mult)
                    dve.tensor_scalar(put_hi[:, o, 1, :], k.iota[:, 0:T], hi[:, o, at], node_f[:, 1 - o, at],
                                      ALU.is_equal, ALU.mult).then_inc(put_ready, 1)
            dve.wait_ge(put_used, 2 * T + 2)
            for o in range(2):
                for w in range(2):
                    link(dve.tensor_copy(k.sorted[:, o, w, :], run_ps[o][:, w * T:(w + 1) * T]))

        @block.tensor
        def _(pe):
            pe.wait_ge(zeroed, 1)
            pe.sem_inc(ones_used, 2)
            for o in range(2):
                pe.matmul(run_ps[o][:, 0:HI], zero_b[:, 0:P], zero_b[:, :], start=True, stop=True, skip_group_check=True)
            with pe.Fori(0, T) as t:
                for o in range(2):
                    pe.wait_ge(ones_ready, t * 2 + o + 1)
                    pe.matmul(run_ps[o][:, 0:HI], one_lo[:, o, :], one_hi[:, o, :], start=False, stop=True,
                              skip_group_check=True).then_inc(ones_used, 1)
            pe.wait_ge(rows_ready, 2)
            pe.matmul(sum_ps[:, 0:2], k.before[:, :], rows[:, :, :].rearrange("p a b -> p (a b)"),
                      start=True, stop=True).then_inc(starts_ready, 1)
            pe.wait_ge(base_in, 2)
            pe.sem_inc(masks_ready, 2)
            for o in range(2):
                pe.matmul(run_ps[o][:, 0:HI], k.ident[:, :], base[:, o, :], start=True, stop=True,
                          skip_group_check=True).then_inc(run_updated, 1)
            with pe.Fori(0, T) as t:
                for o in range(2):
                    n = t * 2 + o + 1
                    pe.wait_ge(masks_ready, n)
                    pe.matmul(row_ps[o][:, 0:P], lo_b[:, o, bass.ds(t, 1)].to_broadcast([P, P]), k.ident_b[:, :],
                              start=True, stop=True).then_inc(row_ready, 1)
                for o in range(2):
                    n = t * 2 + o + 1
                    pe.wait_ge(masks_ready, n + 2)
                    pe.wait_ge(run_copied, n)
                    pe.matmul(pick_ps[o][:, 0:HI], lo_t[:, o, :], base[:, o, :], start=True, stop=False,
                              skip_group_check=True)
                    pe.matmul(pick_ps[o][:, 0:HI], same_lo[:, o, :], one_hi[:, o, :], start=False, stop=True,
                              skip_group_check=True).then_inc(pick_ready, 1)
                    pe.matmul(run_ps[o][:, 0:HI], one_lo[:, o, :], one_hi[:, o, :], start=False, stop=True,
                              skip_group_check=True).then_inc(run_updated, 1)
            pe.sem_inc(put_used, 2)
            for o in range(2):
                pe.matmul(run_ps[o][:, 0:2 * T], zero_b[:, 0:P], zero_b[:, 0:2 * T], start=True, stop=True,
                          skip_group_check=True)
            with pe.Fori(0, T) as t:
                for o in range(2):
                    pe.wait_ge(put_ready, t * 2 + o + 1)
                    pe.matmul(run_ps[o][:, 0:2 * T], put_lo[:, o, :],
                              put_hi[:, o, :, :].rearrange("p w t -> p (w t)"), start=False, stop=True,
                              skip_group_check=True).then_inc(put_used, 1)

        @block.scalar
        def _(act):
            act.wait_ge(zeroed, 1)
            act.activation(warm[:, :], zero_b[:, 0:1], ACT.Relu)
            with act.Fori(0, T) as t:
                for o in range(2):
                    n = t * 2 + o + 1
                    act.wait_ge(run_updated, n)
                    act.copy(base[:, o, :], run_ps[o][:, 0:HI]).then_inc(run_copied, 1)

        @block.gpsimd
        def _(pool):
            pool.sem_inc(got_free, 2)
            with pool.Fori(0, T) as t:
                for o in range(2):
                    pool.wait_ge(pick_read, t * 2 + o + 3)
                    pool.sem_inc(turn, 1)
                    pool.tensor_copy(place[:, o, bass.ds(t, 1)], got[:, o, :]).then_inc(got_free, 1)


def edge_tables(nc, k):
    with Phase(nc) as ctx:
        sb = lambda name, shape, dt=F32: ctx.enter_context(nc.sbuf_tensor("ta_" + name, shape, dt))
        ps = lambda name: ctx.enter_context(nc.psum_tensor("ta_" + name, [P, 512], F32))
        sem = lambda name: ctx.semaphore("ta_" + name)
        H = T // 2
        pay_i, key_i, type_i = (sb(n, [P, 2, T], I32) for n in ("pay_i", "key_i", "type_i"))
        keys = sb("keys", [P, 2, T + 1])
        typ = sb("typ", [P, T])
        nxt = sb("nxt", [P, 2, T])
        lasts, real, real2, idx = (sb(n, [P, 2, T]) for n in ("lasts", "real", "real2", "idx"))
        turned = sb("turned", [H, 2, 2, P])
        flat = sb("flat", [P, 2, T])
        first_f, last_f = sb("first_f", [P, T]), sb("last_f", [P, T])
        edge_key = sb("edge_key", [P, 2])
        of_r = sb("of_r", [P, R, T])
        upto, begin, count = (sb(n, [P, R, T]) for n in ("upto", "begin", "count"))
        hold = sb("hold", [P, R, T])
        per = sb("per", [P, R])
        carry, carry_t = sb("carry", [P, R]), sb("carry_t", [R, P])
        scanned = sb("scanned", [R, P + 1])
        mine = sb("mine", [P, T])
        weight = sb("weight", [P, 2, T])
        w_rows = sb("w_rows", [H, 2, 2, P])
        a_ps, b_ps, c_ps = ps("a"), ps("b"), ps("c")
        deg_inv = sb("deg_inv", [P, T])
        chain, deg_ready = sem("chain"), sem("deg_ready")
        nxt_ready, nxt_done = sem("nxt_ready"), sem("nxt_done")
        turn_asked, turn_ready, rows_ready = sem("turn_asked"), sem("turn_ready"), sem("rows_ready")
        flat_out, flat_in = sem("flat_out"), sem("flat_in")
        pe_asked, pe_done = sem("pe_asked"), sem("pe_done")
        w_ready, w_out, w_in, w_turned = (sem(n) for n in ("w_ready", "w_out", "w_in", "w_turned"))
        key_asked, key_done = sem("key_asked"), sem("key_done")
        block = ctx.enter_context(nc.Block())
        flat_dram = k.flat.rearrange("w (r c) -> r w c", c=P)
        flat_rows = k.flat.rearrange("w (p t) -> p w t", t=T)

        @block.vector
        def _(dve):
            links = [0]

            def link(ins):
                links[0] += 1
                ins.then_inc(chain, 1)
                dve.wait_ge(chain, links[0])

            link(dve.memset(keys[:, :, :], -1.0))
            link(dve.memset(k.key[:, :, :], -1.0))
            link(dve.tensor_copy(pay_i[:, :, :], k.sorted[:, :, 0, :]))
            link(dve.tensor_scalar(key_i[:, :, :], pay_i[:, :, :], 3, None, ALU.logical_shift_right))
            link(dve.tensor_scalar(type_i[:, :, :], pay_i[:, :, :], R - 1, None, ALU.bitwise_and))
            link(dve.tensor_copy(keys[:, :, 0:T], key_i[:, :, :]))
            link(dve.tensor_copy(k.key[:, :, 1:T + 1], key_i[:, :, :]))
            dve.tensor_copy(typ[:, :], type_i[:, 0, :]).then_inc(turn_asked, 1)
            dve.wait_ge(turn_asked, 1)
            dve.sem_inc(nxt_ready, 1)
            dve.wait_ge(turn_ready, 1)
            dve.tensor_copy(turned[:, :, :, :].rearrange("p a b c -> p (a b c)"), a_ps[0:H, :]).then_inc(rows_ready, 1)
            dve.wait_ge(nxt_done, 1)
            for o in range(2):
                link(dve.tensor_copy(nxt[:, o, :], b_ps[:, o * T:(o + 1) * T]))
            link(dve.tensor_tensor(lasts[:, :, :], nxt[:, :, :], keys[:, :, 0:T], ALU.not_equal))
            link(dve.tensor_scalar(real[:, :, :], keys[:, :, 0:T], N - 0.5, None, ALU.is_lt))
            link(dve.tensor_tensor(lasts[:, :, :], lasts[:, :, :], real[:, :, :], ALU.mult))
            link(dve.tensor_copy(k.is_last[:, :], lasts[:, 0, :]))
            link(dve.tensor_scalar(idx[:, :, :], lasts[:, :, :], -float(SKIP), float(SKIP), ALU.mult, ALU.add))
            link(dve.tensor_tensor(idx[:, :, :], idx[:, :, :], keys[:, :, 0:T], ALU.add))
            for o in range(2):
                link(dve.tensor_copy(k.index[:, o, :, 2], idx[:, o, :]))
            link(dve.tensor_tensor(idx[:, :, :], keys[:, :, 0:T], real[:, :, :], ALU.mult))
            for o in range(2):
                link(dve.tensor_copy(k.index[:, o, :, 1 - o], idx[:, o, :]))
            link(dve.tensor_scalar(real2[:, :, :], k.sorted[:, :, 1, :], N - 0.5, None, ALU.is_lt))
            link(dve.tensor_tensor(idx[:, :, :], k.sorted[:, :, 1, :], real2[:, :, :], ALU.mult))
            for o in range(2):
                link(dve.tensor_copy(k.index[:, o, :, o], idx[:, o, :]))
            dve.wait_ge(flat_in, 16)
            link(dve.memset(edge_key[:, :], 0.0))
            dve.tensor_copy(edge_key[:, 0:1], flat[:, 0, 0:1])
            dve.tensor_copy(edge_key[:, 1:2], flat[:, 0, T - 1:T]).then_inc(key_asked, 1)
            dve.wait_ge(key_done, 1)
            link(dve.tensor_tensor(first_f[:, 1:T], flat[:, 0, 1:T], flat[:, 0, 0:T - 1], ALU.not_equal))
            link(dve.tensor_copy(carry[:, 0:2], c_ps[:, 0:2]))
            link(dve.tensor_tensor(first_f[:, 0:1], carry[:, 1:2], flat[:, 0, 0:1], ALU.not_equal))
            link(dve.tensor_tensor(last_f[:, 0:T - 1], flat[:, 0, 1:T], flat[:, 0, 0:T - 1], ALU.not_equal))
            link(dve.tensor_tensor(last_f[:, T - 1:T], carry[:, 0:1], flat[:, 0, T - 1:T], ALU.not_equal))
            link(dve.tensor_tensor(first_f[:, 0:1], first_f[:, 0:1], k.first[:, :], ALU.max))
            link(dve.tensor_tensor(last_f[:, T - 1:T], last_f[:, T - 1:T], k.last[:, :], ALU.max))
            for r in range(R):
                link(dve.tensor_scalar(of_r[:, r, :], flat[:, 1, :], float(r), None, ALU.is_equal))
            for r in range(R):
                link(dve.tensor_tensor_scan(upto[:, r, :], k.ones[:, 0:T], of_r[:, r, :], 0.0, ALU.mult, ALU.add))
            dve.tensor_copy(per[:, :], upto[:, :, T - 1]).then_inc(pe_asked, 1)
            dve.wait_ge(pe_done, 1)
            link(dve.tensor_copy(carry[:, :], c_ps[:, 0:R]))
            for r in range(R):
                link(dve.tensor_scalar(upto[:, r, :], upto[:, r, :], carry[:, r:r + 1], None, ALU.add))
            link(dve.tensor_tensor(begin[:, :, :], upto[:, :, :], of_r[:, :, :], ALU.subtract))
            fb = first_f[:, :].rearrange("p (a t) -> p a t", a=1).to_broadcast([P, R, T])
            link(dve.tensor_tensor(hold[:, :, :], begin[:, :, :], fb, ALU.mult))
            for r in range(R):
                link(dve.tensor_tensor_scan(begin[:, r, :], k.ones[:, 0:T], hold[:, r, :], 0.0, ALU.mult, ALU.max))
            dve.tensor_copy(per[:, :], begin[:, :, T - 1]).then_inc(pe_asked, 1)
            dve.wait_ge(pe_done, 2)
            link(dve.memset(scanned[:, :], 0.0))
            link(dve.tensor_copy(carry_t[:, :], c_ps[0:R, 0:P]))
            link(dve.tensor_tensor_scan(scanned[:, 1:P + 1], k.ones[0:R, 0:P], carry_t[:, :], 0.0, ALU.mult, ALU.max))
            dve.sem_inc(pe_asked, 1)
            dve.wait_ge(pe_done, 3)
            link(dve.tensor_copy(carry[:, :], c_ps[:, 0:R]))
            for r in range(R):
                link(dve.tensor_scalar(begin[:, r, :], begin[:, r, :], carry[:, r:r + 1], None, ALU.max))
            lb = last_f[:, :].rearrange("p (a t) -> p a t", a=1).to_broadcast([P, R, T])
            link(dve.tensor_scalar(hold[:, :, :], upto[:, :, :], -1.0, float(P * T), ALU.mult, ALU.add))
            link(dve.tensor_tensor(hold[:, :, :], hold[:, :, :], lb, ALU.mult))
            for r in range(R):
                link(dve.tensor_tensor_scan(count[:, r, ::-1], k.ones[:, 0:T], hold[:, r, ::-1], 0.0, ALU.mult, ALU.max))
            dve.tensor_copy(per[:, :], count[:, :, 0]).then_inc(pe_asked, 1)
            dve.wait_ge(pe_done, 4)
            link(dve.memset(scanned[:, :], 0.0))
            link(dve.tensor_copy(carry_t[:, :], c_ps[0:R, 0:P]))
            link(dve.tensor_tensor_scan(scanned[:, P - 1::-1], k.ones[0:R, 0:P], carry_t[:, ::-1], 0.0,
                                        ALU.mult, ALU.max))
            dve.sem_inc(pe_asked, 1)
            dve.wait_ge(pe_done, 5)
            link(dve.tensor_copy(carry[:, :], c_ps[:, 0:R]))
            for r in range(R):
                link(dve.tensor_scalar(count[:, r, :], count[:, r, :], carry[:, r:r + 1], None, ALU.max))
            link(dve.tensor_tensor(count[:, :, :], count[:, :, :], begin[:, :, :], ALU.add))
            link(dve.tensor_scalar(count[:, :, :], count[:, :, :], -1.0, float(P * T), ALU.mult, ALU.add))
            link(dve.tensor_reduce(mine[:, :], count[:, :, :].rearrange("p r t -> p t r"), AX.X, ALU.add))
            link(dve.tensor_scalar(mine[:, :], mine[:, :], 1.0, None, ALU.add))
            dve.reciprocal(deg_inv[:, :], mine[:, :]).then_inc(deg_ready, 1)
            link(dve.tensor_tensor(hold[:, :, :], count[:, :, :], of_r[:, :, :], ALU.mult))
            dve.wait_ge(w_ready, 1)
            link(dve.tensor_reduce(mine[:, :], hold[:, :, :].rearrange("p r t -> p t r"), AX.X, ALU.add))
            dve.reciprocal(weight[:, 1, :], mine[:, :]).then_inc(w_ready, 1)
            dve.wait_ge(w_turned, 1)
            link(dve.tensor_copy(k.dinv[:, :], a_ps[:, 0:T]))
            link(dve.tensor_copy(mine[:, :], a_ps[:, T:2 * T]))
            for r in range(R):
                link(dve.tensor_scalar(nxt[:, 0, :], typ[:, :], float(r), None, ALU.is_equal))
                link(dve.tensor_tensor(k.rel_weight[:, :, r], nxt[:, 0, :], mine[:, :], ALU.mult))

        @block.tensor
        def _(pe):
            pe.wait_ge(turn_asked, 1)
            pe.wait_ge(nxt_ready, 1)
            for half in range(2):
                for w, table in enumerate((keys[:, 0, :], typ[:, :])):
                    last = pe.transpose(a_ps[0:H, (w * 2 + half) * P:(w * 2 + half + 1) * P],
                                        table[:, half * H:(half + 1) * H], k.ident[:, :])
            last.then_inc(turn_ready, 1)
            for o in range(2):
                pe.matmul(b_ps[:, o * T:(o + 1) * T], k.shift[:, :], keys[:, o, 0:T], start=True, stop=False)
                last = pe.matmul(b_ps[:, o * T:(o + 1) * T], k.wrap[:, :], keys[:, o, 1:T + 1], start=False, stop=True)
            last.then_inc(nxt_done, 1)
            pe.wait_ge(key_asked, 1)
            pe.matmul(c_ps[:, 0:1], k.shift[:, :], edge_key[:, 0:1], start=True, stop=True)

            pe.matmul(c_ps[:, 1:2], k.unshift[:, :], edge_key[:, 1:2], start=True, stop=True).then_inc(key_done, 1)
            pe.wait_ge(pe_asked, 1)
            pe.matmul(c_ps[:, 0:R], k.before[:, :], per[:, :], start=True, stop=True).then_inc(pe_done, 1)
            pe.wait_ge(pe_asked, 2)
            pe.transpose(c_ps[0:R, 0:P], per[:, :], k.ident[:, :]).then_inc(pe_done, 1)
            pe.wait_ge(pe_asked, 3)
            pe.transpose(c_ps[:, 0:R], scanned[:, 0:P], k.ident[0:R, 0:R]).then_inc(pe_done, 1)
            pe.wait_ge(pe_asked, 4)
            pe.transpose(c_ps[0:R, 0:P], per[:, :], k.ident[:, :]).then_inc(pe_done, 1)
            pe.wait_ge(pe_asked, 5)
            pe.transpose(c_ps[:, 0:R], scanned[:, 1:P + 1], k.ident[0:R, 0:R]).then_inc(pe_done, 1)
            pe.wait_ge(w_in, 32)
            for w in range(2):
                for half in range(2):
                    last = pe.transpose(a_ps[:, w * T + half * H:w * T + (half + 1) * H],
                                        w_rows[:, w, half, :], k.ident[0:H, 0:H])
            last.then_inc(w_turned, 1)

        @block.scalar
        def _(act):
            act.wait_ge(deg_ready, 1)
            act.activation(weight[:, 0, :], deg_inv[:, :], ACT.Sqrt).then_inc(w_ready, 1)

        @block.sync
        def _(sp):
            sp.wait_ge(rows_ready, 1)
            for half in range(2):
                sp.dma_start(flat_dram[half * H:(half + 1) * H], turned[:, :, half, :]).then_inc(flat_out, 16)
            sp.wait_ge(flat_out, 32)
            sp.dma_start(flat[:, :, :], flat_rows).then_inc(flat_in, 16)
            sp.wait_ge(w_ready, 2)
            sp.wait_ge(flat_in, 16)
            sp.dma_start(flat_rows, weight[:, :, :]).then_inc(w_out, 16)
            sp.wait_ge(w_out, 16)
            for half in range(2):
                sp.dma_start(w_rows[:, :, half, :], flat_dram[half * H:(half + 1) * H]).then_inc(w_in, 16)
            sp.wait_ge(w_in, 32)


def split_rows(nc, k):
    with Phase(nc) as ctx:
        sb = lambda name, shape, dt=F32: ctx.enter_context(nc.sbuf_tensor("sp_" + name, shape, dt))
        V = len(k.vectors)
        whole, rest, rest2 = (sb(n, [3, V, C]) for n in ("whole", "rest", "rest2"))
        part = [sb(f"part{i}", [3, V, C], BF16) for i in range(3)]
        sel = sb("sel", [3, 3])
        acc = sb("acc", [3, V, C])
        chain = ctx.semaphore("sp_chain")
        rows_in = ctx.semaphore("sp_rows_in")
        exponent = ctx.semaphore("sp_exponent")
        block = ctx.enter_context(nc.Block())

        @block.sync
        def _(sp):
            for v, vector in enumerate(k.vectors):
                for i in range(3):
                    sp.dma_start(whole[i:i + 1, v, :], vector.rearrange("(a c) -> a c", a=1)).then_inc(rows_in, 16)
            sp.wait_ge(rows_in, 16 * 3 * V)

        @block.gpsimd
        def _(pool):
            pool.memset(k.minus_half[:, :], -0.5).then_inc(exponent, 1)
            pool.wait_ge(exponent, 1)
            pool.tensor_scalar(k.node_dinv[:, :], k.indeg[:, :], 1.0, None, ALU.add).then_inc(exponent, 1)
            pool.tensor_scalar(k.whole[:, :], k.indeg[:, :], 0.5, None, ALU.is_lt).then_inc(exponent, 1)
            pool.wait_ge(exponent, 3)
            pool.tensor_tensor(k.node_dinv[:, :], k.node_dinv[:, :], k.minus_half[:, :], ALU.pow).then_inc(exponent, 1)
            pool.wait_ge(exponent, 4)

        @block.vector
        def _(dve):
            links = [0]

            def link(ins):
                links[0] += 1
                ins.then_inc(chain, 1)
                dve.wait_ge(chain, links[0])

            link(dve.memset(k.ones3[:, :], 1.0))
            dve.wait_ge(rows_in, 16 * 3 * V)
            link(dve.tensor_copy(part[0][:, :, :], whole[:, :, :]))
            link(dve.tensor_tensor(rest[:, :, :], whole[:, :, :], part[0][:, :, :], ALU.subtract))
            link(dve.tensor_copy(part[1][:, :, :], rest[:, :, :]))
            link(dve.tensor_tensor(rest2[:, :, :], rest[:, :, :], part[1][:, :, :], ALU.subtract))
            link(dve.tensor_copy(part[2][:, :, :], rest2[:, :, :]))
            for i in range(3):
                link(dve.tensor_scalar(sel[:, i:i + 1], k.part[0:3, :], float(i), None, ALU.is_equal))
            link(dve.tensor_scalar(acc[:, :, :], part[0][:, :, :], sel[:, 0:1], None, ALU.mult))
            for i in (1, 2):
                link(dve.scalar_tensor_tensor(acc[:, :, :], part[i][:, :, :], sel[:, i:i + 1], acc[:, :, :],
                                              ALU.mult, ALU.add))
            link(dve.tensor_copy(k.rows3[:, :, :], acc[:, :, :]))


def node_rows(table, g, rows):
    return table[bass.ds(g * GROUP, rows * J), :].rearrange("(p j) c -> p j c", j=J)


class Turns:

    def __init__(self, nc, ctx, prefix, L, steps, moves, soft=""):
        self.L = L
        self.steps = {name: ctx.semaphore(f"{prefix}_{name}") for name in steps.split()}
        self.moves = {name: [ctx.semaphore(f"{prefix}_{name}{b}") for b in range(L)]
                      for name in (moves + " " + soft).split()}
        self.start = {name: 0 if name in soft.split() else 16 for name in self.moves}

    def __getitem__(self, name):
        return self.steps[name]

    def credit(self, eng):
        for step in self.steps.values():
            eng.sem_inc(step, self.L)
        for name, lanes in self.moves.items():
            for lane in lanes:
                if self.start[name]:
                    eng.sem_inc(lane, self.start[name])

    def done(self, eng, name, n):
        eng.wait_ge(self.steps[name], n + self.L)

    def freed(self, eng, name, n, back=0):
        eng.wait_ge(self.steps[name], n + self.L - (back or self.L))

    def landed(self, eng, name, b, n):
        assert not isinstance(n, int) or n > 0
        eng.wait_ge(self.moves[name][b], (n - b - 1) * (16 // self.L) + 16 + self.start[name])

    def drained(self, eng, name, b, n):
        if isinstance(n, int) and n <= self.L and not self.start[name]:
            return
        eng.wait_ge(self.moves[name][b], (n - b - 1) * (16 // self.L) + self.start[name])

    def stored(self, eng, name, b, n, back):
        b, n = (b - back) % self.L, n - back
        eng.wait_ge(self.moves[name][b], (n - b - 1) * (16 // self.L) + 16 + self.start[name])

    def drain(self, eng, name, count):
        for n in range(count + 1, count + self.L + 1):
            self.drained(eng, name, (n - 1) % self.L, n)


def row_blocks(bank):
    return bank[:, :].rearrange("c (j p) -> c j p", j=J)


L = 4
LONG = 8


def each_step(eng, step, lag, count=T, L=L):
    for i in range(2 * L):
        step(i, i)
    with eng.Fori(2, count // L) as r:
        for b in range(L):
            step(r * L + b, b)
    for i in range(count // L * L, count + lag):
        step(i, i)


def live(t, count=T):
    return not isinstance(t, int) or 0 <= t < count


class PowerNorm:

    def __init__(self, nc, ctx, prefix, k, w, S, go, used, name):
        sb = lambda n, shape: [ctx.enter_context(nc.sbuf_tensor(f"{prefix}_{name}_{n}{b}", shape, F32)) for b in range(w.L)]
        self.k, self.w, self.S, self.go, self.used, self.name = k, w, S, go, used, name
        self.six, self.mv = sb("six", [P, S, 6]), sb("mv", [P, S, 2])
        self.ve, self.rs = sb("ve", [P, S]), sb("rs", [P, S])

    @staticmethod
    def steps(name):
        return f" {name}_six {name}_mv {name}_ve {name}_rs "

    def stats(self, dve, X, b, n, rows=P):
        w, a = self.w, self.name
        w.freed(dve, a + "_mv", n)
        for s in range(self.S):
            last = dve.bn_stats(self.six[b][0:rows, s, :], X[0:rows, s, :])
        last.then_inc(w[a + "_six"], 1)
        w.done(dve, a + "_six", n)
        w.freed(dve, self.used, n)
        dve.sem_inc(self.go["dve"], 1)
        for s in range(self.S):
            last = dve.bn_aggr(self.mv[b][0:rows, s, :], self.six[b][0:rows, s, :])
        last.then_inc(w[a + "_mv"], 1)

    def power(self, pool, b, n, rows=P):
        w, a = self.w, self.name
        w.done(pool, a + "_mv", n)
        w.freed(pool, a + "_rs", n)
        pool.sem_inc(self.go["pool"], 1)
        pool.tensor_scalar(self.ve[b][0:rows, :], self.mv[b][0:rows, :, 1], EPS, None, ALU.add).then_inc(w[a + "_ve"], 1)
        w.done(pool, a + "_ve", n)
        w.freed(pool, self.used, n)
        pool.tensor_tensor(self.rs[b][0:rows, :], self.ve[b][0:rows, :], self.k.minus_half[0:rows, 0:self.S], ALU.pow)\
            .then_inc(w[a + "_rs"], 1)

    def apply(self, dve, Y, X, b, n, step, rows=P):
        self.w.done(dve, self.name + "_rs", n)
        for s in range(self.S):
            last = dve.tensor_scalar(Y[0:rows, s, :], X[0:rows, s, :], self.mv[b][0:rows, s, 0:1],
                                     self.rs[b][0:rows, s:s + 1], ALU.subtract, ALU.mult)
        last.then_inc(self.w[step], 1)


class Stages:

    def __init__(self, L, count, groups=False):
        self.L, self.count, self.groups = L, count, groups

    def at(self, lag, i, b0):
        t = i - lag
        if not live(t, self.count):
            return None
        place = (t, (b0 - lag) % self.L, t + 1)
        return place + (TAIL if isinstance(t, int) and t == FULL else P,) if self.groups else place

    def each(self, eng, step, lag):
        each_step(eng, step, lag, self.count, self.L)


def nodes_first(nc, k):
    with Phase(nc) as ctx:
        L = LONG
        ring = lambda name, count, shape=[P, J, C]: [ctx.enter_context(nc.sbuf_tensor(f"n1_{name}{b}", shape, F32))
                                                     for b in range(count)]
        X = ring("X", L)
        X1, H, G, O = (ring(n, 4) for n in ("X1", "H", "G", "O"))
        H1, OSQ = ring("H1", 2), ring("OSQ", 2)
        HT, GT, H1T = (ring(n, 2, [C, J, P]) for n in ("HT", "GT", "H1T"))
        rsd, whole = ring("rsd", L, [P, J]), ring("whole", L, [P, J])
        hT, inner, g_ps, outer, h1T, root, stat_ps = (
            ctx.enter_context(nc.psum_tensor(f"n1_{n}_ps", [P, 512], F32))
            for n in ("hT", "inner", "g", "outer", "h1T", "root", "stat"))
        w = Turns(nc, ctx, "n1", L, PowerNorm.steps("a") + "rsd_a xn_a h_a hT_a ht_a w1 gt g_ps g w2 x1"
                  + PowerNorm.steps("b") + "xn_b h_b hT_b ht_b root o osq whole stats", "x_in h_out g_out x1_out o_out")
        stats_taken = ctx.semaphore("n1_stats_taken")
        turn = {e: ctx.semaphore(f"n1_turn_{e}") for e in ("pool", "dve")}
        lnA = PowerNorm(nc, ctx, "n1", k, w, J, turn, "xn_a", "a")
        lnB = PowerNorm(nc, ctx, "n1", k, w, J, turn, "xn_b", "b")
        block = ctx.enter_context(nc.Block())
        s = Stages(L, NG, groups=True)
        flat = lambda tile, rows: tile[0:rows].rearrange("p j c -> p (j c)")

        @block.sync
        def _(sp):
            w.credit(sp)

            def step(i, b0):
                if at := s.at(0, i, b0):
                    g, b, n, rows = at
                    w.freed(sp, "x1", n)
                    sp.dma_start(X[b][0:rows], node_rows(k.x, g, rows)).then_inc(w.moves["x_in"][b], 16)
                for lag, table, tile, size, done, move in ((9, k.O, O, 4, "o", "o_out"), (6, k.X1, X1, 4, "x1", "x1_out"),
                                                           (6, k.G1, G, 4, "g", "g_out"), (3, k.H0, H, 4, "h_a", "h_out")):
                    if at := s.at(lag, i, b0):
                        g, b, n, rows = at
                        w.done(sp, done, n)
                        sp.dma_start(node_rows(table, g, rows), tile[b % size][0:rows]).then_inc(w.moves[move][b], 16)

            s.each(sp, step, 9)
            for move in ("h_out", "g_out", "x1_out", "o_out"):
                w.drain(sp, move, NG)

        @block.vector
        def _(dve):
            def step(i, b0):
                if at := s.at(6, i, b0):
                    g, b, n, rows = at
                    w.freed(dve, "hT_b", n, 2)
                    lnB.apply(dve, H1[b % 2], X1[b % 4], b, n, "xn_b", rows)
                if at := s.at(5, i, b0):
                    g, b, n, rows = at
                    w.done(dve, "w2", n)
                    w.freed(dve, "xn_b", n, 4)
                    w.stored(dve, "x1_out", b, n, 4)
                    dve.tensor_tensor(flat(X1[b % 4], rows), outer[0:rows, :], flat(X[b], rows), ALU.add)\
                        .then_inc(w["x1"], 1)
                    w.done(dve, "x1", n)
                    lnB.stats(dve, X1[b % 4], b, n, rows)
                if at := s.at(2, i, b0):
                    g, b, n, rows = at
                    w.done(dve, "rsd_a", n)
                    w.freed(dve, "hT_a", n, 4)
                    w.stored(dve, "h_out", b, n, 4)
                    for j in range(J):
                        last = dve.tensor_scalar(H[b % 4][0:rows, j, :], X[b][0:rows, j, :], lnA.mv[b][0:rows, j, 0:1],
                                                 rsd[b][0:rows, j:j + 1], ALU.subtract, ALU.mult)
                    last.then_inc(w["xn_a"], 1)
                if at := s.at(1, i, b0):
                    g, b, n, rows = at
                    w.landed(dve, "x_in", b, n)
                    lnA.stats(dve, X[b], b, n, rows)

            s.each(dve, step, 6)
            dve.wait_ge(w["stats"], NG + L)
            dve.tensor_copy(k.stats_whole[:, :], stat_ps[:, 0:2]).then_inc(stats_taken, 1)
            dve.wait_ge(stats_taken, 1)

        @block.gpsimd
        def _(pool):
            def step(i, b0):
                if at := s.at(8, i, b0):
                    g, b, n, rows = at
                    w.freed(pool, "stats", n)
                    pool.sem_inc(turn["pool"], 1)
                    pool.tensor_copy(whole[b][:, :], k.whole[:, bass.ds(g * J, J)]).then_inc(w["whole"], 1)
                if at := s.at(5, i, b0):
                    g, b, n, rows = at
                    lnB.power(pool, b, n, rows)
                if at := s.at(1, i, b0):
                    g, b, n, rows = at
                    lnA.power(pool, b, n, rows)
                    w.done(pool, "a_rs", n)
                    w.freed(pool, "xn_a", n)
                    pool.sem_inc(turn["pool"], 1)
                    pool.tensor_tensor(rsd[b][0:rows, :], lnA.rs[b][0:rows, :],
                                       k.node_dinv[0:rows, bass.ds(g * J, J)], ALU.mult).then_inc(w["rsd_a"], 1)

            s.each(pool, step, 8)

        @block.tensor
        def _(pe):
            pe.matmul(stat_ps[:, 0:2], k.zero_row[:, :], k.zero_row[:, 0:2], start=True, stop=True, skip_group_check=True)

            def rowwise(dst, src, weight, v, rows):
                pe.matmul(dst[0:rows, :].rearrange("p (j c) -> p j c", j=J), k.ones3[:, 0:rows],
                          k.rows3[:, v:v + 1, :].to_broadcast([3, J, C]), start=True, stop=False, skip_group_check=True)
                for j in range(J):
                    last = pe.matmul(dst[0:rows, j * C:(j + 1) * C], src[:, j, 0:rows], weight[:, :], start=False,
                                     stop=True, skip_group_check=True)
                return last

            def turned(dst, src, rows):
                for j in range(J):
                    last = pe.transpose(dst[:, j * P:j * P + rows], src[0:rows, j, :], k.ident[0:rows, 0:rows])
                return last

            def step(i, b0):
                if at := s.at(9, i, b0):
                    g, b, n, rows = at
                    w.done(pe, "osq", n)
                    w.done(pe, "whole", n)
                    for c, src in enumerate((O[b % 4], OSQ[b % 2])):
                        for j in range(J):
                            last = pe.matmul(stat_ps[:, c:c + 1], src[0:rows, j, :], whole[b][0:rows, j:j + 1],
                                             start=False, stop=True, skip_group_check=True)
                    last.then_inc(w["stats"], 1)
                if at := s.at(8, i, b0):
                    g, b, n, rows = at
                    w.done(pe, "ht_b", n)
                    w.freed(pe, "osq", n, 1)
                    rowwise(root, H1T[b % 2], k.root, 2, rows).then_inc(w["root"], 1)
                if at := s.at(7, i, b0):
                    g, b, n, rows = at
                    w.done(pe, "h_b", n)
                    w.freed(pe, "ht_b", n, 1)
                    turned(h1T, H1[b % 2], rows).then_inc(w["hT_b"], 1)
                if at := s.at(5, i, b0):
                    g, b, n, rows = at
                    w.done(pe, "gt", n)
                    w.freed(pe, "g", n, 1)
                    for j in range(J):
                        last = pe.transpose(g_ps[0:rows, j * C:(j + 1) * C], GT[b % 2][:, j, 0:rows], k.ident[:, :])
                    last.then_inc(w["g_ps"], 1)
                    w.freed(pe, "x1", n, 1)
                    rowwise(outer, GT[b % 2], k.w2, 1, rows).then_inc(w["w2"], 1)
                if at := s.at(4, i, b0):
                    g, b, n, rows = at
                    w.done(pe, "ht_a", n)
                    w.freed(pe, "gt", n, 1)
                    pe.matmul(row_blocks(inner)[:, :, 0:rows], k.w1[:, :], HT[b % 2][:, :, 0:rows],
                              start=True, stop=True).then_inc(w["w1"], 1)
                if at := s.at(3, i, b0):
                    g, b, n, rows = at
                    w.done(pe, "h_a", n)
                    w.freed(pe, "ht_a", n, 1)
                    turned(hT, H[b % 4], rows).then_inc(w["hT_a"], 1)

            s.each(pe, step, 9)

        @block.scalar
        def _(act):
            def step(i, b0):
                if at := s.at(8, i, b0):
                    g, b, n, rows = at
                    w.done(act, "root", n)
                    w.freed(act, "stats", n, 4)
                    w.stored(act, "o_out", b, n, 4)
                    act.copy(flat(O[b % 4], rows), root[0:rows, :]).then_inc(w["o"], 1)
                    w.freed(act, "stats", n, 2)
                    act.activation(flat(OSQ[b % 2], rows), root[0:rows, :], ACT.Square).then_inc(w["osq"], 1)
                if at := s.at(7, i, b0):
                    g, b, n, rows = at
                    w.done(act, "hT_b", n)
                    w.freed(act, "root", n, 2)
                    act.copy(H1T[b % 2][:, :, 0:rows], row_blocks(h1T)[:, :, 0:rows]).then_inc(w["ht_b"], 1)
                if at := s.at(6, i, b0):
                    g, b, n, rows = at
                    w.done(act, "xn_b", n)
                    act.activation(H1[b % 2][0:rows], H1[b % 2][0:rows], ACT.Relu).then_inc(w["h_b"], 1)
                if at := s.at(5, i, b0):
                    g, b, n, rows = at
                    w.done(act, "g_ps", n)
                    w.stored(act, "g_out", b, n, 4)
                    act.copy(flat(G[b % 4], rows), g_ps[0:rows, :]).then_inc(w["g"], 1)
                if at := s.at(4, i, b0):
                    g, b, n, rows = at
                    w.done(act, "w1", n)
                    w.freed(act, "w2", n, 2)
                    act.activation(GT[b % 2][:, :, 0:rows], row_blocks(inner)[:, :, 0:rows], ACT.Relu,
                                   bias=k.b1_col[:, :]).then_inc(w["gt"], 1)
                if at := s.at(3, i, b0):
                    g, b, n, rows = at
                    w.done(act, "hT_a", n)
                    w.freed(act, "w1", n, 2)
                    act.copy(HT[b % 2][:, :, 0:rows], row_blocks(hT)[:, :, 0:rows]).then_inc(w["ht_a"], 1)
                if at := s.at(2, i, b0):
                    g, b, n, rows = at
                    w.done(act, "xn_a", n)
                    act.activation(H[b % 4][0:rows], H[b % 4][0:rows], ACT.Relu).then_inc(w["h_a"], 1)

            s.each(act, step, 8)


def tile_rows(table, t):
    return table[bass.ds(t * P, P), :]


class EdgePass:

    def __init__(self, nc, ctx, prefix, k, order, steps, moves, soft, L=L):
        self.k, self.o, self.L = k, order, L
        sb = lambda name, shape, dt=F32: ctx.enter_context(nc.sbuf_tensor(f"{prefix}_{name}", shape, dt))
        self.w = Turns(nc, ctx, prefix, L, "ids sid keys krow masks tot totsb " + steps, moves, soft)
        self.gid = [sb(f"gid{b}", [P, 2], I32) for b in range(L)]
        self.sid = [sb(f"sid{b}", [P, 1], I32) for b in range(L)]
        self.keys = [sb(f"keys{b}", [P, 2]) for b in range(L)]
        self.same, self.carry = ([sb(f"{n}{b}", [P, P]) for b in range(L)] for n in ("same", "carry"))
        self.totsb = [sb(f"totsb{b}", [P, C]) for b in range(L)]
        self.zeroed = ctx.semaphore(f"{prefix}_zeroed")
        self.turn = {e: ctx.semaphore(f"{prefix}_turn_{e}") for e in ("pool", "dve", "act")}

    def start(self, dve):
        dve.memset(self.totsb[self.L - 1][:, :], 0.0).then_inc(self.zeroed, 1)

    def load_ids(self, pool, t, b, n, gathered):
        for move in gathered:
            self.w.drained(pool, move, b, n)
        pool.sem_inc(self.turn["pool"], 1)
        pool.tensor_copy(self.gid[b][:, :], self.k.index[:, self.o, bass.ds(t, 1), 0:2].rearrange("p a c -> p (a c)"))\
            .then_inc(self.w["ids"], 1)

    def gather(self, pool, tile, table, which, b, n, move):
        self.w.done(pool, "ids", n)
        pool.sem_inc(self.turn["pool"], 1)
        pool.indirect_dma_start(tile, None, table, bass.IndirectOffsetOnAxis(ap=self.gid[b][:, which:which + 1], axis=0))\
            .then_inc(self.w.moves[move][b], 16)

    def scatter(self, pool, table, tile, t, b, n, move):
        self.w.drained(pool, move, b, n)
        pool.sem_inc(self.turn["pool"], 1)
        pool.tensor_copy(self.sid[b][:, :], self.k.index[:, self.o, bass.ds(t, 1), 2]).then_inc(self.w["sid"], 1)
        self.w.done(pool, "sid", n)
        pool.sem_inc(self.turn["pool"], 1)
        pool.indirect_dma_start(table, bass.IndirectOffsetOnAxis(ap=self.sid[b][:, 0:1], axis=0), tile, None,
                                bounds_check=N - 1, oob_is_err=False).then_inc(self.w.moves[move][b], 16)

    def load_keys(self, dve, t, b, n):
        self.w.freed(dve, "masks", n)
        dve.tensor_copy(self.keys[b][:, :], self.k.key[:, self.o, bass.ds(t, 2)]).then_inc(self.w["keys"], 1)

    def spread_keys(self, pe, banks, b, n, back=2):
        self.w.done(pe, "keys", n)
        self.w.freed(pe, "masks", n, back)
        pe.matmul(banks[b % 2][:, 0:P], self.keys[b][:, 1:2].to_broadcast([P, P]), self.k.ident[:, :], start=True,
                  stop=True).then_inc(self.w["krow"], 1)

    def masks(self, dve, banks, b, n):
        self.w.done(dve, "krow", n)
        self.w.freed(dve, "tot", n)
        dve.tensor_scalar(self.same[b][:, :], banks[b % 2][:, 0:P], self.keys[b][:, 1:2], None, ALU.is_equal)
        dve.tensor_scalar(self.carry[b][:, :], banks[b % 2][:, 0:P], self.keys[b][:, 0:1], self.k.last[:, :],
                          ALU.is_equal, ALU.mult).then_inc(self.w["masks"], 1)

    def sums(self, pe, banks, parts, b, n):
        self.w.done(pe, "masks", n)
        self.w.done(pe, "totsb", n - 1)
        for i, rows in enumerate(parts):
            pe.matmul(banks[b % 2][:, 0:C], self.same[b][:, :], rows, start=i == 0, stop=False)
        pe.matmul(banks[b % 2][:, 0:C], self.carry[b][:, :], self.totsb[(b - 1) % self.L][:, :], start=False,
                  stop=True).then_inc(self.w["tot"], 1)

    def keep_sums(self, act, banks, b, n):
        self.w.done(act, "tot", n)
        act.copy(self.totsb[b][:, :], banks[b % 2][:, 0:C]).then_inc(self.w["totsb"], 1)


class Norm:

    STEPS = "ln_six ln_mv ln_ve ln_iv ln_rs "

    def __init__(self, nc, ctx, prefix, w, S, go, used, name="ln"):
        L = w.L
        sb = lambda n, shape: [ctx.enter_context(nc.sbuf_tensor(f"{prefix}_{name}_{n}{b}", shape, F32)) for b in range(L)]
        self.w, self.S, self.go, self.name = w, S, go, name
        self.used = used
        self.six, self.mv = sb("six", [P, S, 6]), sb("mv", [P, S, 2])
        self.ve, self.iv, self.rs = (sb(n, [P, S]) for n in ("ve", "iv", "rs"))

    def stats(self, dve, X, b, n):
        w, a = self.w, self.name
        w.freed(dve, a + "_mv", n)
        for s in range(self.S):
            last = dve.bn_stats(self.six[b][:, s, :], X[:, s, :])
        last.then_inc(w[a + "_six"], 1)
        w.done(dve, a + "_six", n)
        w.freed(dve, self.used, n)
        dve.sem_inc(self.go, 1)
        for s in range(self.S):
            last = dve.bn_aggr(self.mv[b][:, s, :], self.six[b][:, s, :])
        last.then_inc(w[a + "_mv"], 1)
        w.done(dve, a + "_mv", n)
        dve.tensor_scalar(self.ve[b][:, :], self.mv[b][:, :, 1], EPS, None, ALU.add).then_inc(w[a + "_ve"], 1)

    def inverse(self, dve, b, n):
        self.w.done(dve, self.name + "_ve", n)
        dve.reciprocal(self.iv[b][:, :], self.ve[b][:, :]).then_inc(self.w[self.name + "_iv"], 1)

    def root(self, act, b, n):
        self.w.done(act, self.name + "_iv", n)
        act.activation(self.rs[b][:, :], self.iv[b][:, :], ACT.Sqrt).then_inc(self.w[self.name + "_rs"], 1)


def edges_first(nc, k):
    with Phase(nc) as ctx:
        L = LONG
        sb = lambda name, shape: [ctx.enter_context(nc.sbuf_tensor(f"e1_{name}{b}", shape, F32)) for b in range(L)]
        p = EdgePass(nc, ctx, "e1", k, 0, Norm.STEPS + "rs3 dv nm a aT at y go hd", "slot_x slot_g", "g_in x_in go_out", L)
        w = p.w
        ln = Norm(nc, ctx, "e1", w, 1, p.turn["dve"], "nm")
        GS, HD, A, AT, GO = (sb(n, [P, C]) for n in ("GS", "HD", "A", "AT", "GO"))
        XD = sb("XD", [P, 1, C])
        rs3, nm, dv = (sb(n, [P, 1]) for n in ("rs3", "nm", "dv"))
        krow, tot, aT, y = ([ctx.enter_context(nc.psum_tensor(f"e1_{n}{b}", [P, 512], F32)) for b in range(2)]
                            for n in ("krow", "tot", "aT", "y"))
        s = Stages(L, T)
        block = ctx.enter_context(nc.Block())

        @block.sync
        def _(sp):
            w.credit(sp)

            def step(i, b0):
                if at := s.at(7, i, b0):
                    t, b, n = at
                    w.done(sp, "go", n)
                    sp.dma_start(tile_rows(k.slot_g, t), GO[b][:, :]).then_inc(w.moves["slot_g"][b], 16)
                if at := s.at(3, i, b0):
                    t, b, n = at
                    w.landed(sp, "x_in", b, n)
                    sp.dma_start(tile_rows(k.slot_x, t), XD[b][:, 0, :]).then_inc(w.moves["slot_x"][b], 16)

            s.each(sp, step, 7)
            w.drain(sp, "slot_x", T)
            w.drain(sp, "slot_g", T)

        @block.gpsimd
        def _(pool):
            def step(i, b0):
                if at := s.at(6, i, b0):
                    t, b, n = at
                    w.done(pool, "go", n)
                    p.scatter(pool, k.G1, GO[b][:, :], t, b, n, "go_out")
                if at := s.at(0, i, b0):
                    t, b, n = at
                    p.load_ids(pool, t, b, n, ("g_in", "x_in"))
                    w.freed(pool, "tot", n)
                    p.gather(pool, GS[b][:, :], k.H0, 0, b, n, "g_in")
                    w.freed(pool, "hd", n)
                    w.drained(pool, "slot_x", b, n)
                    p.gather(pool, XD[b][:, 0, :], k.x, 1, b, n, "x_in")

            s.each(pool, step, 6)
            w.drain(pool, "go_out", T)

        @block.vector
        def _(dve):
            p.start(dve)

            def step(i, b0):
                if at := s.at(4, i, b0):
                    t, b, n = at
                    w.done(dve, "totsb", n)
                    w.done(dve, "hd", n)
                    w.freed(dve, "aT", n)
                    dve.scalar_tensor_tensor(A[b][:, :], p.totsb[b][:, :], dv[b][:, :], HD[b][:, :], ALU.mult,
                                             ALU.add).then_inc(w["a"], 1)
                if at := s.at(3, i, b0):
                    t, b, n = at
                    w.done(dve, "ln_rs", n)
                    w.done(dve, "dv", n)
                    w.freed(dve, "hd", n)
                    dve.tensor_scalar(rs3[b][:, :], ln.rs[b][:, :], dv[b][:, :], dv[b][:, :], ALU.mult, ALU.mult)\
                        .then_inc(w["rs3"], 1)
                    w.done(dve, "rs3", n)
                    dve.tensor_scalar(nm[b][:, :], ln.mv[b][:, :, 0], rs3[b][:, :], -1.0, ALU.mult, ALU.mult)\
                        .then_inc(w["nm"], 1)
                if at := s.at(2, i, b0):
                    t, b, n = at
                    w.freed(dve, "go", n)
                    w.freed(dve, "a", n)
                    dve.tensor_copy(dv[b][:, :], k.dinv[:, bass.ds(t, 1)]).then_inc(w["dv"], 1)
                    p.masks(dve, krow, b, n)
                    w.landed(dve, "x_in", b, n)
                    w.freed(dve, "nm", n)
                    ln.stats(dve, XD[b], b, n)
                    ln.inverse(dve, b, n)
                if at := s.at(1, i, b0):
                    t, b, n = at
                    p.load_keys(dve, t, b, n)

            s.each(dve, step, 4)

        @block.tensor
        def _(pe):
            pe.wait_ge(p.zeroed, 1)

            def step(i, b0):
                if at := s.at(6, i, b0):
                    t, b, n = at
                    w.done(pe, "at", n)
                    w.freed(pe, "go", n, 2)
                    pe.matmul(y[b % 2][:, 0:C], k.ones3[:, :], k.rows3[:, 0, :], start=True, stop=False, skip_group_check=True)
                    pe.matmul(y[b % 2][:, 0:C], AT[b][:, :], k.w1[:, :], start=False, stop=True, skip_group_check=True)\
                        .then_inc(w["y"], 1)
                if at := s.at(5, i, b0):
                    t, b, n = at
                    w.done(pe, "a", n)
                    w.freed(pe, "at", n, 2)
                    pe.transpose(aT[b % 2][:, 0:P], A[b][:, :], k.ident[:, :]).then_inc(w["aT"], 1)
                if at := s.at(3, i, b0):
                    t, b, n = at
                    w.landed(pe, "g_in", b, n)
                    p.sums(pe, tot, [GS[b][:, :]], b, n)
                if at := s.at(2, i, b0):
                    t, b, n = at
                    p.spread_keys(pe, krow, b, n)

            s.each(pe, step, 6)

        @block.scalar
        def _(act):
            def step(i, b0):
                if at := s.at(6, i, b0):
                    t, b, n = at
                    w.done(act, "y", n)
                    w.drained(act, "go_out", b, n)
                    w.drained(act, "slot_g", b, n)
                    act.activation(GO[b][:, :], y[b % 2][:, 0:C], ACT.Relu, scale=dv[b][:, :]).then_inc(w["go"], 1)
                if at := s.at(5, i, b0):
                    t, b, n = at
                    w.done(act, "aT", n)
                    w.freed(act, "y", n)
                    act.copy(AT[b][:, :], aT[b % 2][:, 0:P]).then_inc(w["at"], 1)
                if at := s.at(4, i, b0):
                    t, b, n = at
                    w.done(act, "nm", n)
                    w.freed(act, "a", n)
                    act.activation(HD[b][:, :], XD[b][:, 0, :], ACT.Relu, bias=nm[b][:, :], scale=rs3[b][:, :])\
                        .then_inc(w["hd"], 1)
                if at := s.at(3, i, b0):
                    t, b, n = at
                    w.freed(act, "a", n)
                    p.keep_sums(act, tot, b, n)
                    ln.root(act, b, n)

            s.each(act, step, 6)


def edges_second(nc, k):
    with Phase(nc) as ctx:
        L = LONG
        sb = lambda name, shape: [ctx.enter_context(nc.sbuf_tensor(f"e2_{name}{b}", shape, F32)) for b in range(L)]
        p = EdgePass(nc, ctx, "e2", k, 0, "dv a as aT at y xo", "x_in d_in slot_x", "g_in xo_out", L)
        w = p.w
        GS, XD, GD, A, AS, AT, XO = (sb(n, [P, C]) for n in ("GS", "XD", "GD", "A", "AS", "AT", "XO"))
        dv = sb("dv", [P, 1])
        krow, tot, aT, y = ([ctx.enter_context(nc.psum_tensor(f"e2_{n}{b}", [P, 512], F32)) for b in range(2)]
                            for n in ("krow", "tot", "aT", "y"))
        s = Stages(L, T)
        block = ctx.enter_context(nc.Block())

        @block.sync
        def _(sp):
            w.credit(sp)

            def step(i, b0):
                if at := s.at(6, i, b0):
                    t, b, n = at
                    w.done(sp, "xo", n)
                    sp.dma_start(tile_rows(k.slot_x2, t), XO[b][:, :]).then_inc(w.moves["slot_x"][b], 16)
                if at := s.at(0, i, b0):
                    t, b, n = at
                    w.freed(sp, "xo", n)
                    sp.dma_start(XD[b][:, :], tile_rows(k.slot_x, t)).then_inc(w.moves["x_in"][b], 16)
                    w.freed(sp, "a", n)
                    sp.dma_start(GD[b][:, :], tile_rows(k.slot_g, t)).then_inc(w.moves["d_in"][b], 16)

            s.each(sp, step, 6)
            w.drain(sp, "slot_x", T)

        @block.gpsimd
        def _(pool):
            def step(i, b0):
                if at := s.at(5, i, b0):
                    t, b, n = at
                    w.done(pool, "xo", n)
                    p.scatter(pool, k.X1, XO[b][:, :], t, b, n, "xo_out")
                if at := s.at(0, i, b0):
                    t, b, n = at
                    p.load_ids(pool, t, b, n, ("g_in",))
                    w.freed(pool, "tot", n)
                    p.gather(pool, GS[b][:, :], k.G1, 0, b, n, "g_in")

            s.each(pool, step, 5)
            w.drain(pool, "xo_out", T)

        @block.vector
        def _(dve):
            p.start(dve)

            def step(i, b0):
                if at := s.at(5, i, b0):
                    t, b, n = at
                    w.done(dve, "y", n)
                    w.landed(dve, "x_in", b, n)
                    w.drained(dve, "xo_out", b, n)
                    w.drained(dve, "slot_x", b, n)
                    dve.tensor_tensor(XO[b][:, :], y[b % 2][:, 0:C], XD[b][:, :], ALU.add).then_inc(w["xo"], 1)
                if at := s.at(3, i, b0):
                    t, b, n = at
                    w.done(dve, "totsb", n)
                    w.landed(dve, "d_in", b, n)
                    w.freed(dve, "as", n)
                    dve.tensor_tensor(A[b][:, :], p.totsb[b][:, :], GD[b][:, :], ALU.add).then_inc(w["a"], 1)
                    w.done(dve, "a", n)
                    w.done(dve, "dv", n)
                    w.freed(dve, "aT", n)
                    dve.tensor_scalar(AS[b][:, :], A[b][:, :], dv[b][:, :], None, ALU.mult).then_inc(w["as"], 1)
                if at := s.at(2, i, b0):
                    t, b, n = at
                    w.freed(dve, "as", n)
                    dve.tensor_copy(dv[b][:, :], k.dinv[:, bass.ds(t, 1)]).then_inc(w["dv"], 1)
                    p.masks(dve, krow, b, n)
                if at := s.at(1, i, b0):
                    t, b, n = at
                    p.load_keys(dve, t, b, n)

            s.each(dve, step, 5)

        @block.tensor
        def _(pe):
            pe.wait_ge(p.zeroed, 1)

            def step(i, b0):
                if at := s.at(5, i, b0):
                    t, b, n = at
                    w.done(pe, "at", n)
                    w.freed(pe, "xo", n, 2)
                    pe.matmul(y[b % 2][:, 0:C], k.ones3[:, :], k.rows3[:, 1, :], start=True, stop=False, skip_group_check=True)
                    pe.matmul(y[b % 2][:, 0:C], AT[b][:, :], k.w2[:, :], start=False, stop=True, skip_group_check=True)\
                        .then_inc(w["y"], 1)
                if at := s.at(4, i, b0):
                    t, b, n = at
                    w.done(pe, "as", n)
                    w.freed(pe, "at", n, 2)
                    pe.transpose(aT[b % 2][:, 0:P], AS[b][:, :], k.ident[:, :]).then_inc(w["aT"], 1)
                if at := s.at(3, i, b0):
                    t, b, n = at
                    w.landed(pe, "g_in", b, n)
                    p.sums(pe, tot, [GS[b][:, :]], b, n)
                if at := s.at(2, i, b0):
                    t, b, n = at
                    p.spread_keys(pe, krow, b, n)

            s.each(pe, step, 5)

        @block.scalar
        def _(act):
            def step(i, b0):
                if at := s.at(4, i, b0):
                    t, b, n = at
                    w.done(act, "aT", n)
                    w.freed(act, "y", n)
                    act.copy(AT[b][:, :], aT[b % 2][:, 0:P]).then_inc(w["at"], 1)
                if at := s.at(3, i, b0):
                    t, b, n = at
                    w.freed(act, "a", n)
                    p.keep_sums(act, tot, b, n)

            s.each(act, step, 4)


def edges_third(nc, k):
    with Phase(nc) as ctx:
        L = LONG
        sb = lambda name, shape, count=L: [ctx.enter_context(nc.sbuf_tensor(f"e3_{name}{b}", shape, F32))
                                           for b in range(count)]
        p = EdgePass(nc, ctx, "e3", k, 0, Norm.STEPS + "rw nm h hT ht rel pm ps pq msg y o osq st", "x_in",
                     "g_in o_out", L)
        w = p.w
        ln = Norm(nc, ctx, "e3", w, 2, p.turn["dve"], "h")
        XX, H = sb("XX", [P, 2, C]), sb("H", [P, 2, C])
        HT = sb("HT", [C, 2, P])
        PM, PS, PQ = sb("PM", [P, R, C], 2), sb("PS", [P, R // 2, C], 2), sb("PQ", [P, R // 4, C], 2)
        MSG, O, OSQ = sb("MSG", [P, C]), sb("O", [P, C]), sb("OSQ", [P, C])
        rw, lst, nm = sb("rw", [P, R]), sb("lst", [P, 1]), sb("nm", [P, 2])
        bank = lambda name: ctx.enter_context(nc.psum_tensor(f"e3_{name}", [P, 512], F32))
        krow, tot, hT, stat = (bank(n) for n in ("krow", "tot", "hT", "stat"))
        y = [bank(f"y{b}") for b in range(2)]
        rel = [bank(f"rel{h}") for h in range(2)]
        stats_taken = ctx.semaphore("e3_stats_taken")
        block = ctx.enter_context(nc.Block())
        s = Stages(L, T)

        @block.sync
        def _(sp):
            w.credit(sp)

            def step(i, b0):
                if at := s.at(0, i, b0):
                    t, b, n = at
                    w.freed(sp, "h", n)
                    sp.dma_start(XX[b][:, 1, :], tile_rows(k.slot_x2, t)).then_inc(w.moves["x_in"][b], 16)

            s.each(sp, step, 0)

        @block.gpsimd
        def _(pool):
            def step(i, b0):
                if at := s.at(9, i, b0):
                    t, b, n = at
                    w.done(pool, "o", n)
                    p.scatter(pool, k.O, O[b][:, :], t, b, n, "o_out")
                if at := s.at(0, i, b0):
                    t, b, n = at
                    p.load_ids(pool, t, b, n, ("g_in",))
                    w.freed(pool, "h", n)
                    p.gather(pool, XX[b][:, 0, :], k.X1, 0, b, n, "g_in")

            s.each(pool, step, 9)
            w.drain(pool, "o_out", T)

        @block.vector
        def _(dve):
            p.start(dve)

            def step(i, b0):
                if at := s.at(9, i, b0):
                    t, b, n = at
                    w.done(dve, "totsb", n)
                    w.done(dve, "y", n)
                    w.drained(dve, "o_out", b, n)
                    w.freed(dve, "st", n)
                    dve.tensor_tensor(O[b][:, :], y[b % 2][:, 0:C], p.totsb[b][:, :], ALU.add)\
                        .then_inc(w["o"], 1)
                if at := s.at(6, i, b0):
                    t, b, n = at
                    w.freed(dve, "pm", n)
                    w.freed(dve, "st", n)
                    dve.tensor_copy(lst[b][:, :], k.is_last[:, bass.ds(t, 1)])
                    dve.tensor_copy(rw[b][:, :], k.rel_weight[:, bass.ds(t, 1), :].rearrange("p a r -> p (a r)"))\
                        .then_inc(w["rw"], 1)
                    p.masks(dve, [krow, krow], b, n)
                    w.done(dve, "rw", n)
                    w.done(dve, "rel", n)
                    w.freed(dve, "ps", n, 2)
                    for h in range(2):
                        last = dve.tensor_tensor(
                            PM[b % 2][:, h * 4:h * 4 + 4, :], rel[h][:, :].rearrange("p (r c) -> p r c", c=C),
                            rw[b][:, h * 4:h * 4 + 4].rearrange("p (r c) -> p r c", c=1).to_broadcast([P, 4, C]), ALU.mult)
                    last.then_inc(w["pm"], 1)
                    w.done(dve, "pm", n)
                    w.freed(dve, "pq", n, 2)
                    dve.tensor_tensor(PS[b % 2][:, :, :], PM[b % 2][:, 0:4, :], PM[b % 2][:, 4:8, :], ALU.add)\
                        .then_inc(w["ps"], 1)
                    w.done(dve, "ps", n)
                    w.freed(dve, "msg", n, 2)
                    dve.tensor_tensor(PQ[b % 2][:, :, :], PS[b % 2][:, 0:2, :], PS[b % 2][:, 2:4, :], ALU.add)\
                        .then_inc(w["pq"], 1)
                    w.done(dve, "pq", n)
                    w.freed(dve, "tot", n)
                    dve.tensor_tensor(MSG[b][:, :], PQ[b % 2][:, 0, :], PQ[b % 2][:, 1, :], ALU.add)\
                        .then_inc(w["msg"], 1)
                if at := s.at(3, i, b0):
                    t, b, n = at
                    p.load_keys(dve, t, b, n)
                    w.done(dve, "ln_rs", n)
                    w.freed(dve, "h", n)
                    dve.scalar_tensor_tensor(nm[b][:, :], ln.mv[b][:, :, 0], -1.0, ln.rs[b][:, :], ALU.mult, ALU.mult)\
                        .then_inc(w["nm"], 1)
                if at := s.at(2, i, b0):
                    t, b, n = at
                    w.landed(dve, "g_in", b, n)
                    w.landed(dve, "x_in", b, n)
                    w.freed(dve, "nm", n)
                    ln.stats(dve, XX[b], b, n)
                    ln.inverse(dve, b, n)

            s.each(dve, step, 9)
            dve.wait_ge(w["st"], T + L)
            dve.tensor_copy(k.stats_edges[:, :], stat[:, 0:2]).then_inc(stats_taken, 1)
            dve.wait_ge(stats_taken, 1)

        @block.tensor
        def _(pe):
            pe.wait_ge(p.zeroed, 1)
            pe.matmul(stat[:, 0:2], k.zero_row[:, :], k.zero_row[:, 0:2], start=True, stop=True, skip_group_check=True)

            def step(i, b0):
                if at := s.at(11, i, b0):
                    t, b, n = at
                    w.done(pe, "osq", n)
                    for c, src in enumerate((O, OSQ)):
                        last = pe.matmul(stat[:, c:c + 1], src[b][:, :], lst[b][:, :], start=False, stop=True,
                                         skip_group_check=True)
                    last.then_inc(w["st"], 1)
                if at := s.at(8, i, b0):
                    t, b, n = at
                    w.done(pe, "msg", n)
                    p.sums(pe, [tot, tot], [MSG[b][:, :]], b, n)
                    w.freed(pe, "o", n, 2)
                    pe.matmul(y[b % 2][:, 0:C], k.ones3[:, :], k.rows3[:, 2, :], start=True, stop=False, skip_group_check=True)
                    pe.matmul(y[b % 2][:, 0:C], HT[b][:, 1, :], k.root[:, :], start=False, stop=True, skip_group_check=True)\
                        .then_inc(w["y"], 1)
                if at := s.at(6, i, b0):
                    t, b, n = at
                    p.spread_keys(pe, [krow, krow], b, n, 1)
                    w.done(pe, "ht", n)
                    w.freed(pe, "pm", n, 1)
                    for h in range(2):
                        last = pe.matmul(rel[h][:, :], HT[b][:, 0, :],
                                         k.w_rel[:, h * 4:h * 4 + 4, :].rearrange("c r d -> c (r d)"), start=True, stop=True)
                    last.then_inc(w["rel"], 1)
                if at := s.at(5, i, b0):
                    t, b, n = at
                    w.done(pe, "h", n)
                    w.freed(pe, "ht", n, 1)
                    for half in range(2):
                        last = pe.transpose(hT[:, half * P:(half + 1) * P], H[b][:, half, :], k.ident[:, :])
                    last.then_inc(w["hT"], 1)

            s.each(pe, step, 11)

        @block.scalar
        def _(act):
            def step(i, b0):
                if at := s.at(10, i, b0):
                    t, b, n = at
                    w.done(act, "o", n)
                    w.freed(act, "st", n)
                    act.activation(OSQ[b][:, :], O[b][:, :], ACT.Square).then_inc(w["osq"], 1)
                if at := s.at(8, i, b0):
                    t, b, n = at
                    w.freed(act, "o", n)
                    p.keep_sums(act, [tot, tot], b, n)
                if at := s.at(5, i, b0):
                    t, b, n = at
                    w.done(act, "hT", n)
                    w.freed(act, "y", n)
                    act.copy(HT[b][:, :, :].rearrange("c s p -> c (s p)"), hT[:, 0:2 * P]).then_inc(w["ht"], 1)
                if at := s.at(4, i, b0):
                    t, b, n = at
                    w.done(act, "nm", n)
                    w.freed(act, "hT", n)
                    act.activation(H[b][:, 0, :], XX[b][:, 0, :], ACT.Relu, bias=nm[b][:, 0:1], scale=ln.rs[b][:, 0:1])
                    act.activation(H[b][:, 1, :], XX[b][:, 1, :], ACT.Relu, bias=nm[b][:, 1:2], scale=ln.rs[b][:, 1:2])\
                        .then_inc(w["h"], 1)
                if at := s.at(3, i, b0):
                    t, b, n = at
                    ln.root(act, b, n)

            s.each(act, step, 10)


def row_tables(nc, k):
    with Phase(nc) as ctx:
        sb = lambda name, shape: ctx.enter_context(nc.sbuf_tensor("rt_" + name, shape, F32))
        cols = sb("cols", [C, 6])
        gamma_beta = sb("gamma_beta", [C, 2])
        bm2 = sb("bm2", [C, 1])
        total, mean, tmp, var, std, shift = (sb(n, [C, w]) for n, w in
                                             (("total", 2), ("mean", 2), ("tmp", 1), ("var", 1), ("std", 1), ("shift", 1)))
        wm2, wm2_t, wu1b = (sb(n, [C, C]) for n in ("wm2", "wm2_t", "wu1b"))
        spread = [ctx.enter_context(nc.psum_tensor(f"rt_spread{i}", [P, 512], F32)) for i in range(2)]
        wt_ps, wc_ps = (ctx.enter_context(nc.psum_tensor(f"rt_{n}", [P, 512], F32)) for n in ("wt", "wc"))
        chain, loaded, var_ready, std_ready = (ctx.semaphore("rt_" + n) for n in ("chain", "loaded", "var_ready", "std_ready"))
        turned, turned_in, product, cols_ready, spread_ready = (
            ctx.semaphore("rt_" + n) for n in ("turned", "turned_in", "product", "cols_ready", "spread_ready"))
        block = ctx.enter_context(nc.Block())
        col = lambda vector: vector.rearrange("(c a) -> c a", a=1)
        loads = [(gamma_beta[:, 0:1], col(k.L1_gamma)), (gamma_beta[:, 1:2], col(k.L1_beta)),
                 (cols[:, 2:3], col(k.L2_gamma)), (cols[:, 3:4], col(k.L2_beta)),
                 (cols[:, 4:5], col(k.L3_W2)), (cols[:, 5:6], col(k.L3_W3)), (bm2[:, :], col(k.L2_bm2)),
                 (k.bm1_col[:, :], col(k.L2_bm1)), (k.bu1_col[:, :], col(k.L2_bu1)), (wm2[:, :], k.L2_wm2),
                 (wu1b[:, :], k.L2_wu1[C:2 * C, :]), (k.wu1a[:, :], k.L2_wu1[0:C, :]), (k.wu2[:, :], k.L2_wu2),
                 (k.wm1a[:, :], k.L2_wm1[0:C, :]), (k.wm1b[:, :], k.L2_wm1[C:2 * C, :])]

        @block.sync
        def _(sp):
            for tile, source in loads:
                sp.dma_start(tile, source).then_inc(loaded, 16)
            sp.wait_ge(loaded, 16 * len(loads))

        @block.vector
        def _(dve):
            links = [0]

            def link(ins):
                links[0] += 1
                ins.then_inc(chain, 1)
                dve.wait_ge(chain, links[0])

            link(dve.tensor_tensor(total[:, :], k.stats_whole[:, :], k.stats_edges[:, :], ALU.add))
            link(dve.tensor_scalar(mean[:, :], total[:, :], 1.0 / N, None, ALU.mult))
            link(dve.tensor_tensor(tmp[:, :], mean[:, 0:1], mean[:, 0:1], ALU.mult))
            link(dve.tensor_tensor(var[:, :], mean[:, 1:2], tmp[:, :], ALU.subtract))
            link(dve.tensor_scalar(var[:, :], var[:, :], 0.0, EPS, ALU.max, ALU.add))
            dve.reciprocal(tmp[:, :], var[:, :]).then_inc(var_ready, 1)
            dve.wait_ge(std_ready, 1)
            dve.wait_ge(loaded, 16 * len(loads))
            link(dve.tensor_tensor(cols[:, 0:1], gamma_beta[:, 0:1], std[:, :], ALU.mult))
            link(dve.tensor_tensor(shift[:, :], mean[:, 0:1], cols[:, 0:1], ALU.mult))
            dve.tensor_tensor(cols[:, 1:2], gamma_beta[:, 1:2], shift[:, :], ALU.subtract).then_inc(cols_ready, 1)
            dve.wait_ge(turned, 1)
            dve.tensor_copy(wm2_t[:, :], wt_ps[:, 0:C]).then_inc(turned_in, 1)
            dve.wait_ge(product, 1)
            dve.tensor_copy(k.wc[:, :], wc_ps[:, 0:C])
            link(dve.tensor_copy(k.cb[:, :], wc_ps[:, C:2 * C]))
            dve.wait_ge(spread_ready, 1)
            for i in range(2):
                link(dve.tensor_copy(k.spread[:, i * 3:i * 3 + 3, :].rearrange("p a c -> p (a c)"), spread[i][:, 0:3 * C]))

        @block.scalar
        def _(act):
            act.wait_ge(var_ready, 1)
            act.activation(std[:, :], tmp[:, :], ACT.Sqrt).then_inc(std_ready, 1)

        @block.tensor
        def _(pe):
            pe.wait_ge(loaded, 16 * len(loads))
            pe.transpose(wt_ps[:, 0:C], wm2[:, :], k.ident[:, :]).then_inc(turned, 1)
            pe.wait_ge(turned_in, 1)
            pe.matmul(wc_ps[:, 0:C], wm2_t[:, :], wu1b[:, :], start=True, stop=True)
            pe.matmul(wc_ps[:, C:2 * C], bm2[:, :].to_broadcast([C, P]), wu1b[:, :], start=True, stop=True)\
                .then_inc(product, 1)
            pe.wait_ge(cols_ready, 1)
            for i in range(6):
                last = pe.matmul(spread[i // 3][:, i % 3 * C:(i % 3 + 1) * C], cols[:, i:i + 1].to_broadcast([C, P]),
                                 k.ident[:, :], start=True, stop=True)
            last.then_inc(spread_ready, 1)


def nodes_second(nc, k):
    with Phase(nc) as ctx:
        L = LONG
        ring = lambda name, count, shape=[P, J, C]: [ctx.enter_context(nc.sbuf_tensor(f"n2_{name}{b}", shape, F32))
                                                     for b in range(count)]
        X1, O, Z, Q, X2, H = (ring(n, 4) for n in ("X1", "O", "Z", "Q", "X2", "H"))
        S, YG = ring("S", 2), ring("YG", 2)
        X3 = ring("X3", L)
        HT = ring("HT", 4, [C, J, P])
        SU, UT = (ring(n, 2, [C, J, P]) for n in ("SU", "UT"))
        hT, u, y = ([ctx.enter_context(nc.psum_tensor(f"n2_{n}{b}", [P, 512], F32)) for b in range(2)]
                    for n in ("hT", "u", "y"))
        w = Turns(nc, ctx, "n2", L, "z0 z s sq q1 iq gate zg x2 x2b" + PowerNorm.steps("a") + "xn h hT ht u su ut y"
                  + PowerNorm.steps("b") + "yg x3", "x1_in o_in x2_out h_out out")
        turn = {e: ctx.semaphore(f"n2_turn_{e}") for e in ("pool", "dve")}
        lnA = PowerNorm(nc, ctx, "n2", k, w, J, turn, "xn", "a")
        lnB = PowerNorm(nc, ctx, "n2", k, w, J, turn, "x3", "b")
        minus_one = ctx.enter_context(nc.sbuf_tensor("n2_minus_one", [P, 1], F32))
        constant = ctx.semaphore("n2_constant")
        block = ctx.enter_context(nc.Block())
        s = Stages(L, NG, groups=True)
        vec = lambda i, rows: k.spread[0:rows, i:i + 1, :].to_broadcast([rows, J, C])

        @block.sync
        def _(sp):
            w.credit(sp)

            def step(i, b0):
                if at := s.at(0, i, b0):
                    g, b, n, rows = at
                    w.freed(sp, "x2", n, 4)
                    sp.dma_start(X1[b % 4][0:rows], node_rows(k.X1, g, rows)).then_inc(w.moves["x1_in"][b], 16)
                    w.freed(sp, "z0", n, 4)
                    sp.dma_start(O[b % 4][0:rows], node_rows(k.O, g, rows)).then_inc(w.moves["o_in"][b], 16)
                if at := s.at(11, i, b0):
                    g, b, n, rows = at
                    w.done(sp, "x3", n)
                    sp.dma_start(node_rows(k.out, g, rows), X3[b][0:rows]).then_inc(w.moves["out"][b], 16)
                if at := s.at(7, i, b0):
                    g, b, n, rows = at
                    w.done(sp, "h", n)
                    sp.dma_start(node_rows(k.XH[:, C:2 * C], g, rows), H[b % 4][0:rows]).then_inc(w.moves["h_out"][b], 16)
                if at := s.at(4, i, b0):
                    g, b, n, rows = at
                    w.done(sp, "x2", n)
                    sp.dma_start(node_rows(k.XH[:, 0:C], g, rows), X2[b % 4][0:rows]).then_inc(w.moves["x2_out"][b], 16)

            s.each(sp, step, 11)
            for move in ("x2_out", "h_out", "out"):
                w.drain(sp, move, NG)

        @block.gpsimd
        def _(pool):
            def step(i, b0):
                if at := s.at(9, i, b0):
                    g, b, n, rows = at
                    lnB.power(pool, b, n, rows)
                if at := s.at(4, i, b0):
                    g, b, n, rows = at
                    lnA.power(pool, b, n, rows)
                    w.done(pool, "x2", n)
                    w.stored(pool, "out", b, n, L)
                    pool.tensor_tensor(X3[b][0:rows], X2[b % 4][0:rows], vec(3, rows), ALU.add).then_inc(w["x2b"], 1)
                if at := s.at(3, i, b0):
                    g, b, n, rows = at
                    w.done(pool, "gate", n)
                    pool.tensor_tensor(Q[b % 4][0:rows], Q[b % 4][0:rows], Z[b % 4][0:rows], ALU.mult).then_inc(w["zg"], 1)
                    w.done(pool, "zg", n)
                    w.freed(pool, "xn", n, 4)
                    w.freed(pool, "x2b", n, 4)
                    w.stored(pool, "x2_out", b, n, 4)
                    pool.tensor_tensor(X2[b % 4][0:rows], X1[b % 4][0:rows], Q[b % 4][0:rows], ALU.add)\
                        .then_inc(w["x2"], 1)
                if at := s.at(1, i, b0):
                    g, b, n, rows = at
                    z = Z[b % 4][0:rows]
                    w.landed(pool, "o_in", b, n)
                    w.freed(pool, "x2", n, 4)
                    pool.tensor_tensor(z, O[b % 4][0:rows], vec(0, rows), ALU.mult).then_inc(w["z0"], 1)
                    w.done(pool, "z0", n)
                    w.landed(pool, "x1_in", b, n)
                    pool.tensor_tensor(z, z, vec(1, rows), ALU.add).then_inc(w["z"], 1)

            s.each(pool, step, 9)

        @block.vector
        def _(dve):
            dve.memset(minus_one[:, :], -1.0).then_inc(constant, 1)

            def step(i, b0):
                if at := s.at(10, i, b0):
                    g, b, n, rows = at
                    w.done(dve, "b_rs", n)
                    w.freed(dve, "x3", n, 2)
                    for j in range(J):
                        last = dve.scalar_tensor_tensor(
                            YG[b % 2][0:rows, j, :], y[b % 2][0:rows, j * C:(j + 1) * C], lnB.mv[b][0:rows, j, 0:1],
                            k.spread[0:rows, 2, :], ALU.subtract, ALU.mult)
                    last.then_inc(w["yg"], 1)
                    w.done(dve, "yg", n)
                    w.done(dve, "x2b", n)
                    for j in range(J):
                        last = dve.scalar_tensor_tensor(
                            X3[b][0:rows, j, :], YG[b % 2][0:rows, j, :], lnB.rs[b][0:rows, j:j + 1],
                            X3[b][0:rows, j, :], ALU.mult, ALU.add)
                    last.then_inc(w["x3"], 1)
                if at := s.at(9, i, b0):
                    g, b, n, rows = at
                    w.done(dve, "y", n)
                    lnB.stats(dve, y[b % 2][:, :].rearrange("p (j c) -> p j c", j=J), b, n, rows)
                if at := s.at(8, i, b0):
                    g, b, n, rows = at
                    w.done(dve, "su", n)
                    w.freed(dve, "y", n, 2)
                    dve.scalar_tensor_tensor(UT[b % 2][:, :, 0:rows], row_blocks(u[b % 2])[:, :, 0:rows],
                                             k.bu1_col[:, :], SU[b % 2][:, :, 0:rows], ALU.add, ALU.mult)\
                        .then_inc(w["ut"], 1)
                if at := s.at(5, i, b0):
                    g, b, n, rows = at
                    w.freed(dve, "hT", n, 4)
                    w.stored(dve, "h_out", b, n, 4)
                    lnA.apply(dve, H[b % 4], X2[b % 4], b, n, "xn", rows)
                if at := s.at(4, i, b0):
                    g, b, n, rows = at
                    w.done(dve, "x2", n)
                    lnA.stats(dve, X2[b % 4], b, n, rows)
                if at := s.at(2, i, b0):
                    g, b, n, rows = at
                    q = Q[b % 4][0:rows]
                    w.done(dve, "q1", n)
                    dve.reciprocal(q, q).then_inc(w["iq"], 1)

            s.each(dve, step, 10)

        @block.scalar
        def _(act):
            act.wait_ge(constant, 1)

            def step(i, b0):
                if at := s.at(8, i, b0):
                    g, b, n, rows = at
                    w.done(act, "u", n)
                    w.freed(act, "ut", n, 2)
                    act.activation(SU[b % 2][:, :, 0:rows], row_blocks(u[b % 2])[:, :, 0:rows], ACT.Sigmoid,
                                   bias=k.bu1_col[:, :]).then_inc(w["su"], 1)
                if at := s.at(7, i, b0):
                    g, b, n, rows = at
                    w.done(act, "hT", n)
                    w.freed(act, "y", n, 4)
                    act.copy(HT[b % 4][:, :, 0:rows], row_blocks(hT[b % 2])[:, :, 0:rows]).then_inc(w["ht"], 1)
                if at := s.at(6, i, b0):
                    g, b, n, rows = at
                    w.done(act, "xn", n)
                    act.activation(H[b % 4][0:rows], H[b % 4][0:rows], ACT.Relu).then_inc(w["h"], 1)
                if at := s.at(3, i, b0):
                    g, b, n, rows = at
                    q = Q[b % 4][0:rows]
                    w.done(act, "iq", n)
                    act.activation(q, q, ACT.Relu, bias=minus_one[0:rows, :], scale=2.0).then_inc(w["gate"], 1)
                if at := s.at(2, i, b0):
                    g, b, n, rows = at
                    sg, q = S[b % 2][0:rows], Q[b % 4][0:rows]
                    w.done(act, "z", n)
                    w.freed(act, "sq", n, 2)
                    act.activation(sg, Z[b % 4][0:rows], ACT.Sigmoid, scale=-1.0).then_inc(w["s"], 1)
                    w.done(act, "s", n)
                    w.freed(act, "x2", n, 4)
                    act.activation(q, sg, ACT.Square).then_inc(w["sq"], 1)
                    w.done(act, "sq", n)
                    act.activation(q, q, ACT.Relu, bias=k.ones[0:rows, 0:1]).then_inc(w["q1"], 1)

            s.each(act, step, 8)

        @block.tensor
        def _(pe):
            def step(i, b0):
                if at := s.at(9, i, b0):
                    g, b, n, rows = at
                    w.done(pe, "ut", n)
                    w.freed(pe, "x3", n, 2)
                    pe.matmul(y[b % 2][0:rows, :].rearrange("p (j c) -> p j c", j=J), k.ones3[:, 0:rows],
                              k.rows3[:, 6:7, :].to_broadcast([3, J, C]), start=True, stop=False, skip_group_check=True)
                    for j in range(J):
                        for left, right in ((UT[b % 2], k.wu2), (HT[b % 4], k.ident)):
                            last = pe.matmul(y[b % 2][0:rows, j * C:(j + 1) * C], left[:, j, 0:rows], right[:, :],
                                             start=False, stop=True, skip_group_check=True)
                    last.then_inc(w["y"], 1)
                if at := s.at(8, i, b0):
                    g, b, n, rows = at
                    w.done(pe, "ht", n)
                    w.freed(pe, "ut", n, 2)
                    pe.matmul(row_blocks(u[b % 2])[:, :, 0:rows], k.wu1a[:, :], HT[b % 4][:, :, 0:rows],
                              start=True, stop=True).then_inc(w["u"], 1)
                if at := s.at(7, i, b0):
                    g, b, n, rows = at
                    w.done(pe, "h", n)
                    w.freed(pe, "ht", n, 2)
                    for j in range(J):
                        last = pe.transpose(hT[b % 2][:, j * P:j * P + rows], H[b % 4][0:rows, j, :],
                                            k.ident[0:rows, 0:rows])
                    last.then_inc(w["hT"], 1)

            s.each(pe, step, 9)


def edges_fourth(nc, k):
    with Phase(nc) as ctx:
        L = LONG
        sb = lambda name, shape, count=L: [ctx.enter_context(nc.sbuf_tensor(f"e4_{name}{b}", shape, F32))
                                           for b in range(count)]
        p = EdgePass(nc, ctx, "e4", k, 1, "hT ht m sm mt q qq u su ut y" + PowerNorm.steps("b") + "xb yg x3", "",
                     "s_in d_in x_out", L)
        w = p.w
        lnB = PowerNorm(nc, ctx, "e4", k, w, 1, p.turn, "x3", "b")
        XS, XD = sb("XS", [P, 2 * C]), sb("XD", [P, 2 * C])
        HT = sb("HT", [C, 2, P])
        SM, MT, QQ, SU, UT = (sb(n, [P, C]) for n in ("SM", "MT", "QQ", "SU", "UT"))
        XB, YG = sb("XB", [P, C]), sb("YG", [P, C])
        bank = lambda name: ctx.enter_context(nc.psum_tensor(f"e4_{name}", [P, 512], F32))
        krow, hT, m, q, tot, u = (bank(n) for n in ("krow", "hT", "m", "q", "tot", "u"))
        y = [bank("y0"), bank("y1")]
        block = ctx.enter_context(nc.Block())
        s = Stages(L, T)

        @block.sync
        def _(sp):
            w.credit(sp)

        @block.gpsimd
        def _(pool):
            def step(i, b0):
                if at := s.at(8, i, b0):
                    t, b, n = at
                    w.done(pool, "x3", n)
                    p.scatter(pool, k.out, XB[b][:, :], t, b, n, "x_out")
                if at := s.at(7, i, b0):
                    t, b, n = at
                    lnB.power(pool, b, n)
                if at := s.at(0, i, b0):
                    t, b, n = at
                    p.load_ids(pool, t, b, n, ("s_in", "d_in"))
                    w.freed(pool, "xb", n)
                    p.gather(pool, XS[b][:, :], k.XH, 0, b, n, "s_in")
                    w.freed(pool, "hT", n)
                    p.gather(pool, XD[b][:, :], k.XH, 1, b, n, "d_in")

            s.each(pool, step, 8)
            w.drain(pool, "x_out", T)

        @block.vector
        def _(dve):
            p.start(dve)

            def step(i, b0):
                if at := s.at(8, i, b0):
                    t, b, n = at
                    w.done(dve, "b_rs", n)
                    w.freed(dve, "x3", n)
                    dve.scalar_tensor_tensor(YG[b][:, :], y[b % 2][:, 0:C], lnB.mv[b][:, 0, 0:1], k.spread[:, 2, :],
                                             ALU.subtract, ALU.mult).then_inc(w["yg"], 1)
                    w.done(dve, "yg", n)
                    w.done(dve, "xb", n)
                    dve.scalar_tensor_tensor(XB[b][:, :], YG[b][:, :], lnB.rs[b][:, 0:1], XB[b][:, :],
                                             ALU.mult, ALU.add).then_inc(w["x3"], 1)
                if at := s.at(7, i, b0):
                    t, b, n = at
                    w.drained(dve, "x_out", b, n)
                    dve.tensor_tensor(XB[b][:, :], XS[b][:, 0:C], k.spread[:, 3, :], ALU.add).then_inc(w["xb"], 1)
                    w.done(dve, "y", n)
                    lnB.stats(dve, y[b % 2][:, 0:C].rearrange("p (a c) -> p a c", a=1), b, n)
                if at := s.at(6, i, b0):
                    t, b, n = at
                    w.done(dve, "su", n)
                    w.freed(dve, "y", n)
                    dve.scalar_tensor_tensor(UT[b][:, :], u[:, 0:P], k.bu1_col[:, :], SU[b][:, :], ALU.add, ALU.mult)\
                        .then_inc(w["ut"], 1)
                if at := s.at(4, i, b0):
                    t, b, n = at
                    w.done(dve, "q", n)
                    w.freed(dve, "tot", n)
                    dve.tensor_tensor(QQ[b][:, :], q[:, 0:C], k.cb[:, :], ALU.add).then_inc(w["qq"], 1)
                if at := s.at(3, i, b0):
                    t, b, n = at
                    w.done(dve, "sm", n)
                    w.freed(dve, "q", n)
                    dve.scalar_tensor_tensor(MT[b][:, :], m[:, 0:P], k.bm1_col[:, :], SM[b][:, :], ALU.add, ALU.mult)\
                        .then_inc(w["mt"], 1)
                if at := s.at(2, i, b0):
                    t, b, n = at
                    p.masks(dve, [krow, krow], b, n)
                if at := s.at(1, i, b0):
                    t, b, n = at
                    p.load_keys(dve, t, b, n)

            s.each(dve, step, 8)

        @block.scalar
        def _(act):
            def step(i, b0):
                if at := s.at(6, i, b0):
                    t, b, n = at
                    w.done(act, "u", n)
                    w.freed(act, "ut", n)
                    act.activation(SU[b][:, :], u[:, 0:P], ACT.Sigmoid, bias=k.bu1_col[:, :]).then_inc(w["su"], 1)
                if at := s.at(5, i, b0):
                    t, b, n = at
                    w.freed(act, "u", n)
                    p.keep_sums(act, [tot, tot], b, n)
                if at := s.at(3, i, b0):
                    t, b, n = at
                    w.done(act, "m", n)
                    w.freed(act, "mt", n)
                    act.activation(SM[b][:, :], m[:, 0:P], ACT.Sigmoid, bias=k.bm1_col[:, :]).then_inc(w["sm"], 1)
                if at := s.at(2, i, b0):
                    t, b, n = at
                    w.done(act, "hT", n)
                    w.freed(act, "y", n)
                    act.copy(HT[b][:, :, :].rearrange("c s p -> c (s p)"), hT[:, 0:2 * P]).then_inc(w["ht"], 1)

            s.each(act, step, 6)

        @block.tensor
        def _(pe):
            pe.wait_ge(p.zeroed, 1)

            def step(i, b0):
                if at := s.at(7, i, b0):
                    t, b, n = at
                    w.done(pe, "ut", n)
                    w.freed(pe, "x3", n, 2)
                    pe.matmul(y[b % 2][:, 0:C], k.ones3[:, :], k.rows3[:, 6, :], start=True, stop=False,
                              skip_group_check=True)
                    pe.matmul(y[b % 2][:, 0:C], UT[b][:, :], k.wu2[:, :], start=False, stop=True, skip_group_check=True)
                    pe.matmul(y[b % 2][:, 0:C], HT[b][:, 0, :], k.ident[:, :], start=False, stop=True,
                              skip_group_check=True).then_inc(w["y"], 1)
                if at := s.at(6, i, b0):
                    t, b, n = at
                    w.done(pe, "totsb", n)
                    w.freed(pe, "ut", n, 1)
                    pe.matmul(u[:, 0:P], k.wu1a[:, :], HT[b][:, 0, :], start=True, stop=False)
                    pe.matmul(u[:, 0:P], p.totsb[b][:, :], k.ident[:, :], start=False, stop=True).then_inc(w["u"], 1)
                if at := s.at(5, i, b0):
                    t, b, n = at
                    w.done(pe, "qq", n)
                    p.sums(pe, [tot, tot], [QQ[b][:, :]], b, n)
                if at := s.at(4, i, b0):
                    t, b, n = at
                    w.done(pe, "mt", n)
                    w.freed(pe, "qq", n, 1)
                    pe.matmul(q[:, 0:C], MT[b][:, :], k.wc[:, :], start=True, stop=True).then_inc(w["q"], 1)
                if at := s.at(3, i, b0):
                    t, b, n = at
                    w.done(pe, "ht", n)
                    w.freed(pe, "mt", n, 1)
                    pe.matmul(m[:, 0:P], k.wm1a[:, :], HT[b][:, 0, :], start=True, stop=False)
                    pe.matmul(m[:, 0:P], k.wm1b[:, :], HT[b][:, 1, :], start=False, stop=True).then_inc(w["m"], 1)
                if at := s.at(2, i, b0):
                    t, b, n = at
                    p.spread_keys(pe, [krow, krow], b, n, 1)
                    w.landed(pe, "s_in", b, n)
                    w.landed(pe, "d_in", b, n)
                    w.freed(pe, "ht", n, 1)
                    for half, rows in enumerate((XS[b], XD[b])):
                        last = pe.transpose(hT[:, half * P:(half + 1) * P], rows[:, C:2 * C], k.ident[:, :])
                    last.then_inc(w["hT"], 1)

            s.each(pe, step, 7)


def edges_fifth(nc, k):
    with Phase(nc) as ctx:
        L = LONG
        sb = lambda name, shape: [ctx.enter_context(nc.sbuf_tensor(f"e5_{name}{b}", shape, F32)) for b in range(L)]
        p = EdgePass(nc, ctx, "e5", k, 0, Norm.STEPS + "nm h hw attn msg st r", "r_out", "s_in d_in", L)
        w = p.w
        ln = Norm(nc, ctx, "e5", w, 2, p.turn["dve"], "h")
        XX, H = sb("XX", [P, 2, C]), sb("H", [P, 2, C])
        HW, HH, MSG, ST, RES = (sb(n, [P, C]) for n in ("HW", "HH", "MSG", "ST", "RES"))
        nm, attn = sb("nm", [P, 2]), sb("attn", [P, 1])
        krow, tot = ([ctx.enter_context(nc.psum_tensor(f"e5_{n}{b}", [P, 512], F32)) for b in range(2)]
                     for n in ("krow", "tot"))
        block = ctx.enter_context(nc.Block())
        each = lambda eng, step, lag: each_step(eng, step, lag, T, L)

        def stage(lag, i, b0):
            return (i - lag, (b0 - lag) % L, i - lag + 1) if live(i - lag) else None

        @block.sync
        def _(sp):
            w.credit(sp)

            def step(i, b0):
                at = stage(6, i, b0)
                if at:
                    t, b, n = at
                    w.done(sp, "r", n)
                    sp.dma_start(tile_rows(k.slot_g, t), RES[b][:, :]).then_inc(w.moves["r_out"][b], 16)

            each(sp, step, 6)
            w.drain(sp, "r_out", T)

        @block.gpsimd
        def _(pool):
            def step(i, b0):
                at = stage(0, i, b0)
                if at:
                    t, b, n = at
                    p.load_ids(pool, t, b, n, ("s_in", "d_in"))
                    w.freed(pool, "r", n)
                    p.gather(pool, XX[b][:, 0, :], k.out, 0, b, n, "s_in")
                    p.gather(pool, XX[b][:, 1, :], k.out, 1, b, n, "d_in")

            each(pool, step, 0)

        @block.vector
        def _(dve):
            p.start(dve)

            def step(i, b0):
                at = stage(6, i, b0)
                if at:
                    t, b, n = at
                    w.done(dve, "totsb", n)
                    w.freed(dve, "r", n)
                    dve.tensor_tensor(ST[b][:, :], p.totsb[b][:, :], k.spread[:, 4, :], ALU.mult).then_inc(w["st"], 1)
                    w.done(dve, "st", n)
                    w.drained(dve, "r_out", b, n)
                    dve.tensor_tensor(RES[b][:, :], ST[b][:, :], XX[b][:, 1, :], ALU.add).then_inc(w["r"], 1)
                at = stage(4, i, b0)
                if at:
                    t, b, n = at
                    w.done(dve, "h", n)
                    w.freed(dve, "attn", n)
                    dve.tensor_tensor(HW[b][:, :], H[b][:, 1, :], k.spread[:, 5, :], ALU.mult).then_inc(w["hw"], 1)
                    p.masks(dve, krow, b, n)
                    w.done(dve, "hw", n)
                    w.freed(dve, "msg", n)
                    dve.tensor_tensor_reduce(HH[b][:, :], HW[b][:, :], H[b][:, 0, :], 1.0, 0.0, ALU.mult, ALU.add,
                                             attn[b][:, :]).then_inc(w["attn"], 1)
                    w.done(dve, "attn", n)
                    w.freed(dve, "tot", n)
                    dve.tensor_scalar(MSG[b][:, :], H[b][:, 0, :], attn[b][:, :], None, ALU.mult).then_inc(w["msg"], 1)
                at = stage(3, i, b0)
                if at:
                    t, b, n = at
                    w.done(dve, "ln_rs", n)
                    w.freed(dve, "h", n)
                    dve.scalar_tensor_tensor(nm[b][:, :], ln.mv[b][:, :, 0], -1.0, ln.rs[b][:, :], ALU.mult, ALU.mult)\
                        .then_inc(w["nm"], 1)
                    p.load_keys(dve, t, b, n)
                at = stage(2, i, b0)
                if at:
                    t, b, n = at
                    w.landed(dve, "s_in", b, n)
                    w.landed(dve, "d_in", b, n)
                    w.freed(dve, "nm", n)
                    ln.stats(dve, XX[b], b, n)
                    ln.inverse(dve, b, n)

            each(dve, step, 6)

        @block.scalar
        def _(act):
            def step(i, b0):
                at = stage(5, i, b0)
                if at:
                    t, b, n = at
                    w.freed(act, "st", n)
                    p.keep_sums(act, tot, b, n)
                at = stage(3, i, b0)
                if at:
                    t, b, n = at
                    w.done(act, "nm", n)
                    w.freed(act, "msg", n)
                    for s in range(2):
                        last = act.activation(H[b][:, s, :], XX[b][:, s, :], ACT.Relu, bias=nm[b][:, s:s + 1],
                                              scale=ln.rs[b][:, s:s + 1])
                    last.then_inc(w["h"], 1)
                at = stage(2, i, b0)
                if at:
                    t, b, n = at
                    ln.root(act, b, n)

            each(act, step, 5)

        @block.tensor
        def _(pe):
            pe.wait_ge(p.zeroed, 1)

            def step(i, b0):
                at = stage(5, i, b0)
                if at:
                    t, b, n = at
                    w.done(pe, "msg", n)
                    p.sums(pe, tot, [MSG[b][:, :]], b, n)
                at = stage(3, i, b0)
                if at:
                    t, b, n = at
                    p.spread_keys(pe, krow, b, n)

            each(pe, step, 5)


def last_rows(nc, k):
    with Phase(nc) as ctx:
        L = LONG
        p = EdgePass(nc, ctx, "e6", k, 0, "", "r_in", "x_out", L)
        w = p.w
        RES = [ctx.enter_context(nc.sbuf_tensor(f"e6_RES{b}", [P, C], F32)) for b in range(L)]
        block = ctx.enter_context(nc.Block())

        @block.sync
        def _(sp):
            w.credit(sp)

            def step(i, b):
                if live(i):
                    w.drained(sp, "x_out", b % L, i + 1)
                    sp.dma_start(RES[b % L][:, :], tile_rows(k.slot_g, i)).then_inc(w.moves["r_in"][b % L], 16)

            each_step(sp, step, 0, T, L)

        @block.gpsimd
        def _(pool):
            def step(i, b):
                if live(i):
                    w.landed(pool, "r_in", b % L, i + 1)
                    p.scatter(pool, k.out, RES[b % L][:, :], i, b % L, i + 1, "x_out")

            each_step(pool, step, 0, T, L)
            w.drain(pool, "x_out", T)


class Kept:
    pass


def program(nc, x, src, dst, edge_type, weights, out):
    k = Kept()
    k.x, k.src, k.dst, k.edge_type, k.out = x, src, dst, edge_type, out
    k.L0_W1, k.L0_b1, k.L0_W2, k.L0_b2 = (weights["L0_" + n] for n in ("W1", "b1", "W2", "b2"))
    k.L1_W, k.L1_root, k.L1_bias, k.L1_gamma, k.L1_beta = (
        weights["L1_" + n] for n in ("W", "root", "bias", "gamma", "beta"))
    k.L2_wm1, k.L2_bm1, k.L2_wm2, k.L2_bm2 = (weights["L2_" + n] for n in ("wm1", "bm1", "wm2", "bm2"))
    k.L2_wu1, k.L2_bu1, k.L2_wu2, k.L2_bu2 = (weights["L2_" + n] for n in ("wu1", "bu1", "wu2", "bu2"))
    k.L2_gamma, k.L2_beta, k.L3_W2, k.L3_W3 = (weights[n] for n in ("L2_gamma", "L2_beta", "L3_W2", "L3_W3"))
    with ExitStack() as ctx:
        sb = lambda name, shape, dt=F32: ctx.enter_context(nc.sbuf_tensor(name, shape, dt))
        k.edge_i = sb("edge_i", [P, 3, T], I32)
        k.iota = sb("iota", [P, HI])
        k.iota_b = sb("iota_b", [P, HI], BF16)
        k.ident_b = sb("ident_b", [P, P], BF16)
        k.part = sb("part", [P, 1])
        k.ident, k.before, k.shift, k.unshift, k.wrap = (sb(n, [P, P]) for n in ("ident", "before", "shift", "unshift", "wrap"))
        k.first, k.last = sb("first", [P, 1]), sb("last", [P, 1])
        k.ones = sb("ones", [P, HI])
        k.w1, k.w2, k.root = (sb(n, [C, C]) for n in ("w1", "w2", "root"))
        k.b1_col = sb("b1_col", [C, 1])
        k.indeg = sb("indeg", [P, HI])
        k.sorted = sb("sorted", [P, 2, 2, T])
        k.key = sb("key", [P, 2, T + 2])
        k.index = sb("index", [P, 2, T, 3], I32)
        k.is_last = sb("is_last", [P, T])
        k.dinv = sb("dinv", [P, T])
        k.rel_weight = sb("rel_weight", [P, T, R])
        k.flat = nc.dram_tensor("flat_dram", (2, P * T), F32, kind="Internal").ap()
        k.minus_half = sb("minus_half", [P, HI])
        k.node_dinv, k.whole = sb("node_dinv", [P, HI]), sb("whole", [P, HI])
        k.vectors = [k.L0_b1, k.L0_b2, k.L1_bias, k.L2_bm1, k.L2_bm2, k.L2_bu1, k.L2_bu2]
        k.ones3, k.rows3 = sb("ones3", [3, P], BF16), sb("rows3", [3, len(k.vectors), C], BF16)
        k.zero_row = sb("zero_row", [1, P])
        k.w_rel = sb("w_rel", [C, R, C])
        k.stats_edges = sb("stats_edges", [C, 2])
        k.stats_whole = sb("stats_whole", [C, 2])
        k.spread = sb("spread", [P, 6, C])
        k.bm1_col, k.bu1_col = sb("bm1_col", [C, 1]), sb("bu1_col", [C, 1])
        k.wm1a, k.wm1b, k.wu1a, k.wu2, k.wc, k.cb = (sb(n, [C, C]) for n in ("wm1a", "wm1b", "wu1a", "wu2", "wc", "cb"))
        table = lambda name: nc.dram_tensor(name, (N, C), F32, kind="Internal").ap()
        k.H0, k.G1, k.X1, k.O = (table(n) for n in ("h0_dram", "g1_dram", "x1_dram", "o_dram"))
        k.XH = nc.dram_tensor("xh_dram", (N, 2 * C), F32, kind="Internal").ap()
        slots = lambda name: nc.dram_tensor(name, (T * P, C), F32, kind="Internal").ap()
        k.slot_x, k.slot_g, k.slot_x2 = (slots(n) for n in ("slot_x_dram", "slot_g_dram", "slot_x2_dram"))
        constants(nc, k)
        sort_edges(nc, k)
        edge_tables(nc, k)
        split_rows(nc, k)
        nodes_first(nc, k)
        edges_first(nc, k)
        edges_second(nc, k)
        edges_third(nc, k)
        row_tables(nc, k)
        nodes_second(nc, k)
        edges_fourth(nc, k)
        edges_fifth(nc, k)
        last_rows(nc, k)


def kernel(**inputs):
    import numpy as np
    import concourse.bacc as bacc
    from concourse.bass_utils import run_bass_kernel_spmd

    nc = bacc.Bacc("TRN2", target_bir_lowering=False, num_devices=1)
    arrays = {"in_" + name: np.ascontiguousarray(array) for name, array in inputs.items()}
    given = {name: nc.dram_tensor("in_" + name, array.shape, mybir.dt.from_np(array.dtype), kind="ExternalInput").ap()
             for name, array in ((n[3:], a) for n, a in arrays.items())}
    out = nc.dram_tensor("out", (N, C), F32, kind="ExternalOutput").ap()
    weights = {name.replace("_gnn_", "_"): ap for name, ap in given.items() if name.startswith("L")}
    program(nc, given["x"], given["src"], given["dst"], given["edge_type_8"], weights, out)
    run = run_bass_kernel_spmd(nc, [arrays], core_ids=[0])
    return run.results[0]["out"]
```

```python
from contextlib import ExitStack

import concourse.bass as bass
from concourse import mybir

P = 128
F32 = mybir.dt.float32
BF16 = mybir.dt.bfloat16
I32 = mybir.dt.int32
ALU = mybir.AluOpType
ACT = mybir.ActivationFunctionType
AX = mybir.AxisListType

C = 128
N = 50000
E = 25000
R = 8
EPS = 1e-5
J = 4
GROUP = P * J
NG = -(-N // GROUP)
FULL = N // GROUP
TAIL = (N - FULL * GROUP) // J
HI = NG * J
MID = HI // 2
T = -(-E // P)
ETAIL = E - (P - 1) * T
PAD = NG * GROUP - 1
SKIP = 1 << 20
assert N % J == 0 and T % 2 == 0 and 0 < ETAIL <= T and PAD >= N


class Phase:

    def __init__(self, nc):
        self.nc, self.stack, self.semaphores = nc, ExitStack(), []

    def __enter__(self):
        self.stack.__enter__()
        return self

    def enter_context(self, what):
        return self.stack.enter_context(what)

    def semaphore(self, name):
        self.semaphores.append(self.nc.alloc_semaphore(name))
        return self.semaphores[-1]

    def __exit__(self, *error):
        self.stack.__exit__(*error)
        if error[0] is None:
            self.nc.clear_and_free_semaphores(self.semaphores)
            with self.nc.Block():
                pass


def constants(nc, k):
    with Phase(nc) as ctx:
        raw = ctx.enter_context(nc.sbuf_tensor("raw_iota", [P, HI], I32))
        part = ctx.enter_context(nc.sbuf_tensor("raw_part", [P, 1], I32))
        iota_ready = ctx.semaphore("const_iota_ready")
        chain = ctx.semaphore("const_chain")
        pads_set = ctx.semaphore("const_pads_set")
        edges_in = ctx.semaphore("const_edges_in")
        weights_in = ctx.semaphore("const_weights_in")
        block = ctx.enter_context(nc.Block())

        @block.gpsimd
        def _(pool):
            pool.iota(raw[:, :], pattern=[[1, HI]], base=0, channel_multiplier=0).then_inc(iota_ready, 1)
            pool.iota(part[:, :], pattern=[[0, 1]], base=0, channel_multiplier=1).then_inc(iota_ready, 1)

        @block.vector
        def _(dve):
            dve.memset(k.edge_i[:, :, :], PAD).then_inc(pads_set, 1)
            dve.memset(k.ones[:, :], 1.0)
            dve.memset(k.zero_row[:, :], 0.0)
            dve.wait_ge(iota_ready, 2)
            dve.tensor_copy(k.iota[:, :], raw[:, :]).then_inc(chain, 1)
            dve.tensor_copy(k.part[:, :], part[:, :]).then_inc(chain, 1)
            dve.wait_ge(chain, 2)
            dve.tensor_scalar(k.ident[:, :], k.iota[:, 0:P], k.part[:, :], None, ALU.is_equal).then_inc(chain, 1)
            dve.tensor_scalar(k.before[:, :], k.iota[:, 0:P], k.part[:, :], None, ALU.is_gt).then_inc(chain, 1)
            dve.tensor_scalar(k.shift[:, :], k.iota[:, 0:P], 1.0, k.part[:, :], ALU.add, ALU.is_equal).then_inc(chain, 1)
            dve.tensor_scalar(k.unshift[:, :], k.iota[:, 0:P], -1.0, k.part[:, :], ALU.add, ALU.is_equal).then_inc(chain, 1)
            dve.tensor_scalar(k.first[:, :], k.part[:, :], 0.0, None, ALU.is_equal).then_inc(chain, 1)
            dve.tensor_scalar(k.last[:, :], k.part[:, :], P - 1.0, None, ALU.is_equal).then_inc(chain, 1)
            dve.tensor_scalar(k.ident_b[:, :], k.iota[:, 0:P], k.part[:, :], None, ALU.is_equal)
            dve.tensor_scalar(k.iota_b[:, :], k.iota[:, :], -float(MID), None, ALU.add).then_inc(chain, 1)
            dve.wait_ge(chain, 9)
            dve.tensor_scalar(k.wrap[:, :], k.iota[:, 0:P], P - 1.0, k.first[:, :], ALU.is_equal, ALU.mult).then_inc(chain, 1)
            dve.wait_ge(chain, 10)

        @block.sync
        def _(sp):
            sp.dma_start(k.w1[:, :], k.L0_W1).then_inc(weights_in, 16)
            sp.dma_start(k.w2[:, :], k.L0_W2).then_inc(weights_in, 16)
            sp.dma_start(k.w_rel[:, :, :], k.L1_W.rearrange("r i o -> i r o")).then_inc(weights_in, 16)
            sp.dma_start(k.root[:, :], k.L1_root).then_inc(weights_in, 16)
            sp.dma_start(k.b1_col[:, :], k.L0_b1.rearrange("(c a) -> c a", a=1)).then_inc(weights_in, 16)
            sp.wait_ge(pads_set, 1)
            lists = [k.dst, k.src, k.edge_type]
            for r, flat in enumerate(lists):
                sp.dma_start(k.edge_i[0:P - 1, r, :],
                             flat[0:(P - 1) * T].rearrange("(p t) -> p t", t=T)).then_inc(edges_in, 16)
                sp.dma_start(k.edge_i[P - 1:P, r, 0:ETAIL],
                             flat[(P - 1) * T:E].rearrange("(a t) -> a t", a=1)).then_inc(edges_in, 16)
            sp.wait_ge(edges_in, 16 * 2 * len(lists))
            sp.wait_ge(weights_in, 16 * 5)


def sort_edges(nc, k):
    with Phase(nc) as ctx:
        sb = lambda name, shape, dt=F32: ctx.enter_context(nc.sbuf_tensor("so_" + name, shape, dt))
        ps = lambda name: ctx.enter_context(nc.psum_tensor("so_" + name, [P, 512], F32))
        sem = lambda name: ctx.semaphore("so_" + name)
        node = k.edge_i
        part_i, hi_i, tmp_i = (sb(n, [P, 2, T], I32) for n in ("part_i", "hi_i", "tmp_i"))
        lo, hi, node_f = (sb(n, [P, 2, T]) for n in ("lo", "hi", "node_f"))
        numbers = sb("numbers", [P, T, 2, 2])
        H = T // 2
        rows_back = sb("rows_back", [H, 2, 2, P, 2])
        lo_b = sb("lo_b", [P, 2, T], BF16)
        type_i = sb("type_i", [P, T], I32)
        type_f = sb("type_f", [P, T])
        place = [sb(f"place{q}", [P, 1], I32) for q in range(4)]
        travels = [sb(f"travels{q}", [P, 2]) for q in range(4)]
        one_lo = sb("one_lo", [P, 2, 2, P], BF16)
        one_hi = sb("one_hi", [P, 2, 2, HI], BF16)
        lo_t = sb("lo_t", [P, 2, 2, P])
        same_lo = sb("same_lo", [P, 2, 2, P], BF16)
        base = sb("base", [P, 2, HI])
        hist = sb("hist", [P, 2, HI])
        picked = sb("picked", [P, 2, HI])
        got = sb("got", [P, 2, 1])
        rows = sb("rows", [P, 2, 1])
        starts = sb("starts", [P, 2, 1])
        zero_b = sb("zero_b", [P, HI], BF16)
        warm = sb("warm", [P, 1])
        run_ps = [ps("run0"), ps("run1")]
        pick_ps = [ps("pick0"), ps("pick1")]
        row_ps = [ps("row0"), ps("row1")]
        sum_ps = ps("sum")
        chain = sem("chain")
        digits = sem("digits")
        zeroed = sem("zeroed")
        ones_ready, ones_used = sem("ones_ready"), sem("ones_used")
        rows_ready, starts_ready, base_ready, base_in = (sem(n) for n in ("rows_ready", "starts_ready", "base_ready", "base_in"))
        row_ready, masks_ready, run_copied, run_updated = (sem(n) for n in ("row_ready", "masks_ready", "run_copied", "run_updated"))
        pick_ready, pick_read, got_free, turn = (sem(n) for n in ("pick_ready", "pick_read", "got_free", "turn"))
        put_ready, turned_back = sem("put_ready"), sem("turned_back")
        put_out = [sem(f"put_out{q}") for q in range(4)]
        all_put, back_in = sem("all_put"), sem("back_in")
        block = ctx.enter_context(nc.Block())

        def one_hots(dve, t, c, o):
            dve.tensor_scalar(one_lo[:, c, o, :], k.iota_b[:, MID:MID + P], lo[:, o, bass.ds(t, 1)], None, ALU.is_equal)
            return dve.tensor_scalar(one_hi[:, c, o, :], k.iota_b[:, :], hi[:, o, bass.ds(t, 1)], None, ALU.is_equal)

        @block.vector
        def _(dve):
            links = [0]

            def link(ins):
                links[0] += 1
                ins.then_inc(chain, 1)
                dve.wait_ge(chain, links[0])

            dve.memset(zero_b[:, :], 0.0).then_inc(zeroed, 1)
            both = node[:, 0:2, :]
            dve.tensor_scalar(part_i[:, :, :], both, 2, 127, ALU.logical_shift_right, ALU.bitwise_and).then_inc(digits, 1)
            dve.tensor_scalar(hi_i[:, :, :], both, 9, 2, ALU.logical_shift_right, ALU.logical_shift_left).then_inc(digits, 1)
            dve.tensor_scalar(tmp_i[:, :, :], both, 3, None, ALU.bitwise_and).then_inc(digits, 1)
            dve.tensor_scalar(type_i[:, :], node[:, 2, :], R - 1, None, ALU.bitwise_and).then_inc(digits, 1)
            dve.wait_ge(digits, 4)
            dve.tensor_tensor(hi[:, :, :], hi_i[:, :, :], tmp_i[:, :, :], ALU.add).then_inc(digits, 1)
            dve.tensor_copy(lo[:, :, :], part_i[:, :, :]).then_inc(digits, 1)
            dve.wait_ge(digits, 5)
            dve.tensor_scalar(hi[:, :, :], hi[:, :, :], -float(MID), None, ALU.add)
            dve.tensor_copy(type_f[:, :], type_i[:, :]).then_inc(digits, 1)
            dve.tensor_copy(node_f[:, :, :], both).then_inc(digits, 1)
            dve.tensor_copy(lo_b[:, :, :], part_i[:, :, :]).then_inc(digits, 1)
            dve.wait_ge(digits, 9)
            for o in range(2):
                dve.scalar_tensor_tensor(numbers[:, :, o, 0], node_f[:, o, :], float(R), type_f[:, :],
                                         ALU.mult, ALU.add).then_inc(digits, 1)
                dve.tensor_copy(numbers[:, :, o, 1], node_f[:, 1 - o, :]).then_inc(digits, 1)
            with dve.Fori(0, T // 2) as r:
                for c in range(2):
                    for o in range(2):
                        dve.wait_ge(ones_used, r * 4 + c * 2 + o + 1)
                        one_hots(dve, r * 2 + c, c, o).then_inc(ones_ready, 1)
            dve.wait_ge(ones_used, 2 * T + 4)
            for o in range(2):
                dve.tensor_copy(hist[:, o, :], run_ps[o][:, 0:HI]).then_inc(base_ready, 1)
            dve.wait_ge(base_ready, 2)
            dve.tensor_copy(k.indeg[:, :], hist[:, 0, :])
            for o in range(2):
                dve.tensor_reduce(rows[:, o, :], hist[:, o, :], AX.X, ALU.add).then_inc(rows_ready, 1)
            dve.wait_ge(starts_ready, 1)
            for o in range(2):
                link(dve.tensor_copy(starts[:, o, :], sum_ps[:, o:o + 1]))
                link(dve.tensor_tensor_scan(picked[:, o, :], k.ones[:, 0:HI], hist[:, o, :], starts[:, o, :],
                                            ALU.mult, ALU.add))
                dve.tensor_tensor(base[:, o, :], picked[:, o, :], hist[:, o, :], ALU.subtract).then_inc(base_in, 1)
            dve.wait_ge(base_in, 2)
            dve.sem_inc(pick_read, 4)

            def masks(t, c):
                for o in range(2):
                    n = t * 2 + o + 1
                    dve.wait_ge(run_updated, n)
                    dve.wait_ge(pick_read, n)
                    one_hots(dve, t, c, o)
                    dve.wait_ge(row_ready, n)
                    dve.tensor_scalar(lo_t[:, c, o, :], row_ps[o][:, 0:P], k.part[:, :], None, ALU.is_equal)
                    dve.scalar_tensor_tensor(same_lo[:, c, o, :], row_ps[o][:, 0:P], lo[:, o, bass.ds(t, 1)],
                                             k.before[:, :], ALU.is_equal, ALU.mult).then_inc(masks_ready, 1)

            def pick(t, c):
                for o in range(2):
                    n = t * 2 + o + 1
                    dve.wait_ge(pick_ready, n)
                    dve.wait_ge(pick_read, n + 2)
                    dve.wait_ge(got_free, n)
                    dve.tensor_tensor_reduce(picked[:, o, :], pick_ps[o][:, 0:HI], one_hi[:, c, o, :], 1.0, 0.0,
                                             ALU.mult, ALU.add, got[:, o, :]).then_inc(pick_read, 1)

            masks(0, 0)
            with dve.Fori(0, T // 2 - 1) as r:
                masks(r * 2 + 1, 1)
                pick(r * 2, 0)
                masks(r * 2 + 2, 0)
                pick(r * 2 + 1, 1)
            masks(T - 1, 1)
            pick(T - 2, 0)
            pick(T - 1, 1)
            dve.wait_ge(turned_back, 1)
            for o in range(2):
                for w in range(2):
                    link(dve.tensor_copy(k.sorted[:, o, w, :], row_ps[o][:, w * T:(w + 1) * T]))

        @block.tensor
        def _(pe):
            pe.wait_ge(zeroed, 1)
            pe.sem_inc(ones_used, 4)
            for o in range(2):
                pe.matmul(run_ps[o][:, 0:HI], zero_b[:, 0:P], zero_b[:, :], start=True, stop=True, skip_group_check=True)
            with pe.Fori(0, T // 2) as r:
                for c in range(2):
                    for o in range(2):
                        pe.wait_ge(ones_ready, r * 4 + c * 2 + o + 1)
                        pe.matmul(run_ps[o][:, 0:HI], one_lo[:, c, o, :], one_hi[:, c, o, :], start=False, stop=True,
                                  skip_group_check=True).then_inc(ones_used, 1)
            pe.wait_ge(rows_ready, 2)
            pe.matmul(sum_ps[:, 0:2], k.before[:, :], rows[:, :, :].rearrange("p a b -> p (a b)"),
                      start=True, stop=True).then_inc(starts_ready, 1)
            pe.wait_ge(base_in, 2)
            pe.sem_inc(masks_ready, 2)
            pe.sem_inc(run_updated, 2)
            for o in range(2):
                pe.matmul(run_ps[o][:, 0:HI], k.ident[:, :], base[:, o, :], start=True, stop=True,
                          skip_group_check=True).then_inc(run_updated, 1)

            def spread(t):
                for o in range(2):
                    pe.wait_ge(masks_ready, t * 2 + o + 1)
                    pe.matmul(row_ps[o][:, 0:P], lo_b[:, o, bass.ds(t, 1)].to_broadcast([P, P]), k.ident_b[:, :],
                              start=True, stop=True).then_inc(row_ready, 1)

            def pick(t, c):
                for o in range(2):
                    n = t * 2 + o + 1
                    pe.wait_ge(masks_ready, n + 2)
                    pe.wait_ge(run_copied, n)
                    pe.wait_ge(pick_read, n + 2)
                    pe.matmul(pick_ps[o][:, 0:HI], lo_t[:, c, o, :], base[:, o, :], start=True, stop=False,
                              skip_group_check=True)
                    pe.matmul(pick_ps[o][:, 0:HI], same_lo[:, c, o, :], one_hi[:, c, o, :], start=False, stop=True,
                              skip_group_check=True).then_inc(pick_ready, 1)
                    pe.matmul(run_ps[o][:, 0:HI], one_lo[:, c, o, :], one_hi[:, c, o, :], start=False, stop=True,
                              skip_group_check=True).then_inc(run_updated, 1)

            spread(0)
            with pe.Fori(0, T // 2 - 1) as r:
                for c in range(2):
                    spread(r * 2 + c + 1)
                    pick(r * 2 + c, c)
            spread(T - 1)
            pick(T - 2, 0)
            pick(T - 1, 1)
            pe.wait_ge(masks_ready, 2 * T + 2)
            pe.wait_ge(back_in, 16 * 4)
            for o in range(2):
                for w in range(2):
                    for half in range(2):
                        at = w * T + half * H
                        last = pe.transpose(row_ps[o][:, at:at + H], rows_back[:, o, half, :, w], k.ident[0:H, 0:H])
            last.then_inc(turned_back, 1)

        @block.sync
        def _(sp):
            sp.wait_ge(all_put, 1)
            for o in range(2):
                for half in range(2):
                    sp.dma_start(rows_back[:, o, half, :, :], k.pairs[o][half * H * P:(half + 1) * H * P, :]
                                 .rearrange("(r c) w -> r c w", c=P)).then_inc(back_in, 16)

        @block.scalar
        def _(act):
            act.wait_ge(zeroed, 1)
            act.activation(warm[:, :], zero_b[:, 0:1], ACT.Relu)
            with act.Fori(0, T) as t:
                for o in range(2):
                    n = t * 2 + o + 1
                    act.wait_ge(run_updated, n + 2)
                    act.copy(base[:, o, :], run_ps[o][:, 0:HI]).then_inc(run_copied, 1)

        @block.gpsimd
        def _(pool):
            pool.sem_inc(got_free, 2)
            pool.wait_ge(digits, 13)

            def put(r, first=False):
                for c in range(2):
                    for o in range(2):
                        q, t = c * 2 + o, r * 2 + c
                        n = t * 2 + o + 1
                        pool.wait_ge(pick_read, n + 4)
                        if not first:
                            pool.wait_ge(put_out[q], r * 16)
                        pool.sem_inc(turn, 1)
                        pool.tensor_copy(place[q][:, :], got[:, o, :]).then_inc(got_free, 1)
                        pool.tensor_copy(travels[q][:, :], numbers[:, bass.ds(t, 1), o, :].rearrange("p a w -> p (a w)"))\
                            .then_inc(put_ready, 1)
                        pool.wait_ge(put_ready, n)
                        pool.wait_ge(got_free, n + 2)
                        pool.sem_inc(turn, 1)
                        pool.indirect_dma_start(k.pairs[o], bass.IndirectOffsetOnAxis(ap=place[q][:, 0:1], axis=0),
                                                travels[q][:, :], None).then_inc(put_out[q], 16)

            put(0, first=True)
            with pool.Fori(1, T // 2) as r:
                put(r)
            for q in range(4):
                pool.wait_ge(put_out[q], 16 * (T // 2))
            pool.sem_inc(all_put, 1)


def edge_tables(nc, k):
    with Phase(nc) as ctx:
        sb = lambda name, shape, dt=F32: ctx.enter_context(nc.sbuf_tensor("ta_" + name, shape, dt))
        ps = lambda name: ctx.enter_context(nc.psum_tensor("ta_" + name, [P, 512], F32))
        sem = lambda name: ctx.semaphore("ta_" + name)
        H = T // 2
        pay_i, key_i, type_i = (sb(n, [P, 2, T], I32) for n in ("pay_i", "key_i", "type_i"))
        keys = sb("keys", [P, 2, T + 1])
        typ = sb("typ", [P, T])
        nxt = sb("nxt", [P, 2, T])
        lasts, real, real2, idx = (sb(n, [P, 2, T]) for n in ("lasts", "real", "real2", "idx"))
        turned = sb("turned", [H, 2, 2, P])
        flat = sb("flat", [P, 2, T])
        first_f, last_f = sb("first_f", [P, T]), sb("last_f", [P, T])
        edge_key = sb("edge_key", [P, 2])
        of_r = sb("of_r", [P, R, T])
        upto, begin, count = (sb(n, [P, R, T]) for n in ("upto", "begin", "count"))
        hold = sb("hold", [P, R, T])
        per = sb("per", [P, R])
        carry, carry_t = sb("carry", [P, R]), sb("carry_t", [R, P])
        scanned = sb("scanned", [R, P + 1])
        mine = sb("mine", [P, T])
        weight = sb("weight", [P, 2, T])
        w_rows = sb("w_rows", [H, 2, 2, P])
        a_ps, b_ps, c_ps = ps("a"), ps("b"), ps("c")
        deg_inv = sb("deg_inv", [P, T])
        chain, deg_ready = sem("chain"), sem("deg_ready")
        nxt_ready, nxt_done = sem("nxt_ready"), sem("nxt_done")
        turn_asked, turn_ready, rows_ready = sem("turn_asked"), sem("turn_ready"), sem("rows_ready")
        flat_out, flat_in = sem("flat_out"), sem("flat_in")
        pe_asked, pe_done = sem("pe_asked"), sem("pe_done")
        w_ready, w_out, w_in, w_turned = (sem(n) for n in ("w_ready", "w_out", "w_in", "w_turned"))
        key_asked, key_done = sem("key_asked"), sem("key_done")
        exponent = sem("exponent")
        block = ctx.enter_context(nc.Block())
        flat_dram = k.flat.rearrange("w (r c) -> r w c", c=P)
        flat_rows = k.flat.rearrange("w (p t) -> p w t", t=T)

        @block.vector
        def _(dve):
            links = [0]

            def link(ins):
                links[0] += 1
                ins.then_inc(chain, 1)
                dve.wait_ge(chain, links[0])

            link(dve.memset(keys[:, :, :], -1.0))
            link(dve.memset(k.key[:, :, :], -1.0))
            link(dve.tensor_copy(pay_i[:, :, :], k.sorted[:, :, 0, :]))
            link(dve.tensor_scalar(key_i[:, :, :], pay_i[:, :, :], 3, None, ALU.logical_shift_right))
            link(dve.tensor_scalar(type_i[:, :, :], pay_i[:, :, :], R - 1, None, ALU.bitwise_and))
            link(dve.tensor_copy(keys[:, :, 0:T], key_i[:, :, :]))
            link(dve.tensor_copy(k.key[:, :, 1:T + 1], key_i[:, :, :]))
            dve.tensor_copy(typ[:, :], type_i[:, 0, :]).then_inc(turn_asked, 1)
            dve.wait_ge(turn_asked, 1)
            dve.sem_inc(nxt_ready, 1)
            dve.wait_ge(turn_ready, 1)
            dve.tensor_copy(turned[:, :, :, :].rearrange("p a b c -> p (a b c)"), a_ps[0:H, :]).then_inc(rows_ready, 1)
            dve.wait_ge(nxt_done, 1)
            for o in range(2):
                link(dve.tensor_copy(nxt[:, o, :], b_ps[:, o * T:(o + 1) * T]))
            link(dve.tensor_tensor(lasts[:, :, :], nxt[:, :, :], keys[:, :, 0:T], ALU.not_equal))
            link(dve.tensor_scalar(real[:, :, :], keys[:, :, 0:T], N - 0.5, None, ALU.is_lt))
            link(dve.tensor_tensor(lasts[:, :, :], lasts[:, :, :], real[:, :, :], ALU.mult))
            link(dve.tensor_copy(k.is_last[:, :], lasts[:, 0, :]))
            link(dve.tensor_scalar(idx[:, :, :], lasts[:, :, :], -float(SKIP), float(SKIP), ALU.mult, ALU.add))
            link(dve.tensor_tensor(idx[:, :, :], idx[:, :, :], keys[:, :, 0:T], ALU.add))
            for o in range(2):
                link(dve.tensor_copy(k.index[:, o, :, 2], idx[:, o, :]))
            link(dve.tensor_tensor(idx[:, :, :], keys[:, :, 0:T], real[:, :, :], ALU.mult))
            for o in range(2):
                link(dve.tensor_copy(k.index[:, o, :, 1 - o], idx[:, o, :]))
            link(dve.tensor_scalar(real2[:, :, :], k.sorted[:, :, 1, :], N - 0.5, None, ALU.is_lt))
            link(dve.tensor_tensor(idx[:, :, :], k.sorted[:, :, 1, :], real2[:, :, :], ALU.mult))
            for o in range(2):
                link(dve.tensor_copy(k.index[:, o, :, o], idx[:, o, :]))
            dve.wait_ge(flat_in, 16)
            link(dve.memset(edge_key[:, :], 0.0))
            dve.tensor_copy(edge_key[:, 0:1], flat[:, 0, 0:1])
            dve.tensor_copy(edge_key[:, 1:2], flat[:, 0, T - 1:T]).then_inc(key_asked, 1)
            dve.wait_ge(key_done, 1)
            link(dve.tensor_tensor(first_f[:, 1:T], flat[:, 0, 1:T], flat[:, 0, 0:T - 1], ALU.not_equal))
            link(dve.tensor_copy(carry[:, 0:2], c_ps[:, 0:2]))
            link(dve.tensor_tensor(first_f[:, 0:1], carry[:, 1:2], flat[:, 0, 0:1], ALU.not_equal))
            link(dve.tensor_tensor(last_f[:, 0:T - 1], flat[:, 0, 1:T], flat[:, 0, 0:T - 1], ALU.not_equal))
            link(dve.tensor_tensor(last_f[:, T - 1:T], carry[:, 0:1], flat[:, 0, T - 1:T], ALU.not_equal))
            link(dve.tensor_tensor(first_f[:, 0:1], first_f[:, 0:1], k.first[:, :], ALU.max))
            link(dve.tensor_tensor(last_f[:, T - 1:T], last_f[:, T - 1:T], k.last[:, :], ALU.max))
            for r in range(R):
                link(dve.tensor_scalar(of_r[:, r, :], flat[:, 1, :], float(r), None, ALU.is_equal))
            for r in range(R):
                link(dve.tensor_tensor_scan(upto[:, r, :], k.ones[:, 0:T], of_r[:, r, :], 0.0, ALU.mult, ALU.add))
            dve.tensor_copy(per[:, :], upto[:, :, T - 1]).then_inc(pe_asked, 1)
            dve.wait_ge(pe_done, 1)
            link(dve.tensor_copy(carry[:, :], c_ps[:, 0:R]))
            for r in range(R):
                link(dve.tensor_scalar(upto[:, r, :], upto[:, r, :], carry[:, r:r + 1], None, ALU.add))
            link(dve.tensor_tensor(begin[:, :, :], upto[:, :, :], of_r[:, :, :], ALU.subtract))
            fb = first_f[:, :].rearrange("p (a t) -> p a t", a=1).to_broadcast([P, R, T])
            link(dve.tensor_tensor(hold[:, :, :], begin[:, :, :], fb, ALU.mult))
            for r in range(R):
                link(dve.tensor_tensor_scan(begin[:, r, :], k.ones[:, 0:T], hold[:, r, :], 0.0, ALU.mult, ALU.max))
            dve.tensor_copy(per[:, :], begin[:, :, T - 1]).then_inc(pe_asked, 1)
            dve.wait_ge(pe_done, 2)
            link(dve.memset(scanned[:, :], 0.0))
            link(dve.tensor_copy(carry_t[:, :], c_ps[0:R, 0:P]))
            link(dve.tensor_tensor_scan(scanned[:, 1:P + 1], k.ones[0:R, 0:P], carry_t[:, :], 0.0, ALU.mult, ALU.max))
            dve.sem_inc(pe_asked, 1)
            dve.wait_ge(pe_done, 3)
            link(dve.tensor_copy(carry[:, :], c_ps[:, 0:R]))
            for r in range(R):
                link(dve.tensor_scalar(begin[:, r, :], begin[:, r, :], carry[:, r:r + 1], None, ALU.max))
            lb = last_f[:, :].rearrange("p (a t) -> p a t", a=1).to_broadcast([P, R, T])
            link(dve.tensor_scalar(hold[:, :, :], upto[:, :, :], -1.0, float(P * T), ALU.mult, ALU.add))
            link(dve.tensor_tensor(hold[:, :, :], hold[:, :, :], lb, ALU.mult))
            for r in range(R):
                link(dve.tensor_tensor_scan(count[:, r, ::-1], k.ones[:, 0:T], hold[:, r, ::-1], 0.0, ALU.mult, ALU.max))
            dve.tensor_copy(per[:, :], count[:, :, 0]).then_inc(pe_asked, 1)
            dve.wait_ge(pe_done, 4)
            link(dve.memset(scanned[:, :], 0.0))
            link(dve.tensor_copy(carry_t[:, :], c_ps[0:R, 0:P]))
            link(dve.tensor_tensor_scan(scanned[:, P - 1::-1], k.ones[0:R, 0:P], carry_t[:, ::-1], 0.0,
                                        ALU.mult, ALU.max))
            dve.sem_inc(pe_asked, 1)
            dve.wait_ge(pe_done, 5)
            link(dve.tensor_copy(carry[:, :], c_ps[:, 0:R]))
            for r in range(R):
                link(dve.tensor_scalar(count[:, r, :], count[:, r, :], carry[:, r:r + 1], None, ALU.max))
            link(dve.tensor_tensor(count[:, :, :], count[:, :, :], begin[:, :, :], ALU.add))
            link(dve.tensor_scalar(count[:, :, :], count[:, :, :], -1.0, float(P * T), ALU.mult, ALU.add))
            link(dve.tensor_reduce(mine[:, :], count[:, :, :].rearrange("p r t -> p t r"), AX.X, ALU.add))
            link(dve.tensor_scalar(mine[:, :], mine[:, :], 1.0, None, ALU.add))
            dve.reciprocal(deg_inv[:, :], mine[:, :]).then_inc(deg_ready, 1)
            link(dve.tensor_tensor(hold[:, :, :], count[:, :, :], of_r[:, :, :], ALU.mult))
            dve.wait_ge(w_ready, 1)
            link(dve.tensor_reduce(mine[:, :], hold[:, :, :].rearrange("p r t -> p t r"), AX.X, ALU.add))
            dve.reciprocal(weight[:, 1, :], mine[:, :]).then_inc(w_ready, 1)
            dve.wait_ge(w_turned, 1)
            link(dve.tensor_copy(k.dinv[:, :], a_ps[:, 0:T]))
            link(dve.tensor_copy(mine[:, :], a_ps[:, T:2 * T]))
            for r in range(R):
                link(dve.tensor_scalar(nxt[:, 0, :], typ[:, :], float(r), None, ALU.is_equal))
                link(dve.tensor_tensor(k.rel_weight[:, :, r], nxt[:, 0, :], mine[:, :], ALU.mult))

        @block.gpsimd
        def _(pool):
            pool.memset(k.minus_half[:, :], -0.5).then_inc(exponent, 1)
            pool.wait_ge(exponent, 1)
            pool.tensor_scalar(k.node_dinv[:, :], k.indeg[:, :], 1.0, None, ALU.add).then_inc(exponent, 1)
            pool.tensor_scalar(k.whole[:, :], k.indeg[:, :], 0.5, None, ALU.is_lt).then_inc(exponent, 1)
            pool.wait_ge(exponent, 3)
            pool.tensor_tensor(k.node_dinv[:, :], k.node_dinv[:, :], k.minus_half[:, :], ALU.pow).then_inc(exponent, 1)
            pool.wait_ge(exponent, 4)

        @block.tensor
        def _(pe):
            pe.wait_ge(turn_asked, 1)
            pe.wait_ge(nxt_ready, 1)
            for half in range(2):
                for w, table in enumerate((keys[:, 0, :], typ[:, :])):
                    last = pe.transpose(a_ps[0:H, (w * 2 + half) * P:(w * 2 + half + 1) * P],
                                        table[:, half * H:(half + 1) * H], k.ident[:, :])
            last.then_inc(turn_ready, 1)
            for o in range(2):
                pe.matmul(b_ps[:, o * T:(o + 1) * T], k.shift[:, :], keys[:, o, 0:T], start=True, stop=False)
                last = pe.matmul(b_ps[:, o * T:(o + 1) * T], k.wrap[:, :], keys[:, o, 1:T + 1], start=False, stop=True)
            last.then_inc(nxt_done, 1)
            pe.wait_ge(key_asked, 1)
            pe.matmul(c_ps[:, 0:1], k.shift[:, :], edge_key[:, 0:1], start=True, stop=True)
            pe.matmul(c_ps[:, 1:2], k.unshift[:, :], edge_key[:, 1:2], start=True, stop=True).then_inc(key_done, 1)
            pe.wait_ge(pe_asked, 1)
            pe.matmul(c_ps[:, 0:R], k.before[:, :], per[:, :], start=True, stop=True).then_inc(pe_done, 1)
            pe.wait_ge(pe_asked, 2)
            pe.transpose(c_ps[0:R, 0:P], per[:, :], k.ident[:, :]).then_inc(pe_done, 1)
            pe.wait_ge(pe_asked, 3)
            pe.transpose(c_ps[:, 0:R], scanned[:, 0:P], k.ident[0:R, 0:R]).then_inc(pe_done, 1)
            pe.wait_ge(pe_asked, 4)
            pe.transpose(c_ps[0:R, 0:P], per[:, :], k.ident[:, :]).then_inc(pe_done, 1)
            pe.wait_ge(pe_asked, 5)
            pe.transpose(c_ps[:, 0:R], scanned[:, 1:P + 1], k.ident[0:R, 0:R]).then_inc(pe_done, 1)
            pe.wait_ge(w_in, 32)
            for w in range(2):
                for half in range(2):
                    last = pe.transpose(a_ps[:, w * T + half * H:w * T + (half + 1) * H],
                                        w_rows[:, w, half, :], k.ident[0:H, 0:H])
            last.then_inc(w_turned, 1)

        @block.scalar
        def _(act):
            act.wait_ge(deg_ready, 1)
            act.activation(weight[:, 0, :], deg_inv[:, :], ACT.Sqrt).then_inc(w_ready, 1)

        @block.sync
        def _(sp):
            sp.wait_ge(rows_ready, 1)
            for half in range(2):
                sp.dma_start(flat_dram[half * H:(half + 1) * H], turned[:, :, half, :]).then_inc(flat_out, 16)
            sp.wait_ge(flat_out, 32)
            sp.dma_start(flat[:, :, :], flat_rows).then_inc(flat_in, 16)
            sp.wait_ge(w_ready, 2)
            sp.wait_ge(flat_in, 16)
            sp.dma_start(flat_rows, weight[:, :, :]).then_inc(w_out, 16)
            sp.wait_ge(w_out, 16)
            for half in range(2):
                sp.dma_start(w_rows[:, :, half, :], flat_dram[half * H:(half + 1) * H]).then_inc(w_in, 16)
            sp.wait_ge(w_in, 32)


def split_rows(nc, k):
    with Phase(nc) as ctx:
        sb = lambda name, shape, dt=F32: ctx.enter_context(nc.sbuf_tensor("sp_" + name, shape, dt))
        V = len(k.vectors)
        whole, rest, rest2 = (sb(n, [3, V, C]) for n in ("whole", "rest", "rest2"))
        part = [sb(f"part{i}", [3, V, C], BF16) for i in range(3)]
        sel = sb("sel", [3, 3])
        acc = sb("acc", [3, V, C])
        chain = ctx.semaphore("sp_chain")
        rows_in = ctx.semaphore("sp_rows_in")
        block = ctx.enter_context(nc.Block())

        @block.sync
        def _(sp):
            for v, vector in enumerate(k.vectors):
                for i in range(3):
                    sp.dma_start(whole[i:i + 1, v, :], vector.rearrange("(a c) -> a c", a=1)).then_inc(rows_in, 16)
            sp.wait_ge(rows_in, 16 * 3 * V)

        @block.vector
        def _(dve):
            links = [0]

            def link(ins):
                links[0] += 1
                ins.then_inc(chain, 1)
                dve.wait_ge(chain, links[0])

            link(dve.memset(k.ones3[:, :], 1.0))
            dve.wait_ge(rows_in, 16 * 3 * V)
            link(dve.tensor_copy(part[0][:, :, :], whole[:, :, :]))
            link(dve.tensor_tensor(rest[:, :, :], whole[:, :, :], part[0][:, :, :], ALU.subtract))
            link(dve.tensor_copy(part[1][:, :, :], rest[:, :, :]))
            link(dve.tensor_tensor(rest2[:, :, :], rest[:, :, :], part[1][:, :, :], ALU.subtract))
            link(dve.tensor_copy(part[2][:, :, :], rest2[:, :, :]))
            for i in range(3):
                link(dve.tensor_scalar(sel[:, i:i + 1], k.part[0:3, :], float(i), None, ALU.is_equal))
            link(dve.tensor_scalar(acc[:, :, :], part[0][:, :, :], sel[:, 0:1], None, ALU.mult))
            for i in (1, 2):
                link(dve.scalar_tensor_tensor(acc[:, :, :], part[i][:, :, :], sel[:, i:i + 1], acc[:, :, :],
                                              ALU.mult, ALU.add))
            link(dve.tensor_copy(k.rows3[:, :, :], acc[:, :, :]))


def node_rows(table, g, rows):
    return table[bass.ds(g * GROUP, rows * J), :].rearrange("(p j) c -> p j c", j=J)


class Turns:

    def __init__(self, nc, ctx, prefix, L, steps, moves, soft=""):
        self.L = L
        self.steps = {name: ctx.semaphore(f"{prefix}_{name}") for name in steps.split()}
        self.moves = {name: [ctx.semaphore(f"{prefix}_{name}{b}") for b in range(L)]
                      for name in (moves + " " + soft).split()}
        self.start = {name: 0 if name in soft.split() else 16 for name in self.moves}

    def __getitem__(self, name):
        return self.steps[name]

    def credit(self, eng):
        for step in self.steps.values():
            eng.sem_inc(step, self.L)
        for name, lanes in self.moves.items():
            for lane in lanes:
                if self.start[name]:
                    eng.sem_inc(lane, self.start[name])

    def done(self, eng, name, n):
        eng.wait_ge(self.steps[name], n + self.L)

    def freed(self, eng, name, n, back=0):
        eng.wait_ge(self.steps[name], n + self.L - (back or self.L))

    def landed(self, eng, name, b, n):
        assert not isinstance(n, int) or n > 0
        eng.wait_ge(self.moves[name][b], (n - b - 1) * (16 // self.L) + 16 + self.start[name])

    def drained(self, eng, name, b, n):
        if isinstance(n, int) and n <= self.L and not self.start[name]:
            return
        eng.wait_ge(self.moves[name][b], (n - b - 1) * (16 // self.L) + self.start[name])

    def stored(self, eng, name, b, n, back):
        b, n = (b - back) % self.L, n - back
        eng.wait_ge(self.moves[name][b], (n - b - 1) * (16 // self.L) + 16 + self.start[name])

    def drain(self, eng, name, count):
        for n in range(count + 1, count + self.L + 1):
            self.drained(eng, name, (n - 1) % self.L, n)


def row_blocks(bank):
    return bank[:, :].rearrange("c (j p) -> c j p", j=J)


L = 4
LONG = 8


def each_step(eng, step, lag, count=T, L=L):
    for i in range(2 * L):
        step(i, i)
    with eng.Fori(2, count // L) as r:
        for b in range(L):
            step(r * L + b, b)
    for i in range(count // L * L, count + lag):
        step(i, i)


def live(t, count=T):
    return not isinstance(t, int) or 0 <= t < count


class PowerNorm:

    def __init__(self, nc, ctx, prefix, k, w, S, go, used, name):
        sb = lambda n, shape: [ctx.enter_context(nc.sbuf_tensor(f"{prefix}_{name}_{n}{b}", shape, F32)) for b in range(w.L)]
        self.k, self.w, self.S, self.go, self.used, self.name = k, w, S, go, used, name
        self.six, self.mv = sb("six", [P, S, 6]), sb("mv", [P, S, 2])
        self.ve, self.rs = sb("ve", [P, S]), sb("rs", [P, S])

    @staticmethod
    def steps(name):
        return f" {name}_six {name}_mv {name}_ve {name}_rs "

    def stats(self, dve, X, b, n, rows=P):
        w, a = self.w, self.name
        w.freed(dve, a + "_mv", n)
        for s in range(self.S):
            last = dve.bn_stats(self.six[b][0:rows, s, :], X[0:rows, s, :])
        last.then_inc(w[a + "_six"], 1)

    def mean(self, dve, b, n, rows=P):
        w, a = self.w, self.name
        w.done(dve, a + "_six", n)
        w.freed(dve, self.used, n)
        dve.sem_inc(self.go["dve"], 1)
        for s in range(self.S):
            last = dve.bn_aggr(self.mv[b][0:rows, s, :], self.six[b][0:rows, s, :])
        last.then_inc(w[a + "_mv"], 1)

    def power(self, pool, b, n, rows=P):
        w, a = self.w, self.name
        w.done(pool, a + "_mv", n)
        w.freed(pool, a + "_rs", n)
        pool.sem_inc(self.go["pool"], 1)
        pool.tensor_scalar(self.ve[b][0:rows, :], self.mv[b][0:rows, :, 1], EPS, None, ALU.add).then_inc(w[a + "_ve"], 1)
        w.done(pool, a + "_ve", n)
        w.freed(pool, self.used, n)
        pool.tensor_tensor(self.rs[b][0:rows, :], self.ve[b][0:rows, :], self.k.minus_half[0:rows, 0:self.S], ALU.pow)\
            .then_inc(w[a + "_rs"], 1)

    def apply(self, dve, Y, X, b, n, step, rows=P):
        self.w.done(dve, self.name + "_rs", n)
        for s in range(self.S):
            last = dve.tensor_scalar(Y[0:rows, s, :], X[0:rows, s, :], self.mv[b][0:rows, s, 0:1],
                                     self.rs[b][0:rows, s:s + 1], ALU.subtract, ALU.mult)
        last.then_inc(self.w[step], 1)


class Stages:

    def __init__(self, L, count, groups=False):
        self.L, self.count, self.groups = L, count, groups

    def at(self, lag, i, b0):
        t = i - lag
        if not live(t, self.count):
            return None
        place = (t, (b0 - lag) % self.L, t + 1)
        return place + (TAIL if isinstance(t, int) and t == FULL else P,) if self.groups else place

    def each(self, eng, step, lag):
        each_step(eng, step, lag, self.count, self.L)


def nodes_first(nc, k):
    with Phase(nc) as ctx:
        L = LONG
        ring = lambda name, count, shape=[P, J, C]: [ctx.enter_context(nc.sbuf_tensor(f"n1_{name}{b}", shape, F32))
                                                     for b in range(count)]
        X = ring("X", L)
        X1, H, G, O = (ring(n, 4) for n in ("X1", "H", "G", "O"))
        H1, OSQ = ring("H1", 2), ring("OSQ", 2)
        HT, GT, H1T = (ring(n, 2, [C, J, P]) for n in ("HT", "GT", "H1T"))
        rsd, whole = ring("rsd", L, [P, J]), ring("whole", L, [P, J])
        hT, inner, g_ps, outer, h1T, root, stat_ps = (
            ctx.enter_context(nc.psum_tensor(f"n1_{n}_ps", [P, 512], F32))
            for n in ("hT", "inner", "g", "outer", "h1T", "root", "stat"))
        w = Turns(nc, ctx, "n1", L, PowerNorm.steps("a") + "rsd_a xn_a h_a hT_a ht_a w1 gt g_ps g w2 x1"
                  + PowerNorm.steps("b") + "xn_b h_b hT_b ht_b root o osq whole stats", "x_in h_out g_out x1_out o_out")
        stats_taken = ctx.semaphore("n1_stats_taken")
        turn = {e: ctx.semaphore(f"n1_turn_{e}") for e in ("pool", "dve")}
        lnA = PowerNorm(nc, ctx, "n1", k, w, J, turn, "xn_a", "a")
        lnB = PowerNorm(nc, ctx, "n1", k, w, J, turn, "xn_b", "b")
        block = ctx.enter_context(nc.Block())
        s = Stages(L, NG, groups=True)
        flat = lambda tile, rows: tile[0:rows].rearrange("p j c -> p (j c)")

        @block.sync
        def _(sp):
            w.credit(sp)

            def step(i, b0):
                if at := s.at(0, i, b0):
                    g, b, n, rows = at
                    w.freed(sp, "x1", n)
                    sp.dma_start(X[b][0:rows], node_rows(k.x, g, rows)).then_inc(w.moves["x_in"][b], 16)
                for lag, table, tile, size, done, move in ((9, k.O, O, 4, "o", "o_out"), (6, k.X1, X1, 4, "x1", "x1_out"),
                                                           (6, k.G1, G, 4, "g", "g_out"), (3, k.H0, H, 4, "h_a", "h_out")):
                    if at := s.at(lag, i, b0):
                        g, b, n, rows = at
                        w.done(sp, done, n)
                        sp.dma_start(node_rows(table, g, rows), tile[b % size][0:rows]).then_inc(w.moves[move][b], 16)

            s.each(sp, step, 9)
            for move in ("h_out", "g_out", "x1_out", "o_out"):
                w.drain(sp, move, NG)

        @block.vector
        def _(dve):
            def step(i, b0):
                if at := s.at(6, i, b0):
                    g, b, n, rows = at
                    w.freed(dve, "hT_b", n, 2)
                    lnB.apply(dve, H1[b % 2], X1[b % 4], b, n, "xn_b", rows)
                if at := s.at(5, i, b0):
                    g, b, n, rows = at
                    w.done(dve, "w2", n)
                    w.freed(dve, "xn_b", n, 4)
                    w.stored(dve, "x1_out", b, n, 4)
                    dve.tensor_tensor(flat(X1[b % 4], rows), outer[0:rows, :], flat(X[b], rows), ALU.add)\
                        .then_inc(w["x1"], 1)
                    w.done(dve, "x1", n)
                    lnB.stats(dve, X1[b % 4], b, n, rows)
                    lnB.mean(dve, b, n, rows)
                if at := s.at(2, i, b0):
                    g, b, n, rows = at
                    w.done(dve, "rsd_a", n)
                    w.freed(dve, "hT_a", n, 4)
                    w.stored(dve, "h_out", b, n, 4)
                    for j in range(J):
                        last = dve.tensor_scalar(H[b % 4][0:rows, j, :], X[b][0:rows, j, :], lnA.mv[b][0:rows, j, 0:1],
                                                 rsd[b][0:rows, j:j + 1], ALU.subtract, ALU.mult)
                    last.then_inc(w["xn_a"], 1)
                if at := s.at(1, i, b0):
                    g, b, n, rows = at
                    w.landed(dve, "x_in", b, n)
                    lnA.stats(dve, X[b], b, n, rows)
                    lnA.mean(dve, b, n, rows)

            s.each(dve, step, 6)
            dve.wait_ge(w["stats"], NG + L)
            dve.tensor_copy(k.stats_whole[:, :], stat_ps[:, 0:2]).then_inc(stats_taken, 1)
            dve.wait_ge(stats_taken, 1)

        @block.gpsimd
        def _(pool):
            def step(i, b0):
                if at := s.at(8, i, b0):
                    g, b, n, rows = at
                    w.freed(pool, "stats", n)
                    pool.sem_inc(turn["pool"], 1)
                    pool.tensor_copy(whole[b][:, :], k.whole[:, bass.ds(g * J, J)]).then_inc(w["whole"], 1)
                if at := s.at(5, i, b0):
                    g, b, n, rows = at
                    lnB.power(pool, b, n, rows)
                if at := s.at(1, i, b0):
                    g, b, n, rows = at
                    lnA.power(pool, b, n, rows)
                    w.done(pool, "a_rs", n)
                    w.freed(pool, "xn_a", n)
                    pool.sem_inc(turn["pool"], 1)
                    pool.tensor_tensor(rsd[b][0:rows, :], lnA.rs[b][0:rows, :],
                                       k.node_dinv[0:rows, bass.ds(g * J, J)], ALU.mult).then_inc(w["rsd_a"], 1)

            s.each(pool, step, 8)

        @block.tensor
        def _(pe):
            pe.matmul(stat_ps[:, 0:2], k.zero_row[:, :], k.zero_row[:, 0:2], start=True, stop=True, skip_group_check=True)

            def rowwise(dst, src, weight, v, rows):
                pe.matmul(dst[0:rows, :].rearrange("p (j c) -> p j c", j=J), k.ones3[:, 0:rows],
                          k.rows3[:, v:v + 1, :].to_broadcast([3, J, C]), start=True, stop=False, skip_group_check=True)
                for j in range(J):
                    last = pe.matmul(dst[0:rows, j * C:(j + 1) * C], src[:, j, 0:rows], weight[:, :], start=False,
                                     stop=True, skip_group_check=True)
                return last

            def turned(dst, src, rows):
                for j in range(J):
                    last = pe.transpose(dst[:, j * P:j * P + rows], src[0:rows, j, :], k.ident[0:rows, 0:rows])
                return last

            def step(i, b0):
                if at := s.at(9, i, b0):
                    g, b, n, rows = at
                    w.done(pe, "osq", n)
                    w.done(pe, "whole", n)
                    for c, src in enumerate((O[b % 4], OSQ[b % 2])):
                        for j in range(J):
                            last = pe.matmul(stat_ps[:, c:c + 1], src[0:rows, j, :], whole[b][0:rows, j:j + 1],
                                             start=False, stop=True, skip_group_check=True)
                    last.then_inc(w["stats"], 1)
                if at := s.at(8, i, b0):
                    g, b, n, rows = at
                    w.done(pe, "ht_b", n)
                    w.freed(pe, "osq", n, 1)
                    rowwise(root, H1T[b % 2], k.root, 2, rows).then_inc(w["root"], 1)
                if at := s.at(7, i, b0):
                    g, b, n, rows = at
                    w.done(pe, "h_b", n)
                    w.freed(pe, "ht_b", n, 1)
                    turned(h1T, H1[b % 2], rows).then_inc(w["hT_b"], 1)
                if at := s.at(5, i, b0):
                    g, b, n, rows = at
                    w.done(pe, "gt", n)
                    w.freed(pe, "g", n, 1)
                    for j in range(J):
                        last = pe.transpose(g_ps[0:rows, j * C:(j + 1) * C], GT[b % 2][:, j, 0:rows], k.ident[:, :])
                    last.then_inc(w["g_ps"], 1)
                    w.freed(pe, "x1", n, 1)
                    rowwise(outer, GT[b % 2], k.w2, 1, rows).then_inc(w["w2"], 1)
                if at := s.at(4, i, b0):
                    g, b, n, rows = at
                    w.done(pe, "ht_a", n)
                    w.freed(pe, "gt", n, 1)
                    pe.matmul(row_blocks(inner)[:, :, 0:rows], k.w1[:, :], HT[b % 2][:, :, 0:rows],
                              start=True, stop=True).then_inc(w["w1"], 1)
                if at := s.at(3, i, b0):
                    g, b, n, rows = at
                    w.done(pe, "h_a", n)
                    w.freed(pe, "ht_a", n, 1)
                    turned(hT, H[b % 4], rows).then_inc(w["hT_a"], 1)

            s.each(pe, step, 9)

        @block.scalar
        def _(act):
            def step(i, b0):
                if at := s.at(8, i, b0):
                    g, b, n, rows = at
                    w.done(act, "root", n)
                    w.freed(act, "stats", n, 4)
                    w.stored(act, "o_out", b, n, 4)
                    act.copy(flat(O[b % 4], rows), root[0:rows, :]).then_inc(w["o"], 1)
                    w.freed(act, "stats", n, 2)
                    act.activation(flat(OSQ[b % 2], rows), root[0:rows, :], ACT.Square).then_inc(w["osq"], 1)
                if at := s.at(7, i, b0):
                    g, b, n, rows = at
                    w.done(act, "hT_b", n)
                    w.freed(act, "root", n, 2)
                    act.copy(H1T[b % 2][:, :, 0:rows], row_blocks(h1T)[:, :, 0:rows]).then_inc(w["ht_b"], 1)
                if at := s.at(6, i, b0):
                    g, b, n, rows = at
                    w.done(act, "xn_b", n)
                    act.activation(H1[b % 2][0:rows], H1[b % 2][0:rows], ACT.Relu).then_inc(w["h_b"], 1)
                if at := s.at(5, i, b0):
                    g, b, n, rows = at
                    w.done(act, "g_ps", n)
                    w.stored(act, "g_out", b, n, 4)
                    act.copy(flat(G[b % 4], rows), g_ps[0:rows, :]).then_inc(w["g"], 1)
                if at := s.at(4, i, b0):
                    g, b, n, rows = at
                    w.done(act, "w1", n)
                    w.freed(act, "w2", n, 2)
                    act.activation(GT[b % 2][:, :, 0:rows], row_blocks(inner)[:, :, 0:rows], ACT.Relu,
                                   bias=k.b1_col[:, :]).then_inc(w["gt"], 1)
                if at := s.at(3, i, b0):
                    g, b, n, rows = at
                    w.done(act, "hT_a", n)
                    w.freed(act, "w1", n, 2)
                    act.copy(HT[b % 2][:, :, 0:rows], row_blocks(hT)[:, :, 0:rows]).then_inc(w["ht_a"], 1)
                if at := s.at(2, i, b0):
                    g, b, n, rows = at
                    w.done(act, "xn_a", n)
                    act.activation(H[b % 4][0:rows], H[b % 4][0:rows], ACT.Relu).then_inc(w["h_a"], 1)

            s.each(act, step, 8)


def tile_rows(table, t):
    return table[bass.ds(t * P, P), :]


class EdgePass:

    def __init__(self, nc, ctx, prefix, k, order, steps, moves, soft, L=L):
        self.k, self.o, self.L = k, order, L
        sb = lambda name, shape, dt=F32: ctx.enter_context(nc.sbuf_tensor(f"{prefix}_{name}", shape, dt))
        self.w = Turns(nc, ctx, prefix, L, "ids sid keys krow masks tot totsb " + steps, moves, soft)
        self.gid = [sb(f"gid{b}", [P, 2], I32) for b in range(L)]
        self.sid = [sb(f"sid{b}", [P, 1], I32) for b in range(L)]
        self.keys = [sb(f"keys{b}", [P, 2]) for b in range(L)]
        self.same, self.carry = ([sb(f"{n}{b}", [P, P]) for b in range(L)] for n in ("same", "carry"))
        self.totsb = [sb(f"totsb{b}", [P, C]) for b in range(L)]
        self.zeroed = ctx.semaphore(f"{prefix}_zeroed")
        self.turn = {e: ctx.semaphore(f"{prefix}_turn_{e}") for e in ("pool", "dve")}

    def start(self, dve):
        dve.memset(self.totsb[self.L - 1][:, :], 0.0).then_inc(self.zeroed, 1)

    def load_ids(self, eng, t, b, n, gathered, turn=None):
        for move in gathered:
            self.w.drained(eng, move, b, n)
        if turn is not None:
            eng.sem_inc(turn, 1)
        eng.tensor_copy(self.gid[b][:, :], self.k.index[:, self.o, bass.ds(t, 1), 0:2].rearrange("p a c -> p (a c)"))\
            .then_inc(self.w["ids"], 1)

    def load_sid(self, eng, t, b, n, scattered, turn=None):
        self.w.drained(eng, scattered, b, n)
        if turn is not None:
            eng.sem_inc(turn, 1)
        eng.tensor_copy(self.sid[b][:, :], self.k.index[:, self.o, bass.ds(t, 1), 2]).then_inc(self.w["sid"], 1)

    def gather(self, pool, tile, table, which, b, n, move):
        self.w.done(pool, "ids", n)
        pool.sem_inc(self.turn["pool"], 1)
        pool.indirect_dma_start(tile, None, table, bass.IndirectOffsetOnAxis(ap=self.gid[b][:, which:which + 1], axis=0))\
            .then_inc(self.w.moves[move][b], 16)

    def scatter(self, pool, table, tile, b, n, move):
        self.w.done(pool, "sid", n)
        pool.sem_inc(self.turn["pool"], 1)
        pool.indirect_dma_start(table, bass.IndirectOffsetOnAxis(ap=self.sid[b][:, 0:1], axis=0), tile, None,
                                bounds_check=N - 1, oob_is_err=False).then_inc(self.w.moves[move][b], 16)

    def load_keys(self, dve, t, b, n):
        self.w.freed(dve, "masks", n)
        dve.tensor_copy(self.keys[b][:, :], self.k.key[:, self.o, bass.ds(t, 2)]).then_inc(self.w["keys"], 1)

    def spread_keys(self, pe, banks, b, n, back=2):
        self.w.done(pe, "keys", n)
        self.w.freed(pe, "masks", n, back)
        pe.matmul(banks[b % 2][:, 0:P], self.keys[b][:, 1:2].to_broadcast([P, P]), self.k.ident[:, :], start=True,
                  stop=True).then_inc(self.w["krow"], 1)

    def masks(self, dve, banks, b, n):
        self.w.done(dve, "krow", n)
        self.w.freed(dve, "tot", n)
        dve.tensor_scalar(self.same[b][:, :], banks[b % 2][:, 0:P], self.keys[b][:, 1:2], None, ALU.is_equal)
        dve.tensor_scalar(self.carry[b][:, :], banks[b % 2][:, 0:P], self.keys[b][:, 0:1], self.k.last[:, :],
                          ALU.is_equal, ALU.mult).then_inc(self.w["masks"], 1)

    def sums(self, pe, banks, parts, b, n):
        self.w.done(pe, "masks", n)
        self.w.done(pe, "totsb", n - 1)
        for i, rows in enumerate(parts):
            pe.matmul(banks[b % 2][:, 0:C], self.same[b][:, :], rows, start=i == 0, stop=False)
        pe.matmul(banks[b % 2][:, 0:C], self.carry[b][:, :], self.totsb[(b - 1) % self.L][:, :], start=False,
                  stop=True).then_inc(self.w["tot"], 1)

    def keep_sums(self, act, banks, b, n):
        self.w.done(act, "tot", n)
        act.copy(self.totsb[b][:, :], banks[b % 2][:, 0:C]).then_inc(self.w["totsb"], 1)


class Norm:

    STEPS = "ln_six ln_mv ln_ve ln_iv ln_rs "

    def __init__(self, nc, ctx, prefix, w, S, go, used, name="ln"):
        L = w.L
        sb = lambda n, shape: [ctx.enter_context(nc.sbuf_tensor(f"{prefix}_{name}_{n}{b}", shape, F32)) for b in range(L)]
        self.w, self.S, self.go, self.name = w, S, go, name
        self.used = used
        self.six, self.mv = sb("six", [P, S, 6]), sb("mv", [P, S, 2])
        self.ve, self.iv, self.rs = (sb(n, [P, S]) for n in ("ve", "iv", "rs"))

    def stats(self, dve, X, b, n):
        self.w.freed(dve, self.name + "_mv", n)
        for s in range(self.S):
            last = dve.bn_stats(self.six[b][:, s, :], X[:, s, :])
        last.then_inc(self.w[self.name + "_six"], 1)

    def mean(self, dve, b, n):
        self.w.done(dve, self.name + "_six", n)
        self.w.freed(dve, self.used, n)
        dve.sem_inc(self.go, 1)
        for s in range(self.S):
            last = dve.bn_aggr(self.mv[b][:, s, :], self.six[b][:, s, :])
        last.then_inc(self.w[self.name + "_mv"], 1)

    def shifted(self, dve, b, n):
        self.w.done(dve, self.name + "_mv", n)
        dve.tensor_scalar(self.ve[b][:, :], self.mv[b][:, :, 1], EPS, None, ALU.add).then_inc(self.w[self.name + "_ve"], 1)

    def inverse(self, dve, b, n):
        self.w.done(dve, self.name + "_ve", n)
        dve.reciprocal(self.iv[b][:, :], self.ve[b][:, :]).then_inc(self.w[self.name + "_iv"], 1)

    def root(self, act, b, n):
        self.w.done(act, self.name + "_iv", n)
        act.activation(self.rs[b][:, :], self.iv[b][:, :], ACT.Sqrt).then_inc(self.w[self.name + "_rs"], 1)


def edges_first(nc, k):
    with Phase(nc) as ctx:
        L = LONG
        sb = lambda name, shape: [ctx.enter_context(nc.sbuf_tensor(f"e1_{name}{b}", shape, F32)) for b in range(L)]
        p = EdgePass(nc, ctx, "e1", k, 0, Norm.STEPS + "rs3 dv nm a aT at y go hd", "slot_x slot_g", "g_in x_in go_out", L)
        w = p.w
        ln = Norm(nc, ctx, "e1", w, 1, p.turn["dve"], "nm")
        GS, HD, A, AT, GO = (sb(n, [P, C]) for n in ("GS", "HD", "A", "AT", "GO"))
        XD = sb("XD", [P, 1, C])
        rs3, nm, dv = (sb(n, [P, 1]) for n in ("rs3", "nm", "dv"))
        krow, tot, aT, y = ([ctx.enter_context(nc.psum_tensor(f"e1_{n}{b}", [P, 512], F32)) for b in range(2)]
                            for n in ("krow", "tot", "aT", "y"))
        s = Stages(L, T)
        block = ctx.enter_context(nc.Block())

        @block.sync
        def _(sp):
            w.credit(sp)

            def step(i, b0):
                if at := s.at(7, i, b0):
                    t, b, n = at
                    w.done(sp, "go", n)
                    sp.dma_start(tile_rows(k.slot_g, t), GO[b][:, :]).then_inc(w.moves["slot_g"][b], 16)
                if at := s.at(3, i, b0):
                    t, b, n = at
                    w.landed(sp, "x_in", b, n)
                    sp.dma_start(tile_rows(k.slot_x, t), XD[b][:, 0, :]).then_inc(w.moves["slot_x"][b], 16)

            s.each(sp, step, 7)
            w.drain(sp, "slot_x", T)
            w.drain(sp, "slot_g", T)

        @block.gpsimd
        def _(pool):
            def step(i, b0):
                if at := s.at(6, i, b0):
                    t, b, n = at
                    w.done(pool, "go", n)
                    p.scatter(pool, k.G1, GO[b][:, :], b, n, "go_out")
                if at := s.at(0, i, b0):
                    t, b, n = at
                    w.freed(pool, "tot", n)
                    p.gather(pool, GS[b][:, :], k.H0, 0, b, n, "g_in")
                    w.freed(pool, "hd", n)
                    w.drained(pool, "slot_x", b, n)
                    p.gather(pool, XD[b][:, 0, :], k.x, 1, b, n, "x_in")

            s.each(pool, step, 6)
            w.drain(pool, "go_out", T)

        @block.vector
        def _(dve):
            p.start(dve)

            def step(i, b0):
                if at := s.at(0, i, b0):
                    t, b, n = at
                    p.load_ids(dve, t, b, n, ("g_in", "x_in"))
                if at := s.at(2, i, b0):
                    t, b, n = at
                    p.load_sid(dve, t, b, n, "go_out")
                ends, mid, now = s.at(4, i, b0), s.at(3, i, b0), s.at(2, i, b0)
                if now:
                    t, b, n = now
                    w.landed(dve, "x_in", b, n)
                    ln.stats(dve, XD[b], b, n)
                if mid:
                    t, b, n = mid
                    w.done(dve, "ln_rs", n)
                    w.done(dve, "dv", n)
                    w.freed(dve, "hd", n)
                    dve.tensor_scalar(rs3[b][:, :], ln.rs[b][:, :], dv[b][:, :], dv[b][:, :], ALU.mult, ALU.mult)\
                        .then_inc(w["rs3"], 1)
                if now:
                    t, b, n = now
                    ln.mean(dve, b, n)
                if mid:
                    t, b, n = mid
                    w.done(dve, "rs3", n)
                    dve.tensor_scalar(nm[b][:, :], ln.mv[b][:, :, 0], rs3[b][:, :], -1.0, ALU.mult, ALU.mult)\
                        .then_inc(w["nm"], 1)
                if now:
                    t, b, n = now
                    ln.shifted(dve, b, n)
                if ends:
                    t, b, n = ends
                    w.done(dve, "totsb", n)
                    w.done(dve, "hd", n)
                    w.freed(dve, "aT", n)
                    dve.scalar_tensor_tensor(A[b][:, :], p.totsb[b][:, :], dv[b][:, :], HD[b][:, :], ALU.mult,
                                             ALU.add).then_inc(w["a"], 1)
                if now:
                    t, b, n = now
                    ln.inverse(dve, b, n)
                    w.freed(dve, "go", n)
                    w.freed(dve, "a", n)
                    dve.tensor_copy(dv[b][:, :], k.dinv[:, bass.ds(t, 1)]).then_inc(w["dv"], 1)
                    p.masks(dve, krow, b, n)
                if at := s.at(1, i, b0):
                    t, b, n = at
                    p.load_keys(dve, t, b, n)

            s.each(dve, step, 4)

        @block.tensor
        def _(pe):
            pe.wait_ge(p.zeroed, 1)

            def step(i, b0):
                if at := s.at(6, i, b0):
                    t, b, n = at
                    w.done(pe, "at", n)
                    w.freed(pe, "go", n, 2)
                    pe.matmul(y[b % 2][:, 0:C], k.ones3[:, :], k.rows3[:, 0, :], start=True, stop=False, skip_group_check=True)
                    pe.matmul(y[b % 2][:, 0:C], AT[b][:, :], k.w1[:, :], start=False, stop=True, skip_group_check=True)\
                        .then_inc(w["y"], 1)
                if at := s.at(5, i, b0):
                    t, b, n = at
                    w.done(pe, "a", n)
                    w.freed(pe, "at", n, 2)
                    pe.transpose(aT[b % 2][:, 0:P], A[b][:, :], k.ident[:, :]).then_inc(w["aT"], 1)
                if at := s.at(3, i, b0):
                    t, b, n = at
                    w.landed(pe, "g_in", b, n)
                    p.sums(pe, tot, [GS[b][:, :]], b, n)
                if at := s.at(2, i, b0):
                    t, b, n = at
                    p.spread_keys(pe, krow, b, n)

            s.each(pe, step, 6)

        @block.scalar
        def _(act):
            def step(i, b0):
                if at := s.at(6, i, b0):
                    t, b, n = at
                    w.done(act, "y", n)
                    w.drained(act, "go_out", b, n)
                    w.drained(act, "slot_g", b, n)
                    act.activation(GO[b][:, :], y[b % 2][:, 0:C], ACT.Relu, scale=dv[b][:, :]).then_inc(w["go"], 1)
                if at := s.at(5, i, b0):
                    t, b, n = at
                    w.done(act, "aT", n)
                    w.freed(act, "y", n)
                    act.copy(AT[b][:, :], aT[b % 2][:, 0:P]).then_inc(w["at"], 1)
                if at := s.at(4, i, b0):
                    t, b, n = at
                    w.done(act, "nm", n)
                    w.freed(act, "a", n)
                    act.activation(HD[b][:, :], XD[b][:, 0, :], ACT.Relu, bias=nm[b][:, :], scale=rs3[b][:, :])\
                        .then_inc(w["hd"], 1)
                if at := s.at(3, i, b0):
                    t, b, n = at
                    w.freed(act, "a", n)
                    p.keep_sums(act, tot, b, n)
                    ln.root(act, b, n)

            s.each(act, step, 6)


def edges_second(nc, k):
    with Phase(nc) as ctx:
        L = LONG
        sb = lambda name, shape: [ctx.enter_context(nc.sbuf_tensor(f"e2_{name}{b}", shape, F32)) for b in range(L)]
        p = EdgePass(nc, ctx, "e2", k, 0, "dv a as aT at y xo", "x_in d_in slot_x", "g_in xo_out", L)
        w = p.w
        GS, XD, GD, A, AS, AT, XO = (sb(n, [P, C]) for n in ("GS", "XD", "GD", "A", "AS", "AT", "XO"))
        dv = sb("dv", [P, 1])
        krow, tot, aT, y = ([ctx.enter_context(nc.psum_tensor(f"e2_{n}{b}", [P, 512], F32)) for b in range(2)]
                            for n in ("krow", "tot", "aT", "y"))
        s = Stages(L, T)
        block = ctx.enter_context(nc.Block())

        @block.sync
        def _(sp):
            w.credit(sp)

            def step(i, b0):
                if at := s.at(7, i, b0):
                    t, b, n = at
                    w.done(sp, "xo", n)
                    sp.dma_start(tile_rows(k.slot_x2, t), XO[b][:, :]).then_inc(w.moves["slot_x"][b], 16)
                if at := s.at(0, i, b0):
                    t, b, n = at
                    w.freed(sp, "xo", n)
                    sp.dma_start(XD[b][:, :], tile_rows(k.slot_x, t)).then_inc(w.moves["x_in"][b], 16)
                    w.freed(sp, "a", n)
                    sp.dma_start(GD[b][:, :], tile_rows(k.slot_g, t)).then_inc(w.moves["d_in"][b], 16)

            s.each(sp, step, 7)
            w.drain(sp, "slot_x", T)

        @block.gpsimd
        def _(pool):
            def step(i, b0):
                if at := s.at(6, i, b0):
                    t, b, n = at
                    w.done(pool, "xo", n)
                    p.scatter(pool, k.X1, XO[b][:, :], b, n, "xo_out")
                if at := s.at(0, i, b0):
                    t, b, n = at
                    w.freed(pool, "tot", n)
                    p.gather(pool, GS[b][:, :], k.G1, 0, b, n, "g_in")

            s.each(pool, step, 6)
            w.drain(pool, "xo_out", T)

        @block.vector
        def _(dve):
            p.start(dve)

            def step(i, b0):
                if at := s.at(0, i, b0):
                    t, b, n = at
                    p.load_ids(dve, t, b, n, ("g_in",))
                if at := s.at(2, i, b0):
                    t, b, n = at
                    p.load_sid(dve, t, b, n, "xo_out")
                if at := s.at(6, i, b0):
                    t, b, n = at
                    w.done(dve, "y", n)
                    w.landed(dve, "x_in", b, n)
                    w.drained(dve, "xo_out", b, n)
                    w.drained(dve, "slot_x", b, n)
                    dve.tensor_tensor(XO[b][:, :], y[b % 2][:, 0:C], XD[b][:, :], ALU.add).then_inc(w["xo"], 1)
                if at := s.at(4, i, b0):
                    t, b, n = at
                    w.done(dve, "totsb", n)
                    w.landed(dve, "d_in", b, n)
                    w.freed(dve, "as", n)
                    dve.tensor_tensor(A[b][:, :], p.totsb[b][:, :], GD[b][:, :], ALU.add).then_inc(w["a"], 1)
                    w.done(dve, "a", n)
                    w.done(dve, "dv", n)
                    w.freed(dve, "aT", n)
                    dve.tensor_scalar(AS[b][:, :], A[b][:, :], dv[b][:, :], None, ALU.mult).then_inc(w["as"], 1)
                if at := s.at(2, i, b0):
                    t, b, n = at
                    w.freed(dve, "as", n)
                    dve.tensor_copy(dv[b][:, :], k.dinv[:, bass.ds(t, 1)]).then_inc(w["dv"], 1)
                    p.masks(dve, krow, b, n)
                if at := s.at(1, i, b0):
                    t, b, n = at
                    p.load_keys(dve, t, b, n)

            s.each(dve, step, 6)

        @block.tensor
        def _(pe):
            pe.wait_ge(p.zeroed, 1)

            def step(i, b0):
                if at := s.at(6, i, b0):
                    t, b, n = at
                    w.done(pe, "at", n)
                    w.freed(pe, "xo", n, 2)
                    pe.matmul(y[b % 2][:, 0:C], k.ones3[:, :], k.rows3[:, 1, :], start=True, stop=False, skip_group_check=True)
                    pe.matmul(y[b % 2][:, 0:C], AT[b][:, :], k.w2[:, :], start=False, stop=True, skip_group_check=True)\
                        .then_inc(w["y"], 1)
                if at := s.at(5, i, b0):
                    t, b, n = at
                    w.done(pe, "as", n)
                    w.freed(pe, "at", n, 2)
                    pe.transpose(aT[b % 2][:, 0:P], AS[b][:, :], k.ident[:, :]).then_inc(w["aT"], 1)
                if at := s.at(3, i, b0):
                    t, b, n = at
                    w.landed(pe, "g_in", b, n)
                    p.sums(pe, tot, [GS[b][:, :]], b, n)
                if at := s.at(2, i, b0):
                    t, b, n = at
                    p.spread_keys(pe, krow, b, n)

            s.each(pe, step, 6)

        @block.scalar
        def _(act):
            def step(i, b0):
                if at := s.at(5, i, b0):
                    t, b, n = at
                    w.done(act, "aT", n)
                    w.freed(act, "y", n)
                    act.copy(AT[b][:, :], aT[b % 2][:, 0:P]).then_inc(w["at"], 1)
                if at := s.at(3, i, b0):
                    t, b, n = at
                    w.freed(act, "a", n)
                    p.keep_sums(act, tot, b, n)

            s.each(act, step, 5)


def edges_third(nc, k):
    with Phase(nc) as ctx:
        L = LONG
        sb = lambda name, shape, count=L: [ctx.enter_context(nc.sbuf_tensor(f"e3_{name}{b}", shape, F32))
                                           for b in range(count)]
        p = EdgePass(nc, ctx, "e3", k, 0, Norm.STEPS + "rw nm h hT ht rel pm ps pq msg y o osq st", "x_in",
                     "g_in o_out", L)
        w = p.w
        ln = Norm(nc, ctx, "e3", w, 2, p.turn["dve"], "h")
        XX, H = sb("XX", [P, 2, C]), sb("H", [P, 2, C])
        HT = sb("HT", [C, 2, P])
        PM, PS, PQ = sb("PM", [P, R, C], 2), sb("PS", [P, R // 2, C], 2), sb("PQ", [P, R // 4, C], 2)
        MSG, O, OSQ = sb("MSG", [P, C]), sb("O", [P, C]), sb("OSQ", [P, C])
        rw, lst, nm = sb("rw", [P, R]), sb("lst", [P, 1]), sb("nm", [P, 2])
        bank = lambda name: ctx.enter_context(nc.psum_tensor(f"e3_{name}", [P, 512], F32))
        krow, tot, hT, stat = (bank(n) for n in ("krow", "tot", "hT", "stat"))
        y = [bank(f"y{b}") for b in range(2)]
        rel = [bank(f"rel{h}") for h in range(2)]
        stats_taken = ctx.semaphore("e3_stats_taken")
        block = ctx.enter_context(nc.Block())
        s = Stages(L, T)

        @block.sync
        def _(sp):
            w.credit(sp)

            def step(i, b0):
                if at := s.at(0, i, b0):
                    t, b, n = at
                    w.freed(sp, "h", n)
                    sp.dma_start(XX[b][:, 1, :], tile_rows(k.slot_x2, t)).then_inc(w.moves["x_in"][b], 16)

            s.each(sp, step, 0)

        @block.gpsimd
        def _(pool):
            def step(i, b0):
                if at := s.at(9, i, b0):
                    t, b, n = at
                    w.done(pool, "o", n)
                    p.load_sid(pool, t, b, n, "o_out", p.turn["pool"])
                    p.scatter(pool, k.O, O[b][:, :], b, n, "o_out")
                if at := s.at(0, i, b0):
                    t, b, n = at
                    p.load_ids(pool, t, b, n, ("g_in",), p.turn["pool"])
                    w.freed(pool, "h", n)
                    p.gather(pool, XX[b][:, 0, :], k.X1, 0, b, n, "g_in")

            s.each(pool, step, 9)
            w.drain(pool, "o_out", T)

        @block.vector
        def _(dve):
            p.start(dve)

            def step(i, b0):
                if at := s.at(9, i, b0):
                    t, b, n = at
                    w.done(dve, "totsb", n)
                    w.done(dve, "y", n)
                    w.drained(dve, "o_out", b, n)
                    w.freed(dve, "st", n)
                    dve.tensor_tensor(O[b][:, :], y[b % 2][:, 0:C], p.totsb[b][:, :], ALU.add)\
                        .then_inc(w["o"], 1)
                now, first = s.at(6, i, b0), s.at(2, i, b0)
                if now:
                    t, b, n = now
                    w.freed(dve, "pm", n)
                    w.freed(dve, "st", n)
                    dve.tensor_copy(lst[b][:, :], k.is_last[:, bass.ds(t, 1)])
                    dve.tensor_copy(rw[b][:, :], k.rel_weight[:, bass.ds(t, 1), :].rearrange("p a r -> p (a r)"))\
                        .then_inc(w["rw"], 1)
                    p.masks(dve, [krow, krow], b, n)
                    w.done(dve, "rw", n)
                    w.done(dve, "rel", n)
                    w.freed(dve, "ps", n, 2)
                    for h in range(2):
                        last = dve.tensor_tensor(
                            PM[b % 2][:, h * 4:h * 4 + 4, :], rel[h][:, :].rearrange("p (r c) -> p r c", c=C),
                            rw[b][:, h * 4:h * 4 + 4].rearrange("p (r c) -> p r c", c=1).to_broadcast([P, 4, C]), ALU.mult)
                    last.then_inc(w["pm"], 1)
                if first:
                    t, b, n = first
                    w.landed(dve, "g_in", b, n)
                    w.landed(dve, "x_in", b, n)
                    ln.stats(dve, XX[b], b, n)
                if now:
                    t, b, n = now
                    w.done(dve, "pm", n)
                    w.freed(dve, "pq", n, 2)
                    dve.tensor_tensor(PS[b % 2][:, :, :], PM[b % 2][:, 0:4, :], PM[b % 2][:, 4:8, :], ALU.add)\
                        .then_inc(w["ps"], 1)
                if first:
                    t, b, n = first
                    ln.mean(dve, b, n)
                if now:
                    t, b, n = now
                    w.done(dve, "ps", n)
                    w.freed(dve, "msg", n, 2)
                    dve.tensor_tensor(PQ[b % 2][:, :, :], PS[b % 2][:, 0:2, :], PS[b % 2][:, 2:4, :], ALU.add)\
                        .then_inc(w["pq"], 1)
                if first:
                    t, b, n = first
                    ln.shifted(dve, b, n)
                if at := s.at(3, i, b0):
                    t, b, n = at
                    w.done(dve, "ln_rs", n)
                    w.freed(dve, "h", n)
                    dve.scalar_tensor_tensor(nm[b][:, :], ln.mv[b][:, :, 0], -1.0, ln.rs[b][:, :], ALU.mult, ALU.mult)\
                        .then_inc(w["nm"], 1)
                if now:
                    t, b, n = now
                    w.done(dve, "pq", n)
                    w.freed(dve, "tot", n)
                    dve.tensor_tensor(MSG[b][:, :], PQ[b % 2][:, 0, :], PQ[b % 2][:, 1, :], ALU.add)\
                        .then_inc(w["msg"], 1)
                if first:
                    t, b, n = first
                    ln.inverse(dve, b, n)
                if at := s.at(3, i, b0):
                    t, b, n = at
                    p.load_keys(dve, t, b, n)

            s.each(dve, step, 9)
            dve.wait_ge(w["st"], T + L)
            dve.tensor_copy(k.stats_edges[:, :], stat[:, 0:2]).then_inc(stats_taken, 1)
            dve.wait_ge(stats_taken, 1)

        @block.tensor
        def _(pe):
            pe.wait_ge(p.zeroed, 1)
            pe.matmul(stat[:, 0:2], k.zero_row[:, :], k.zero_row[:, 0:2], start=True, stop=True, skip_group_check=True)

            def step(i, b0):
                if at := s.at(11, i, b0):
                    t, b, n = at
                    w.done(pe, "osq", n)
                    for c, src in enumerate((O, OSQ)):
                        last = pe.matmul(stat[:, c:c + 1], src[b][:, :], lst[b][:, :], start=False, stop=True,
                                         skip_group_check=True)
                    last.then_inc(w["st"], 1)
                if at := s.at(8, i, b0):
                    t, b, n = at
                    w.done(pe, "msg", n)
                    p.sums(pe, [tot, tot], [MSG[b][:, :]], b, n)
                    w.freed(pe, "o", n, 2)
                    pe.matmul(y[b % 2][:, 0:C], k.ones3[:, :], k.rows3[:, 2, :], start=True, stop=False, skip_group_check=True)
                    pe.matmul(y[b % 2][:, 0:C], HT[b][:, 1, :], k.root[:, :], start=False, stop=True, skip_group_check=True)\
                        .then_inc(w["y"], 1)
                if at := s.at(6, i, b0):
                    t, b, n = at
                    p.spread_keys(pe, [krow, krow], b, n, 1)
                    w.done(pe, "ht", n)
                    w.freed(pe, "pm", n, 1)
                    for h in range(2):
                        last = pe.matmul(rel[h][:, :], HT[b][:, 0, :],
                                         k.w_rel[:, h * 4:h * 4 + 4, :].rearrange("c r d -> c (r d)"), start=True, stop=True)
                    last.then_inc(w["rel"], 1)
                if at := s.at(5, i, b0):
                    t, b, n = at
                    w.done(pe, "h", n)
                    w.freed(pe, "ht", n, 1)
                    for half in range(2):
                        last = pe.transpose(hT[:, half * P:(half + 1) * P], H[b][:, half, :], k.ident[:, :])
                    last.then_inc(w["hT"], 1)

            s.each(pe, step, 11)

        @block.scalar
        def _(act):
            def step(i, b0):
                if at := s.at(10, i, b0):
                    t, b, n = at
                    w.done(act, "o", n)
                    w.freed(act, "st", n)
                    act.activation(OSQ[b][:, :], O[b][:, :], ACT.Square).then_inc(w["osq"], 1)
                if at := s.at(8, i, b0):
                    t, b, n = at
                    w.freed(act, "o", n)
                    p.keep_sums(act, [tot, tot], b, n)
                if at := s.at(5, i, b0):
                    t, b, n = at
                    w.done(act, "hT", n)
                    w.freed(act, "y", n)
                    act.copy(HT[b][:, :, :].rearrange("c s p -> c (s p)"), hT[:, 0:2 * P]).then_inc(w["ht"], 1)
                if at := s.at(4, i, b0):
                    t, b, n = at
                    w.done(act, "nm", n)
                    w.freed(act, "hT", n)
                    act.activation(H[b][:, 0, :], XX[b][:, 0, :], ACT.Relu, bias=nm[b][:, 0:1], scale=ln.rs[b][:, 0:1])
                    act.activation(H[b][:, 1, :], XX[b][:, 1, :], ACT.Relu, bias=nm[b][:, 1:2], scale=ln.rs[b][:, 1:2])\
                        .then_inc(w["h"], 1)
                if at := s.at(3, i, b0):
                    t, b, n = at
                    ln.root(act, b, n)

            s.each(act, step, 10)


def row_tables(nc, k):
    with Phase(nc) as ctx:
        sb = lambda name, shape: ctx.enter_context(nc.sbuf_tensor("rt_" + name, shape, F32))
        cols = sb("cols", [C, 6])
        gamma_beta = sb("gamma_beta", [C, 2])
        bm2 = sb("bm2", [C, 1])
        total, mean, tmp, var, std, shift = (sb(n, [C, w]) for n, w in
                                             (("total", 2), ("mean", 2), ("tmp", 1), ("var", 1), ("std", 1), ("shift", 1)))
        wm2, wm2_t, wu1b = (sb(n, [C, C]) for n in ("wm2", "wm2_t", "wu1b"))
        spread = [ctx.enter_context(nc.psum_tensor(f"rt_spread{i}", [P, 512], F32)) for i in range(2)]
        wt_ps, wc_ps = (ctx.enter_context(nc.psum_tensor(f"rt_{n}", [P, 512], F32)) for n in ("wt", "wc"))
        chain, loaded, var_ready, std_ready = (ctx.semaphore("rt_" + n) for n in ("chain", "loaded", "var_ready", "std_ready"))
        turned, turned_in, product, cols_ready, spread_ready = (
            ctx.semaphore("rt_" + n) for n in ("turned", "turned_in", "product", "cols_ready", "spread_ready"))
        block = ctx.enter_context(nc.Block())
        col = lambda vector: vector.rearrange("(c a) -> c a", a=1)
        loads = [(gamma_beta[:, 0:1], col(k.L1_gamma)), (gamma_beta[:, 1:2], col(k.L1_beta)),
                 (cols[:, 2:3], col(k.L2_gamma)), (cols[:, 3:4], col(k.L2_beta)),
                 (cols[:, 4:5], col(k.L3_W2)), (cols[:, 5:6], col(k.L3_W3)), (bm2[:, :], col(k.L2_bm2)),
                 (k.bm1_col[:, :], col(k.L2_bm1)), (k.bu1_col[:, :], col(k.L2_bu1)), (wm2[:, :], k.L2_wm2),
                 (wu1b[:, :], k.L2_wu1[C:2 * C, :]), (k.wu1a[:, :], k.L2_wu1[0:C, :]), (k.wu2[:, :], k.L2_wu2),
                 (k.wm1a[:, :], k.L2_wm1[0:C, :]), (k.wm1b[:, :], k.L2_wm1[C:2 * C, :])]

        @block.sync
        def _(sp):
            for tile, source in loads:
                sp.dma_start(tile, source).then_inc(loaded, 16)
            sp.wait_ge(loaded, 16 * len(loads))

        @block.vector
        def _(dve):
            links = [0]

            def link(ins):
                links[0] += 1
                ins.then_inc(chain, 1)
                dve.wait_ge(chain, links[0])

            link(dve.tensor_tensor(total[:, :], k.stats_whole[:, :], k.stats_edges[:, :], ALU.add))
            link(dve.tensor_scalar(mean[:, :], total[:, :], 1.0 / N, None, ALU.mult))
            link(dve.tensor_tensor(tmp[:, :], mean[:, 0:1], mean[:, 0:1], ALU.mult))
            link(dve.tensor_tensor(var[:, :], mean[:, 1:2], tmp[:, :], ALU.subtract))
            link(dve.tensor_scalar(var[:, :], var[:, :], 0.0, EPS, ALU.max, ALU.add))
            dve.reciprocal(tmp[:, :], var[:, :]).then_inc(var_ready, 1)
            dve.wait_ge(std_ready, 1)
            dve.wait_ge(loaded, 16 * len(loads))
            link(dve.tensor_tensor(cols[:, 0:1], gamma_beta[:, 0:1], std[:, :], ALU.mult))
            link(dve.tensor_tensor(shift[:, :], mean[:, 0:1], cols[:, 0:1], ALU.mult))
            dve.tensor_tensor(cols[:, 1:2], gamma_beta[:, 1:2], shift[:, :], ALU.subtract).then_inc(cols_ready, 1)
            dve.wait_ge(turned, 1)
            dve.tensor_copy(wm2_t[:, :], wt_ps[:, 0:C]).then_inc(turned_in, 1)
            dve.wait_ge(product, 1)
            dve.tensor_copy(k.wc[:, :], wc_ps[:, 0:C])
            link(dve.tensor_copy(k.cb[:, :], wc_ps[:, C:2 * C]))
            dve.wait_ge(spread_ready, 1)
            for i in range(2):
                link(dve.tensor_copy(k.spread[:, i * 3:i * 3 + 3, :].rearrange("p a c -> p (a c)"), spread[i][:, 0:3 * C]))

        @block.scalar
        def _(act):
            act.wait_ge(var_ready, 1)
            act.activation(std[:, :], tmp[:, :], ACT.Sqrt).then_inc(std_ready, 1)

        @block.tensor
        def _(pe):
            pe.wait_ge(loaded, 16 * len(loads))
            pe.transpose(wt_ps[:, 0:C], wm2[:, :], k.ident[:, :]).then_inc(turned, 1)
            pe.wait_ge(turned_in, 1)
            pe.matmul(wc_ps[:, 0:C], wm2_t[:, :], wu1b[:, :], start=True, stop=True)
            pe.matmul(wc_ps[:, C:2 * C], bm2[:, :].to_broadcast([C, P]), wu1b[:, :], start=True, stop=True)\
                .then_inc(product, 1)
            pe.wait_ge(cols_ready, 1)
            for i in range(6):
                last = pe.matmul(spread[i // 3][:, i % 3 * C:(i % 3 + 1) * C], cols[:, i:i + 1].to_broadcast([C, P]),
                                 k.ident[:, :], start=True, stop=True)
            last.then_inc(spread_ready, 1)


def nodes_second(nc, k):
    with Phase(nc) as ctx:
        L = LONG
        ring = lambda name, count, shape=[P, J, C]: [ctx.enter_context(nc.sbuf_tensor(f"n2_{name}{b}", shape, F32))
                                                     for b in range(count)]
        X1, O, Z, Q, X2, H = (ring(n, 4) for n in ("X1", "O", "Z", "Q", "X2", "H"))
        S, YG = ring("S", 2), ring("YG", 2)
        X3 = ring("X3", L)
        nm = ring("nm", L, [P, J])
        HT = ring("HT", 4, [C, J, P])
        SU, UT = (ring(n, 2, [C, J, P]) for n in ("SU", "UT"))
        hT, u, y = ([ctx.enter_context(nc.psum_tensor(f"n2_{n}{b}", [P, 512], F32)) for b in range(2)]
                    for n in ("hT", "u", "y"))
        w = Turns(nc, ctx, "n2", L, "z0 z s sq q1 iq gate zg x2 x2b" + PowerNorm.steps("a") + "nm xn hT ht u su ut y"
                  + PowerNorm.steps("b") + "yg x3", "x1_in o_in x2_out h_out out")
        turn = {e: ctx.semaphore(f"n2_turn_{e}") for e in ("pool", "dve")}
        lnA = PowerNorm(nc, ctx, "n2", k, w, J, turn, "xn", "a")
        lnB = PowerNorm(nc, ctx, "n2", k, w, J, turn, "x3", "b")
        minus_one = ctx.enter_context(nc.sbuf_tensor("n2_minus_one", [P, 1], F32))
        constant = ctx.semaphore("n2_constant")
        block = ctx.enter_context(nc.Block())
        s = Stages(L, NG, groups=True)
        vec = lambda i, rows: k.spread[0:rows, i:i + 1, :].to_broadcast([rows, J, C])

        @block.sync
        def _(sp):
            w.credit(sp)

            def step(i, b0):
                if at := s.at(0, i, b0):
                    g, b, n, rows = at
                    w.freed(sp, "z0", n, 4)
                    sp.dma_start(O[b % 4][0:rows], node_rows(k.O, g, rows)).then_inc(w.moves["o_in"][b], 16)
                if at := s.at(2, i, b0):
                    g, b, n, rows = at
                    w.freed(sp, "x2", n, 4)
                    sp.dma_start(X1[b % 4][0:rows], node_rows(k.X1, g, rows)).then_inc(w.moves["x1_in"][b], 16)
                if at := s.at(12, i, b0):
                    g, b, n, rows = at
                    w.done(sp, "x3", n)
                    sp.dma_start(node_rows(k.out, g, rows), X3[b][0:rows]).then_inc(w.moves["out"][b], 16)
                if at := s.at(8, i, b0):
                    g, b, n, rows = at
                    w.done(sp, "xn", n)
                    sp.dma_start(node_rows(k.XH[:, C:2 * C], g, rows), H[b % 4][0:rows]).then_inc(w.moves["h_out"][b], 16)
                if at := s.at(5, i, b0):
                    g, b, n, rows = at
                    w.done(sp, "x2", n)
                    sp.dma_start(node_rows(k.XH[:, 0:C], g, rows), X2[b % 4][0:rows]).then_inc(w.moves["x2_out"][b], 16)

            s.each(sp, step, 12)
            for move in ("x2_out", "h_out", "out"):
                w.drain(sp, move, NG)

        @block.gpsimd
        def _(pool):
            def step(i, b0):
                if at := s.at(10, i, b0):
                    g, b, n, rows = at
                    lnB.power(pool, b, n, rows)
                if at := s.at(5, i, b0):
                    g, b, n, rows = at
                    lnA.power(pool, b, n, rows)
                    w.done(pool, "x2", n)
                    w.stored(pool, "out", b, n, L)
                    pool.tensor_tensor(X3[b][0:rows], X2[b % 4][0:rows], vec(3, rows), ALU.add).then_inc(w["x2b"], 1)
                if at := s.at(4, i, b0):
                    g, b, n, rows = at
                    w.done(pool, "gate", n)
                    pool.tensor_tensor(Q[b % 4][0:rows], Q[b % 4][0:rows], Z[b % 4][0:rows], ALU.mult).then_inc(w["zg"], 1)
                    w.done(pool, "zg", n)
                    w.landed(pool, "x1_in", b, n)
                    w.freed(pool, "xn", n, 4)
                    w.freed(pool, "x2b", n, 4)
                    w.stored(pool, "x2_out", b, n, 4)
                    pool.tensor_tensor(X2[b % 4][0:rows], X1[b % 4][0:rows], Q[b % 4][0:rows], ALU.add)\
                        .then_inc(w["x2"], 1)
                if at := s.at(1, i, b0):
                    g, b, n, rows = at
                    z = Z[b % 4][0:rows]
                    w.landed(pool, "o_in", b, n)
                    w.freed(pool, "x2", n, 4)
                    pool.tensor_tensor(z, O[b % 4][0:rows], vec(0, rows), ALU.mult).then_inc(w["z0"], 1)
                    w.done(pool, "z0", n)
                    pool.tensor_tensor(z, z, vec(1, rows), ALU.add).then_inc(w["z"], 1)

            s.each(pool, step, 10)

        @block.vector
        def _(dve):
            dve.memset(minus_one[:, :], -1.0).then_inc(constant, 1)

            def step(i, b0):
                if at := s.at(11, i, b0):
                    g, b, n, rows = at
                    w.done(dve, "b_rs", n)
                    w.freed(dve, "x3", n, 2)
                    for j in range(J):
                        last = dve.scalar_tensor_tensor(
                            YG[b % 2][0:rows, j, :], y[b % 2][0:rows, j * C:(j + 1) * C], lnB.mv[b][0:rows, j, 0:1],
                            k.spread[0:rows, 2, :], ALU.subtract, ALU.mult)
                    last.then_inc(w["yg"], 1)
                    w.done(dve, "yg", n)
                    w.done(dve, "x2b", n)
                    for j in range(J):
                        last = dve.scalar_tensor_tensor(
                            X3[b][0:rows, j, :], YG[b % 2][0:rows, j, :], lnB.rs[b][0:rows, j:j + 1],
                            X3[b][0:rows, j, :], ALU.mult, ALU.add)
                    last.then_inc(w["x3"], 1)
                if at := s.at(3, i, b0):
                    g, b, n, rows = at
                    q = Q[b % 4][0:rows]
                    w.done(dve, "q1", n)
                    dve.reciprocal(q, q).then_inc(w["iq"], 1)
                if at := s.at(10, i, b0):
                    g, b, n, rows = at
                    w.done(dve, "y", n)
                    lnB.stats(dve, y[b % 2][:, :].rearrange("p (j c) -> p j c", j=J), b, n, rows)
                if at := s.at(5, i, b0):
                    g, b, n, rows = at
                    w.done(dve, "x2", n)
                    lnA.stats(dve, X2[b % 4], b, n, rows)
                if at := s.at(10, i, b0):
                    g, b, n, rows = at
                    lnB.mean(dve, b, n, rows)
                if at := s.at(9, i, b0):
                    g, b, n, rows = at
                    w.done(dve, "su", n)
                    w.freed(dve, "y", n, 2)
                    dve.scalar_tensor_tensor(UT[b % 2][:, :, 0:rows], row_blocks(u[b % 2])[:, :, 0:rows],
                                             k.bu1_col[:, :], SU[b % 2][:, :, 0:rows], ALU.add, ALU.mult)\
                        .then_inc(w["ut"], 1)
                if at := s.at(6, i, b0):
                    g, b, n, rows = at
                    w.done(dve, "a_rs", n)
                    w.freed(dve, "xn", n)
                    dve.scalar_tensor_tensor(nm[b][0:rows, :], lnA.mv[b][0:rows, :, 0], -1.0, lnA.rs[b][0:rows, :],
                                             ALU.mult, ALU.mult).then_inc(w["nm"], 1)
                if at := s.at(5, i, b0):
                    g, b, n, rows = at
                    lnA.mean(dve, b, n, rows)

            s.each(dve, step, 11)

        @block.scalar
        def _(act):
            act.wait_ge(constant, 1)

            def step(i, b0):
                if at := s.at(9, i, b0):
                    g, b, n, rows = at
                    w.done(act, "u", n)
                    w.freed(act, "ut", n, 2)
                    act.activation(SU[b % 2][:, :, 0:rows], row_blocks(u[b % 2])[:, :, 0:rows], ACT.Sigmoid,
                                   bias=k.bu1_col[:, :]).then_inc(w["su"], 1)
                if at := s.at(8, i, b0):
                    g, b, n, rows = at
                    w.done(act, "hT", n)
                    w.freed(act, "y", n, 4)
                    act.copy(HT[b % 4][:, :, 0:rows], row_blocks(hT[b % 2])[:, :, 0:rows]).then_inc(w["ht"], 1)
                if at := s.at(7, i, b0):
                    g, b, n, rows = at
                    w.done(act, "nm", n)
                    w.freed(act, "hT", n, 4)
                    w.stored(act, "h_out", b, n, 4)
                    for j in range(J):
                        last = act.activation(H[b % 4][0:rows, j, :], X2[b % 4][0:rows, j, :], ACT.Relu,
                                              bias=nm[b][0:rows, j:j + 1], scale=lnA.rs[b][0:rows, j:j + 1])
                    last.then_inc(w["xn"], 1)
                if at := s.at(4, i, b0):
                    g, b, n, rows = at
                    q = Q[b % 4][0:rows]
                    w.done(act, "iq", n)
                    act.activation(q, q, ACT.Relu, bias=minus_one[0:rows, :], scale=2.0).then_inc(w["gate"], 1)
                if at := s.at(2, i, b0):
                    g, b, n, rows = at
                    sg, q = S[b % 2][0:rows], Q[b % 4][0:rows]
                    w.done(act, "z", n)
                    w.freed(act, "sq", n, 2)
                    act.activation(sg, Z[b % 4][0:rows], ACT.Sigmoid, scale=-1.0).then_inc(w["s"], 1)
                    w.done(act, "s", n)
                    w.freed(act, "x2", n, 4)
                    act.activation(q, sg, ACT.Square).then_inc(w["sq"], 1)
                    w.done(act, "sq", n)
                    act.activation(q, q, ACT.Relu, bias=k.ones[0:rows, 0:1]).then_inc(w["q1"], 1)

            s.each(act, step, 9)

        @block.tensor
        def _(pe):
            def step(i, b0):
                if at := s.at(10, i, b0):
                    g, b, n, rows = at
                    w.done(pe, "ut", n)
                    w.freed(pe, "x3", n, 2)
                    pe.matmul(y[b % 2][0:rows, :].rearrange("p (j c) -> p j c", j=J), k.ones3[:, 0:rows],
                              k.rows3[:, 6:7, :].to_broadcast([3, J, C]), start=True, stop=False, skip_group_check=True)
                    for j in range(J):
                        for left, right in ((UT[b % 2], k.wu2), (HT[b % 4], k.ident)):
                            last = pe.matmul(y[b % 2][0:rows, j * C:(j + 1) * C], left[:, j, 0:rows], right[:, :],
                                             start=False, stop=True, skip_group_check=True)
                    last.then_inc(w["y"], 1)
                if at := s.at(9, i, b0):
                    g, b, n, rows = at
                    w.done(pe, "ht", n)
                    w.freed(pe, "ut", n, 2)
                    pe.matmul(row_blocks(u[b % 2])[:, :, 0:rows], k.wu1a[:, :], HT[b % 4][:, :, 0:rows],
                              start=True, stop=True).then_inc(w["u"], 1)
                if at := s.at(8, i, b0):
                    g, b, n, rows = at
                    w.done(pe, "xn", n)
                    w.freed(pe, "ht", n, 2)
                    for j in range(J):
                        last = pe.transpose(hT[b % 2][:, j * P:j * P + rows], H[b % 4][0:rows, j, :],
                                            k.ident[0:rows, 0:rows])
                    last.then_inc(w["hT"], 1)

            s.each(pe, step, 10)


def edges_fourth(nc, k):
    with Phase(nc) as ctx:
        L = LONG
        sb = lambda name, shape, count=L: [ctx.enter_context(nc.sbuf_tensor(f"e4_{name}{b}", shape, F32))
                                           for b in range(count)]
        p = EdgePass(nc, ctx, "e4", k, 1, "hT ht m sm mt q qq u su ut y" + PowerNorm.steps("b") + "xb yg x3", "",
                     "s_in d_in x_out", L)
        w = p.w
        lnB = PowerNorm(nc, ctx, "e4", k, w, 1, p.turn, "x3", "b")
        XS, XD = sb("XS", [P, 2 * C]), sb("XD", [P, 2 * C])
        HT = sb("HT", [C, 2, P])
        SM, MT, QQ, SU, UT = (sb(n, [P, C]) for n in ("SM", "MT", "QQ", "SU", "UT"))
        XB, YG = sb("XB", [P, C]), sb("YG", [P, C])
        bank = lambda name: ctx.enter_context(nc.psum_tensor(f"e4_{name}", [P, 512], F32))
        krow, hT, m, q, tot, u = (bank(n) for n in ("krow", "hT", "m", "q", "tot", "u"))
        y = [bank("y0"), bank("y1")]
        block = ctx.enter_context(nc.Block())
        s = Stages(L, T)

        @block.sync
        def _(sp):
            w.credit(sp)

        @block.gpsimd
        def _(pool):
            def step(i, b0):
                if at := s.at(8, i, b0):
                    t, b, n = at
                    w.done(pool, "x3", n)
                    p.scatter(pool, k.out, XB[b][:, :], b, n, "x_out")
                if at := s.at(7, i, b0):
                    t, b, n = at
                    lnB.power(pool, b, n)
                if at := s.at(0, i, b0):
                    t, b, n = at
                    w.freed(pool, "xb", n)
                    p.gather(pool, XS[b][:, :], k.XH, 0, b, n, "s_in")
                    w.freed(pool, "hT", n)
                    p.gather(pool, XD[b][:, :], k.XH, 1, b, n, "d_in")

            s.each(pool, step, 8)
            w.drain(pool, "x_out", T)

        @block.vector
        def _(dve):
            p.start(dve)

            def step(i, b0):
                if at := s.at(0, i, b0):
                    t, b, n = at
                    p.load_ids(dve, t, b, n, ("s_in", "d_in"))
                if at := s.at(2, i, b0):
                    t, b, n = at
                    p.load_sid(dve, t, b, n, "x_out")
                if at := s.at(8, i, b0):
                    t, b, n = at
                    w.done(dve, "b_rs", n)
                    w.freed(dve, "x3", n)
                    dve.scalar_tensor_tensor(YG[b][:, :], y[b % 2][:, 0:C], lnB.mv[b][:, 0, 0:1], k.spread[:, 2, :],
                                             ALU.subtract, ALU.mult).then_inc(w["yg"], 1)
                    w.done(dve, "yg", n)
                    w.done(dve, "xb", n)
                    dve.scalar_tensor_tensor(XB[b][:, :], YG[b][:, :], lnB.rs[b][:, 0:1], XB[b][:, :],
                                             ALU.mult, ALU.add).then_inc(w["x3"], 1)
                if at := s.at(7, i, b0):
                    t, b, n = at
                    w.drained(dve, "x_out", b, n)
                    dve.tensor_tensor(XB[b][:, :], XS[b][:, 0:C], k.spread[:, 3, :], ALU.add).then_inc(w["xb"], 1)
                    w.done(dve, "y", n)
                    lnB.stats(dve, y[b % 2][:, 0:C].rearrange("p (a c) -> p a c", a=1), b, n)
                    lnB.mean(dve, b, n)
                if at := s.at(6, i, b0):
                    t, b, n = at
                    w.done(dve, "su", n)
                    w.freed(dve, "y", n)
                    dve.scalar_tensor_tensor(UT[b][:, :], u[:, 0:P], k.bu1_col[:, :], SU[b][:, :], ALU.add, ALU.mult)\
                        .then_inc(w["ut"], 1)
                if at := s.at(4, i, b0):
                    t, b, n = at
                    w.done(dve, "q", n)
                    w.freed(dve, "tot", n)
                    dve.tensor_tensor(QQ[b][:, :], q[:, 0:C], k.cb[:, :], ALU.add).then_inc(w["qq"], 1)
                if at := s.at(3, i, b0):
                    t, b, n = at
                    w.done(dve, "sm", n)
                    w.freed(dve, "q", n)
                    dve.scalar_tensor_tensor(MT[b][:, :], m[:, 0:P], k.bm1_col[:, :], SM[b][:, :], ALU.add, ALU.mult)\
                        .then_inc(w["mt"], 1)
                if at := s.at(2, i, b0):
                    t, b, n = at
                    p.masks(dve, [krow, krow], b, n)
                if at := s.at(1, i, b0):
                    t, b, n = at
                    p.load_keys(dve, t, b, n)

            s.each(dve, step, 8)

        @block.scalar
        def _(act):
            def step(i, b0):
                if at := s.at(6, i, b0):
                    t, b, n = at
                    w.done(act, "u", n)
                    w.freed(act, "ut", n)
                    act.activation(SU[b][:, :], u[:, 0:P], ACT.Sigmoid, bias=k.bu1_col[:, :]).then_inc(w["su"], 1)
                if at := s.at(5, i, b0):
                    t, b, n = at
                    w.freed(act, "u", n)
                    p.keep_sums(act, [tot, tot], b, n)
                if at := s.at(3, i, b0):
                    t, b, n = at
                    w.done(act, "m", n)
                    w.freed(act, "mt", n)
                    act.activation(SM[b][:, :], m[:, 0:P], ACT.Sigmoid, bias=k.bm1_col[:, :]).then_inc(w["sm"], 1)
                if at := s.at(2, i, b0):
                    t, b, n = at
                    w.done(act, "hT", n)
                    w.freed(act, "y", n)
                    act.copy(HT[b][:, :, :].rearrange("c s p -> c (s p)"), hT[:, 0:2 * P]).then_inc(w["ht"], 1)

            s.each(act, step, 6)

        @block.tensor
        def _(pe):
            pe.wait_ge(p.zeroed, 1)

            def step(i, b0):
                if at := s.at(7, i, b0):
                    t, b, n = at
                    w.done(pe, "ut", n)
                    w.freed(pe, "x3", n, 2)
                    pe.matmul(y[b % 2][:, 0:C], k.ones3[:, :], k.rows3[:, 6, :], start=True, stop=False,
                              skip_group_check=True)
                    pe.matmul(y[b % 2][:, 0:C], UT[b][:, :], k.wu2[:, :], start=False, stop=True, skip_group_check=True)
                    pe.matmul(y[b % 2][:, 0:C], HT[b][:, 0, :], k.ident[:, :], start=False, stop=True,
                              skip_group_check=True).then_inc(w["y"], 1)
                if at := s.at(6, i, b0):
                    t, b, n = at
                    w.done(pe, "totsb", n)
                    w.freed(pe, "ut", n, 1)
                    pe.matmul(u[:, 0:P], k.wu1a[:, :], HT[b][:, 0, :], start=True, stop=False)
                    pe.matmul(u[:, 0:P], p.totsb[b][:, :], k.ident[:, :], start=False, stop=True).then_inc(w["u"], 1)
                if at := s.at(5, i, b0):
                    t, b, n = at
                    w.done(pe, "qq", n)
                    p.sums(pe, [tot, tot], [QQ[b][:, :]], b, n)
                if at := s.at(4, i, b0):
                    t, b, n = at
                    w.done(pe, "mt", n)
                    w.freed(pe, "qq", n, 1)
                    pe.matmul(q[:, 0:C], MT[b][:, :], k.wc[:, :], start=True, stop=True).then_inc(w["q"], 1)
                if at := s.at(3, i, b0):
                    t, b, n = at
                    w.done(pe, "ht", n)
                    w.freed(pe, "mt", n, 1)
                    pe.matmul(m[:, 0:P], k.wm1a[:, :], HT[b][:, 0, :], start=True, stop=False)
                    pe.matmul(m[:, 0:P], k.wm1b[:, :], HT[b][:, 1, :], start=False, stop=True).then_inc(w["m"], 1)
                if at := s.at(2, i, b0):
                    t, b, n = at
                    p.spread_keys(pe, [krow, krow], b, n, 1)
                    w.landed(pe, "s_in", b, n)
                    w.landed(pe, "d_in", b, n)
                    w.freed(pe, "ht", n, 1)
                    for half, rows in enumerate((XS[b], XD[b])):
                        last = pe.transpose(hT[:, half * P:(half + 1) * P], rows[:, C:2 * C], k.ident[:, :])
                    last.then_inc(w["hT"], 1)

            s.each(pe, step, 7)


def edges_fifth(nc, k):
    with Phase(nc) as ctx:
        L = LONG
        sb = lambda name, shape: [ctx.enter_context(nc.sbuf_tensor(f"e5_{name}{b}", shape, F32)) for b in range(L)]
        p = EdgePass(nc, ctx, "e5", k, 0, Norm.STEPS + "nm h hw attn msg st r", "r_out", "s_in d_in", L)
        w = p.w
        ln = Norm(nc, ctx, "e5", w, 2, p.turn["dve"], "h")
        XX, H = sb("XX", [P, 2, C]), sb("H", [P, 2, C])
        HW, HH, MSG, ST, RES = (sb(n, [P, C]) for n in ("HW", "HH", "MSG", "ST", "RES"))
        nm, attn = sb("nm", [P, 2]), sb("attn", [P, 1])
        krow, tot = ([ctx.enter_context(nc.psum_tensor(f"e5_{n}{b}", [P, 512], F32)) for b in range(2)]
                     for n in ("krow", "tot"))
        block = ctx.enter_context(nc.Block())
        s = Stages(L, T)

        @block.sync
        def _(sp):
            w.credit(sp)

            def step(i, b0):
                if at := s.at(8, i, b0):
                    t, b, n = at
                    w.done(sp, "r", n)
                    sp.dma_start(tile_rows(k.slot_g, t), RES[b][:, :]).then_inc(w.moves["r_out"][b], 16)

            s.each(sp, step, 8)
            w.drain(sp, "r_out", T)

        @block.gpsimd
        def _(pool):
            def step(i, b0):
                if at := s.at(0, i, b0):
                    t, b, n = at
                    p.load_ids(pool, t, b, n, ("s_in", "d_in"), p.turn["pool"])
                    w.freed(pool, "r", n)
                    p.gather(pool, XX[b][:, 0, :], k.out, 0, b, n, "s_in")
                    p.gather(pool, XX[b][:, 1, :], k.out, 1, b, n, "d_in")

            s.each(pool, step, 0)

        @block.vector
        def _(dve):
            p.start(dve)

            def step(i, b0):
                first, mid, now = s.at(2, i, b0), s.at(3, i, b0), s.at(4, i, b0)
                ends = s.at(7, i, b0)
                if first:
                    t, b, n = first
                    w.landed(dve, "s_in", b, n)
                    w.landed(dve, "d_in", b, n)
                    ln.stats(dve, XX[b], b, n)
                if ends:
                    t, b, n = ends
                    w.done(dve, "totsb", n)
                    w.freed(dve, "r", n)
                    dve.tensor_tensor(ST[b][:, :], p.totsb[b][:, :], k.spread[:, 4, :], ALU.mult).then_inc(w["st"], 1)
                if first:
                    t, b, n = first
                    ln.mean(dve, b, n)
                if ends:
                    t, b, n = ends
                    w.done(dve, "st", n)
                    w.drained(dve, "r_out", b, n)
                    dve.tensor_tensor(RES[b][:, :], ST[b][:, :], XX[b][:, 1, :], ALU.add).then_inc(w["r"], 1)
                if first:
                    t, b, n = first
                    ln.shifted(dve, b, n)
                if mid:
                    t, b, n = mid
                    w.done(dve, "ln_rs", n)
                    w.freed(dve, "h", n)
                    dve.scalar_tensor_tensor(nm[b][:, :], ln.mv[b][:, :, 0], -1.0, ln.rs[b][:, :], ALU.mult, ALU.mult)\
                        .then_inc(w["nm"], 1)
                if first:
                    t, b, n = first
                    ln.inverse(dve, b, n)
                if now:
                    t, b, n = now
                    w.done(dve, "h", n)
                    w.freed(dve, "attn", n)
                    dve.tensor_tensor(HW[b][:, :], H[b][:, 1, :], k.spread[:, 5, :], ALU.mult).then_inc(w["hw"], 1)
                    p.masks(dve, krow, b, n)
                    w.done(dve, "hw", n)
                    w.freed(dve, "msg", n)
                    dve.tensor_tensor_reduce(HH[b][:, :], HW[b][:, :], H[b][:, 0, :], 1.0, 0.0, ALU.mult, ALU.add,
                                             attn[b][:, :]).then_inc(w["attn"], 1)
                if mid:
                    t, b, n = mid
                    p.load_keys(dve, t, b, n)
                if now:
                    t, b, n = now
                    w.done(dve, "attn", n)
                    w.freed(dve, "tot", n)
                    dve.tensor_scalar(MSG[b][:, :], H[b][:, 0, :], attn[b][:, :], None, ALU.mult).then_inc(w["msg"], 1)

            s.each(dve, step, 7)

        @block.scalar
        def _(act):
            def step(i, b0):
                if at := s.at(6, i, b0):
                    t, b, n = at
                    w.freed(act, "st", n)
                    p.keep_sums(act, tot, b, n)
                if at := s.at(4, i, b0):
                    t, b, n = at
                    w.done(act, "nm", n)
                    w.freed(act, "msg", n)
                    for half in range(2):
                        last = act.activation(H[b][:, half, :], XX[b][:, half, :], ACT.Relu,
                                              bias=nm[b][:, half:half + 1], scale=ln.rs[b][:, half:half + 1])
                    last.then_inc(w["h"], 1)
                if at := s.at(3, i, b0):
                    t, b, n = at
                    ln.root(act, b, n)

            s.each(act, step, 6)

        @block.tensor
        def _(pe):
            pe.wait_ge(p.zeroed, 1)

            def step(i, b0):
                if at := s.at(6, i, b0):
                    t, b, n = at
                    w.done(pe, "msg", n)
                    p.sums(pe, tot, [MSG[b][:, :]], b, n)
                if at := s.at(4, i, b0):
                    t, b, n = at
                    p.spread_keys(pe, krow, b, n)

            s.each(pe, step, 6)


def last_rows(nc, k):
    with Phase(nc) as ctx:
        L = LONG
        p = EdgePass(nc, ctx, "e6", k, 0, "", "r_in", "x_out", L)
        w = p.w
        RES = [ctx.enter_context(nc.sbuf_tensor(f"e6_RES{b}", [P, C], F32)) for b in range(L)]
        block = ctx.enter_context(nc.Block())

        @block.sync
        def _(sp):
            w.credit(sp)

            def step(i, b):
                if live(i):
                    w.drained(sp, "x_out", b % L, i + 1)
                    sp.dma_start(RES[b % L][:, :], tile_rows(k.slot_g, i)).then_inc(w.moves["r_in"][b % L], 16)

            each_step(sp, step, 0, T, L)

        @block.vector
        def _(dve):
            def step(i, b):
                if live(i):
                    p.load_sid(dve, i, b % L, i + 1, "x_out")

            each_step(dve, step, 0, T, L)

        @block.gpsimd
        def _(pool):
            def step(i, b):
                if live(i):
                    w.landed(pool, "r_in", b % L, i + 1)
                    p.scatter(pool, k.out, RES[b % L][:, :], b % L, i + 1, "x_out")

            each_step(pool, step, 0, T, L)
            w.drain(pool, "x_out", T)


class Kept:
    pass


def program(nc, x, src, dst, edge_type, weights, out):
    k = Kept()
    k.x, k.src, k.dst, k.edge_type, k.out = x, src, dst, edge_type, out
    k.L0_W1, k.L0_b1, k.L0_W2, k.L0_b2 = (weights["L0_" + n] for n in ("W1", "b1", "W2", "b2"))
    k.L1_W, k.L1_root, k.L1_bias, k.L1_gamma, k.L1_beta = (
        weights["L1_" + n] for n in ("W", "root", "bias", "gamma", "beta"))
    k.L2_wm1, k.L2_bm1, k.L2_wm2, k.L2_bm2 = (weights["L2_" + n] for n in ("wm1", "bm1", "wm2", "bm2"))
    k.L2_wu1, k.L2_bu1, k.L2_wu2, k.L2_bu2 = (weights["L2_" + n] for n in ("wu1", "bu1", "wu2", "bu2"))
    k.L2_gamma, k.L2_beta, k.L3_W2, k.L3_W3 = (weights[n] for n in ("L2_gamma", "L2_beta", "L3_W2", "L3_W3"))
    with ExitStack() as ctx:
        sb = lambda name, shape, dt=F32: ctx.enter_context(nc.sbuf_tensor(name, shape, dt))
        k.edge_i = sb("edge_i", [P, 3, T], I32)
        k.iota = sb("iota", [P, HI])
        k.iota_b = sb("iota_b", [P, HI], BF16)
        k.ident_b = sb("ident_b", [P, P], BF16)
        k.part = sb("part", [P, 1])
        k.ident, k.before, k.shift, k.unshift, k.wrap = (sb(n, [P, P]) for n in ("ident", "before", "shift", "unshift", "wrap"))
        k.first, k.last = sb("first", [P, 1]), sb("last", [P, 1])
        k.ones = sb("ones", [P, HI])
        k.w1, k.w2, k.root = (sb(n, [C, C]) for n in ("w1", "w2", "root"))
        k.b1_col = sb("b1_col", [C, 1])
        k.indeg = sb("indeg", [P, HI])
        k.sorted = sb("sorted", [P, 2, 2, T])
        k.key = sb("key", [P, 2, T + 2])
        k.index = sb("index", [P, 2, T, 3], I32)
        k.is_last = sb("is_last", [P, T])
        k.dinv = sb("dinv", [P, T])
        k.rel_weight = sb("rel_weight", [P, T, R])
        k.flat = nc.dram_tensor("flat_dram", (2, P * T), F32, kind="Internal").ap()
        k.pairs = [nc.dram_tensor(f"pairs{o}_dram", (P * T, 2), F32, kind="Internal").ap() for o in range(2)]
        k.minus_half = sb("minus_half", [P, HI])
        k.node_dinv, k.whole = sb("node_dinv", [P, HI]), sb("whole", [P, HI])
        k.vectors = [k.L0_b1, k.L0_b2, k.L1_bias, k.L2_bm1, k.L2_bm2, k.L2_bu1, k.L2_bu2]
        k.ones3, k.rows3 = sb("ones3", [3, P], BF16), sb("rows3", [3, len(k.vectors), C], BF16)
        k.zero_row = sb("zero_row", [1, P])
        k.w_rel = sb("w_rel", [C, R, C])
        k.stats_edges = sb("stats_edges", [C, 2])
        k.stats_whole = sb("stats_whole", [C, 2])
        k.spread = sb("spread", [P, 6, C])
        k.bm1_col, k.bu1_col = sb("bm1_col", [C, 1]), sb("bu1_col", [C, 1])
        k.wm1a, k.wm1b, k.wu1a, k.wu2, k.wc, k.cb = (sb(n, [C, C]) for n in ("wm1a", "wm1b", "wu1a", "wu2", "wc", "cb"))
        table = lambda name: nc.dram_tensor(name, (N, C), F32, kind="Internal").ap()
        k.H0, k.G1, k.X1, k.O = (table(n) for n in ("h0_dram", "g1_dram", "x1_dram", "o_dram"))
        k.XH = nc.dram_tensor("xh_dram", (N, 2 * C), F32, kind="Internal").ap()
        slots = lambda name: nc.dram_tensor(name, (T * P, C), F32, kind="Internal").ap()
        k.slot_x, k.slot_g, k.slot_x2 = (slots(n) for n in ("slot_x_dram", "slot_g_dram", "slot_x2_dram"))
        constants(nc, k)
        sort_edges(nc, k)
        edge_tables(nc, k)
        split_rows(nc, k)
        nodes_first(nc, k)
        edges_first(nc, k)
        edges_second(nc, k)
        edges_third(nc, k)
        row_tables(nc, k)
        nodes_second(nc, k)
        edges_fourth(nc, k)
        edges_fifth(nc, k)
        last_rows(nc, k)


def kernel(**inputs):
    import numpy as np
    import concourse.bacc as bacc
    from concourse.bass_utils import run_bass_kernel_spmd

    nc = bacc.Bacc("TRN2", target_bir_lowering=False, num_devices=1)
    arrays = {"in_" + name: np.ascontiguousarray(array) for name, array in inputs.items()}
    given = {name: nc.dram_tensor("in_" + name, array.shape, mybir.dt.from_np(array.dtype), kind="ExternalInput").ap()
             for name, array in ((n[3:], a) for n, a in arrays.items())}
    out = nc.dram_tensor("out", (N, C), F32, kind="ExternalOutput").ap()
    weights = {name.replace("_gnn_", "_"): ap for name, ap in given.items() if name.startswith("L")}
    program(nc, given["x"], given["src"], given["dst"], given["edge_type_8"], weights, out)
    run = run_bass_kernel_spmd(nc, [arrays], core_ids=[0])
    return run.results[0]["out"]
```
